# Optimizing a Trainium2 kernel written in Bass

```python
import numpy as np
import jax
import jax.numpy as jnp

def _softmax(x, axis=-1):
    return jax.nn.softmax(x, axis=axis)

def _gelu(x):
    return jax.nn.gelu(x, approximate=True)

def _silu(x):
    return jax.nn.silu(x)

def _sigmoid(x):
    return jax.nn.sigmoid(x)

def _layernorm(x, axis=-1, eps=1e-05):
    m = jnp.mean(x, axis=axis, keepdims=True)
    v = jnp.var(x, axis=axis, keepdims=True)
    return (x - m) / jnp.sqrt(v + eps)

def _scatter_add(tgt, idx, src, axis=0):
    return tgt.at[idx].add(src)

def _segment_sum(src, seg, n):
    return jax.ops.segment_sum(src, seg, n)
kernel_name = 'mk_seq_preln_d1_jaxref_r8_0c9815'

def setup_inputs(seed: int=0):
    np.random.seed(seed)
    _w = jnp.asarray

    def _L0_attn_setup():
        import jax, jax.numpy as jnp
        import numpy as np
        N_EMBD = 256
        N_Q_HEAD = 16
        N_KV_HEADS = 4
        HEAD_SIZE = N_EMBD // N_Q_HEAD
        GROUP = N_Q_HEAD // N_KV_HEADS
        ROPE_BASE = 10000.0

        def apply_rope(x, seq_offset=0):
            B, H, T, D = x.shape
            half = D // 2
            inv_freq = 1.0 / ROPE_BASE ** (jnp.arange(0, half, dtype=jnp.float32) / half)
            pos = jnp.arange(seq_offset, seq_offset + T, dtype=jnp.float32)
            ang = pos[:, None] * inv_freq[None, :]
            cos = jnp.cos(ang)[None, None].astype(x.dtype)
            sin = jnp.sin(ang)[None, None].astype(x.dtype)
            x1, x2 = (x[..., :half], x[..., half:])
            return jnp.concatenate([x1 * cos - x2 * sin, x2 * cos + x1 * sin], axis=-1)
        key = jax.random.key(seed)
        k0, k1, k2, k3, k4 = jax.random.split(key, 5)
        B, T = (4, 256)
        s = 1.0 / np.sqrt(N_EMBD)
        x = jax.random.normal(k0, (B, T, N_EMBD), dtype=jnp.float32)
        Wq = jax.random.normal(k1, (N_Q_HEAD * HEAD_SIZE, N_EMBD), dtype=jnp.float32) * s
        Wk = jax.random.normal(k2, (N_KV_HEADS * HEAD_SIZE, N_EMBD), dtype=jnp.float32) * s
        Wv = jax.random.normal(k3, (N_KV_HEADS * HEAD_SIZE, N_EMBD), dtype=jnp.float32) * s
        Wp = jax.random.normal(k4, (N_EMBD, N_Q_HEAD * HEAD_SIZE), dtype=jnp.float32) * s
        return {'x': x, 'Wq': Wq, 'Wk': Wk, 'Wv': Wv, 'Wp': Wp}
    _L0_attn_in = _L0_attn_setup()

    def _L0_ffn_setup():
        import jax, jax.numpy as jnp
        import numpy as np
        H = 256
        I = 176
        E = 16
        K = 2
        SI = I * 2

        def _swiglu(gu, inter):
            g, u = (gu[..., :inter], gu[..., inter:])
            return jax.nn.silu(g) * u
        key = jax.random.key(seed)
        ks = jax.random.split(key, 6)
        s = 0.02
        hidden_states = jax.random.normal(ks[0], (1, 128, H), dtype=jnp.float32)
        gate_w = jax.random.normal(ks[1], (E, H), dtype=jnp.float32) * s
        w_gate_up = jax.random.normal(ks[2], (E, H, 2 * I), dtype=jnp.float32) * s
        w_down = jax.random.normal(ks[3], (E, I, H), dtype=jnp.float32) * s
        shared_gate_up = jax.random.normal(ks[4], (H, 2 * SI), dtype=jnp.float32) * s
        shared_down = jax.random.normal(ks[5], (SI, H), dtype=jnp.float32) * s
        return {'hidden_states': hidden_states, 'gate_w': gate_w, 'w_gate_up': w_gate_up, 'w_down': w_down, 'shared_gate_up': shared_gate_up, 'shared_down': shared_down}
    _L0_ffn_in = _L0_ffn_setup()
    _d = {'L0_attn_x': _L0_attn_in['x'], 'L0_attn_Wq': _L0_attn_in['Wq'], 'L0_attn_Wk': _L0_attn_in['Wk'], 'L0_attn_Wv': _L0_attn_in['Wv'], 'L0_attn_Wp': _L0_attn_in['Wp'], 'L0_ffn_gate_w': _L0_ffn_in['gate_w'], 'L0_ffn_w_gate_up': _L0_ffn_in['w_gate_up'], 'L0_ffn_w_down': _L0_ffn_in['w_down'], 'L0_ffn_shared_gate_up': _L0_ffn_in['shared_gate_up'], 'L0_ffn_shared_down': _L0_ffn_in['shared_down']}
    _x0 = _d['L0_attn_x']
    _d['L0_attn_x'] = jax.random.normal(jax.random.fold_in(jax.random.key(seed), 1), (1, 2048, 256), dtype=_x0.dtype)
    del _x0
    return _d

def reference(L0_attn_x, L0_attn_Wq, L0_attn_Wk, L0_attn_Wv, L0_attn_Wp, L0_ffn_gate_w, L0_ffn_w_gate_up, L0_ffn_w_down, L0_ffn_shared_gate_up, L0_ffn_shared_down):

    def _L0_attn_ref(x, Wq, Wk, Wv, Wp):
        import jax, jax.numpy as jnp
        import numpy as np
        N_EMBD = 256
        N_Q_HEAD = 16
        N_KV_HEADS = 4
        HEAD_SIZE = N_EMBD // N_Q_HEAD
        GROUP = N_Q_HEAD // N_KV_HEADS
        ROPE_BASE = 10000.0

        def apply_rope(x, seq_offset=0):
            B, H, T, D = x.shape
            half = D // 2
            inv_freq = 1.0 / ROPE_BASE ** (jnp.arange(0, half, dtype=jnp.float32) / half)
            pos = jnp.arange(seq_offset, seq_offset + T, dtype=jnp.float32)
            ang = pos[:, None] * inv_freq[None, :]
            cos = jnp.cos(ang)[None, None].astype(x.dtype)
            sin = jnp.sin(ang)[None, None].astype(x.dtype)
            x1, x2 = (x[..., :half], x[..., half:])
            return jnp.concatenate([x1 * cos - x2 * sin, x2 * cos + x1 * sin], axis=-1)
        B, T, C = x.shape
        Q = (x @ Wq.T).reshape(B, T, N_Q_HEAD, HEAD_SIZE).transpose(0, 2, 1, 3)
        K = (x @ Wk.T).reshape(B, T, N_KV_HEADS, HEAD_SIZE).transpose(0, 2, 1, 3)
        V = (x @ Wv.T).reshape(B, T, N_KV_HEADS, HEAD_SIZE).transpose(0, 2, 1, 3)
        Q = apply_rope(Q, 0)
        K = apply_rope(K, 0)
        Qg = Q.reshape(B, N_KV_HEADS, GROUP, T, HEAD_SIZE)
        scale = 1.0 / jnp.sqrt(jnp.asarray(HEAD_SIZE, dtype=Q.dtype))
        scores = jnp.einsum('bkgtd,bksd->bkgts', Qg, K) * scale
        causal = jnp.tril(jnp.ones((T, T), dtype=bool))
        scores = jnp.where(causal, scores, jnp.finfo(scores.dtype).min)
        attn = jax.nn.softmax(scores, axis=-1)
        out = jnp.einsum('bkgts,bksd->bkgtd', attn, V)
        out = out.reshape(B, N_Q_HEAD, T, HEAD_SIZE).transpose(0, 2, 1, 3).reshape(B, T, N_Q_HEAD * HEAD_SIZE)
        return out @ Wp.T

    def _L0_ffn_ref(hidden_states, gate_w, w_gate_up, w_down, shared_gate_up, shared_down):
        import jax, jax.numpy as jnp
        import numpy as np
        H = 256
        I = 176
        E = 16
        K = 2
        SI = I * 2

        def _swiglu(gu, inter):
            g, u = (gu[..., :inter], gu[..., inter:])
            return jax.nn.silu(g) * u
        orig_shape = hidden_states.shape
        x = hidden_states.reshape(-1, H)
        logits = jnp.einsum('th,eh->te', x, gate_w)
        scores = jax.nn.softmax(logits, axis=-1)
        topk_w, topk_idx = jax.lax.top_k(scores, K)
        combine = jnp.sum(jax.nn.one_hot(topk_idx, E, dtype=x.dtype) * topk_w[..., None], axis=1)
        gu = jnp.einsum('th,ehj->etj', x, w_gate_up)
        h = _swiglu(gu, I)
        y = jnp.einsum('eti,eih,te->th', h, w_down, combine)
        gu_s = x @ shared_gate_up
        y = y + _swiglu(gu_s, SI) @ shared_down
        return y.reshape(orig_shape)
    x = L0_attn_x
    x = x + _L0_attn_ref(_layernorm(x, axis=-1), L0_attn_Wq, L0_attn_Wk, L0_attn_Wv, L0_attn_Wp)
    x = x + _L0_ffn_ref(_layernorm(x, axis=-1), L0_ffn_gate_w, L0_ffn_w_gate_up, L0_ffn_w_down, L0_ffn_shared_gate_up, L0_ffn_shared_down)
    return x

_drawn_inputs = setup_inputs


def setup_inputs(seed=0):
    import zlib

    import numpy as np

    out = dict(_drawn_inputs(seed))
    spreads = {}
    factors = {'L0_ffn_gate_w': 8.0,
     'L0_ffn_w_gate_up': 8.0,
     'L0_ffn_w_down': 8.0,
     'L0_ffn_shared_gate_up': 2.853,
     'L0_ffn_shared_down': 2.86}
    for name, (base, spread) in spreads.items():
        noise = np.random.default_rng([zlib.crc32(name.encode()), seed]).standard_normal(out[name].shape)
        drawn = base * np.exp(spread * noise) if base else spread * noise
        out[name] = jnp.asarray(drawn.astype(out[name].dtype))
    for name, factor in factors.items():
        out[name] = (out[name] * factor).astype(out[name].dtype)
    return out
```

```python
import math
from contextlib import ExitStack

import concourse.bass as bass
from concourse import mybir

F32 = mybir.dt.float32
BF16 = mybir.dt.bfloat16
I32 = mybir.dt.int32
U32 = mybir.dt.uint32
ALU = mybir.AluOpType
ACT = mybir.ActivationFunctionType
AX = mybir.AxisListType

P = 128
T, C = 2048, 256
NT = T // P
HQ, HK, D = 16, 4, 16
GH = HQ // HK
HALF = D // 2
QKV = (HQ + 2 * HK) * D
KC = C // P
NCH, CT, CW = 4, 4, 512
NP_ = 6
KROW = NP_ * D
MROW = 3
SROW = KROW + MROW
VC = 32
NEG = -1.0e30
EPS = 1e-5
SCALE = D ** -0.5
PSLOT = 3
E, I = 16, 176
TOPK = 2
IH = I // 2
SI = 2 * I
SH = SI // IH
SLOTS = (TOPK * T + E * (P - 1)) // P
SLOTS += -SLOTS % 4
RING = 4

UNITS = [(c, g) for c in range(NCH) for g in range(HK)]


def key_blocks(c):
    return CT * (c + 1)


STEPS = [(u, j) for u, (c, g) in enumerate(UNITS) for j in range(key_blocks(c))]
PIECES = [(u, hh, r, k) for u, (c, g) in enumerate(UNITS) for r in range(CT) for hh in range(GH)
          for k in range(c + 1)]
STEPS_TO = [sum(1 for s in STEPS if s[0] <= u) for u in range(len(UNITS))]
PIECES_TO = [sum(1 for a in PIECES if a[0] <= u) for u in range(len(UNITS))]
DIAG = [m for m, (u, j) in enumerate(STEPS) if j >= CT * UNITS[u][0]]


def attention_order():
    LEAD = 1.35
    order = []
    later = []
    taken = 0

    def place(done, ends):
        u = 0
        while u < len(ends) and done >= ends[u]:
            u += 1
        if u == len(ends):
            return float(u)
        first = ends[u - 1] if u else 0
        return u + (done - first) / (ends[u] - first)

    def take_maxima(upto):
        nonlocal taken
        while taken < len(PIECES) and place(taken, PIECES_TO) < upto:
            order.append(("max", taken))
            taken += 1
            for u, end in enumerate(PIECES_TO):
                if taken == end:
                    order.append(("split", u))
                    later.append((u + 1.10 - LEAD, ("shift", u, 0)))
                    later.append((u + 1.20 - LEAD, ("shift", u, 1)))

    take_maxima(1.0)
    for e in (("shift", 0, 0), ("shift", 0, 1)):
        order.append(e)
    later.clear()
    order.append(("score", 0, 0))
    order.append(("score", 0, 1))
    for m, (u, j) in enumerate(STEPS):
        pos = place(m, STEPS_TO)
        nxt = place(m + 1, STEPS_TO)
        due = sorted(x for x in later if x[0] <= pos)
        if m + 1 < len(STEPS):
            nu, nj = STEPS[m + 1]
            if nj == 0:
                due = sorted(x for x in later if x[0] <= pos or x[1][0:2] == ("shift", nu))
        for x in due:
            later.remove(x)
            order.append(x[1])
        if m + 1 < len(STEPS):
            order.append(("score", m + 1, 0))
        take_maxima((pos + nxt) / 2 + LEAD)
        if m + 1 < len(STEPS):
            order.append(("score", m + 1, 1))
        order.append(("values", m))
        take_maxima(nxt + LEAD)
        if m + 1 == STEPS_TO[u]:
            order.append(("take", u))
            later.append((u + 1.08, ("turn", u)))
            if u % HK == HK - 1:
                c = u // HK
                for k in range(4):
                    later.append((u + 1.2 + 0.1 * k, (("turn_out", "project")[k % 2], c, k // 2)))
    for x in sorted(later):
        order.append(x[1])
    return order


ORDER = attention_order()
SMALL = [e for e in ORDER if e[0] in ("shift", "turn", "turn_out", "project")]


def pipeline(fori, first, last, ahead, behind, step):
    def straight(t0, t1):
        for t in range(t0, t1):
            step(t, t % RING, t // RING, lambda d, t=t: first <= t + d < last)

    lo = first + behind + RING
    loops = (last - ahead - lo) // RING
    straight(first - ahead, lo)
    with fori(0, loops) as b:
        for q in range(RING):
            step(lo + q + RING * b, (lo + q) % RING, (lo + q) // RING + b, lambda d: True)
    straight(lo + RING * loops, last + behind)


def program(nc, x, wqkv, wp, rope, wgate, wgu, wdn, wsgu, wsdn, out):
    with ExitStack() as ctx:
        def sb(name, shape, dt=F32):
            return ctx.enter_context(nc.sbuf_tensor(name, shape, dt))

        def sem(name):
            return ctx.enter_context(nc.semaphore(name))

        ps = ctx.enter_context(nc.psum_tensor("ps", [P, 8, 512], F32))
        MAXB, SCB, OB, SMB = 0, 2, 6, 7

        x_sb = sb("x_sb", [P, NT, C])
        xn = sb("xn", [P, NT, C])
        wp_sb = sb("wp_sb", [P, KC, C])
        rope_sb = sb("rope_sb", [P, NT, 3, HALF])
        big = sb("big", [P, (HQ + HK) * T], BF16)
        Qs = big[:, 0:HQ * T].rearrange("p (h t) -> p h t", h=HQ)
        Ks = big[:, HQ * T:].rearrange("p (h t) -> p h t", h=HK)
        bigf = big[:, :].bitcast(F32)
        GU0, DN0 = 0, E * KC * 2 * I
        wgu_sb = bigf[:, GU0:DN0].rearrange("p (e k n) -> p e k n", e=E, k=KC)
        wdn_sb = bigf[0:IH, DN0:DN0 + E * 2 * C].rearrange("p (e k n) -> p e k n", e=E, k=2)
        early = sb("early", [P, NT * C + 2304])
        at = [0]

        def piece(n):
            at[0] += n
            return early[:, at[0] - n:at[0]]

        xnT = piece(CT * KC * P).rearrange("p (i k t) -> p i k t", i=CT, k=KC)
        wqkv_sb = piece(KC * QKV).rearrange("p (k n) -> p k n", k=KC)
        Qn = piece(CT * HQ * NP_ * D // 2).bitcast(BF16).rearrange("p (i h s d) -> p i h s d", i=CT, h=HQ, s=NP_)
        Kn = piece(CT * HK * NP_ * D // 2).bitcast(BF16).rearrange("p (i h s d) -> p i h s d", i=CT, h=HK, s=NP_)
        xT_all = early[:, 0:NT * C].rearrange("p (i k t) -> p i k t", i=NT, k=KC)
        V = sb("V", [P, NT, HK, VC])
        stats = sb("stats", [P, NT, 6])
        mv = sb("mv", [P, NT, 2])
        var = sb("var", [P, NT])
        std = sb("std", [P, NT])
        rstd0 = sb("rstd0", [P, NT])
        newt = sb("newt", [P, NT])
        newt2 = sb("newt2", [P, NT])
        newt3 = sb("newt3", [P, NT])
        rstd = sb("rstd", [P, NT])
        probs = sb("probs", [P, PSLOT, GH, CW])
        scratch = probs[:, :, :, :].rearrange("p s h t -> p (s h t)")
        RQ = CT * (HQ + HK) * D
        rc, rs, qk, res = (scratch[:, i * RQ:(i + 1) * RQ].rearrange("p (i h d) -> p i h d", i=CT, d=D)
                           for i in range(4))
        identf = sb("identf", [P, P])
        identb = sb("identb", [P, P], BF16)
        maskq = sb("maskq", [P, 2 * CW - P])
        junk = sb("junk", [P, 2, CW])
        part = sb("part", [P, 2, GH, CT, NCH])
        neg = sb("neg", [P, 2, GH, CT])
        nd1 = sb("nd1", [P, 2, GH, CT])
        nd2 = sb("nd2", [P, 2, GH, CT])
        M3 = sb("M3", [P, 2, GH, CT, 4], BF16)
        OT = sb("OT", [P, CW])
        rden = sb("rden", [P, CT, GH])
        attn = sb("attn", [P, CT, C])
        aT = sb("aT", [P, 2, KC, P])

        at[0] = 0

        def ffn(n, size):
            at[0] += n * size
            return scratch[:, at[0] - n * size:at[0]].rearrange("p (n m) -> p n m", n=n)

        gate_act = ffn(2, SI)
        hidden = ffn(2, SI)
        hT = ffn(2, SH * P)
        xg = ffn(RING, C)
        xgT = ffn(2, KC * P)
        yb = ffn(RING, C)
        yg = xg
        wgate_sb = sb("wgate_sb", [P, KC, E])
        wsgu_sb = sb("wsgu_sb", [P, KC, 2 * SI])
        wsdn_sb = sb("wsdn_sb", [P, SH, C])
        junk_f = junk[:, :, :].rearrange("p a b -> p (a b)")
        attn_f = attn[:, :, :].rearrange("p a b -> p (a b)")
        hot, wsel = (junk_f[:, i * TOPK * NT * E:(i + 1) * TOPK * NT * E]
                     .rearrange("p (k i e) -> p k i e", k=TOPK, i=NT) for i in range(2))
        where, lg = (attn_f[:, i * NT * E:(i + 1) * NT * E].rearrange("p (i e) -> p i e", i=NT) for i in range(2))
        lsub = attn_f[:, 2 * NT * E:2 * NT * E + NT * (E + 1)].rearrange("p (i e) -> p i e", i=NT)
        lexp = OT[:, 0:NT * (E + 1)].rearrange("p (i e) -> p i e", i=NT)
        iota_e = sb("iota_e", [P, E])
        iota_s = sb("iota_s", [P, SLOTS])
        before = sb("before", [P, P], BF16)
        onesb = sb("onesb", [P, P], BF16)
        top = sb("top", [P, NT, 8])
        top_i = sb("top_i", [P, NT, 8], U32)
        top_f = sb("top_f", [P, NT, TOPK])
        lsum = sb("lsum", [P, NT])
        wtok = sb("wtok", [P, TOPK, NT])
        hots = sb("hots", [P, NT + 1, E], BF16)
        cnt_i = sb("cnt_i", [P, E], I32)
        cnt_t = sb("cnt_t", [P, E], I32)
        tiles = sb("tiles", [P, E])
        csum = sb("csum", [P, 2, 8 + E])
        base0 = sb("base0", [P, E])
        base = sb("base", [P, E])
        dest = sb("dest", [P, TOPK, NT])
        dest_i = sb("dest_i", [P, TOPK, NT], U32)
        s_cmp = sb("s_cmp", [1, SLOTS, E])
        s_exp = sb("s_exp", [1, SLOTS])
        s_exp_i = sb("s_exp_i", [1, SLOTS], I32)
        zeros = xn[:, 0, :]

        xs = nc.dram_tensor("xs", (SLOTS * P, C), F32, kind="Internal").ap()
        ys = nc.dram_tensor("ys", (SLOTS * P, C), F32, kind="Internal").ap()

        x_in = [sem(f"x_in{c}") for c in range(NCH)]
        w_in = sem("w_in")
        consts = sem("consts")
        ones_set = sem("ones_set")
        stats_done = sem("stats_done")
        ln_step = sem("ln_step")
        ln_step2 = sem("ln_step2")
        std_done = sem("std_done")
        xn_ready = sem("xn_ready")
        xnT_ps = sem("xnT_ps")
        xnT_ready = sem("xnT_ready")
        qkv_ps = sem("qkv_ps")
        v_ready = sem("v_ready")
        rope_step = sem("rope_step")
        qpart = sem("qpart")
        kpart = sem("kpart")
        split_step = sem("split_step")
        stack_ready = sem("stack_ready")
        stack_ps = sem("stack_ps")
        stack_even = sem("stack_even")
        stack_odd = sem("stack_odd")
        a_ready = sem("a_ready")
        a_used = sem("a_used")
        neg_ready = sem("neg_ready")
        neg_step = sem("neg_step")
        m3_ready = sem("m3_ready")
        s_ready = sem("s_ready")
        exp_done = sem("exp_done")
        masked = sem("masked")
        pv_done = sem("pv_done")
        o_copied = sem("o_copied")
        small_ready = sem("small_ready")
        small_used = sem("small_used")
        rden_ready = sem("rden_ready")
        x2_done = sem("x2_done")
        zero_made = sem("zero_made")
        xs_zero = sem("xs_zero")
        ffn_w = sem("ffn_w")
        expert_w = sem("expert_w")
        stats2 = sem("stats2")
        var2_ready = sem("var2_ready")
        std2_done = sem("std2_done")
        ln2_step = sem("ln2_step")
        xn2_ready = sem("xn2_ready")
        turn2_ps = sem("turn2_ps")
        turn2_dve = sem("turn2_dve")
        turn2_act = sem("turn2_act")
        logits_ps = sem("logits_ps")
        route = sem("route")
        lexp_done = sem("lexp_done")
        hots_ready = sem("hots_ready")
        pos_ps = sem("pos_ps")
        slots_ready = sem("slots_ready")
        dest_ready = sem("dest_ready")
        scattered = sem("scattered")
        xg_in = [sem(f"xg_in{q}") for q in range(RING)]
        xt_ready = sem("xt_ready")
        xt_taken = sem("xt_taken")
        gu_ready = sem("gu_ready")
        silu_done = sem("silu_done")
        h_ready = sem("h_ready")
        th_ready = sem("th_ready")
        ht_taken = sem("ht_taken")
        dn_ready = sem("dn_ready")
        y_taken = sem("y_taken")
        y_out = [sem(f"y_out{q}") for q in range(RING)]
        yg_in = [sem(f"yg_in{q}") for q in range(RING)]
        mixed = sem("mixed")
        out_done = sem("out_done")

        block = ctx.enter_context(nc.Block())
        x_v = x.rearrange("(i p) c -> p i c", p=P)
        out_v = out.rearrange("(i p) c -> p i c", p=P)
        NFILL = (HQ + HK) // 2

        @block.sync
        def _(sp):
            for c in range(NCH):
                sp.dma_start(x_sb[:, CT * c:CT * c + CT, :], x_v[:, CT * c:CT * c + CT, :]).then_inc(x_in[c], 16)
                if c == 0:
                    sp.dma_start(wqkv_sb[:, :, :], wqkv).then_inc(w_in, 16)
                    sp.dma_start(rope_sb[:, :, :, :], rope).then_inc(w_in, 16)
            sp.dma_start(wp_sb[:, :, :], wp).then_inc(w_in, 16)
            sp.dma_start(wgate_sb[:, :, :], wgate).then_inc(ffn_w, 16)
            sp.dma_start(wsgu_sb[:, :, :], wsgu).then_inc(ffn_w, 16)
            sp.dma_start(wsdn_sb[0:IH, :, :], wsdn).then_inc(ffn_w, 16)
            sp.wait_ge(zero_made, 1)
            zslots = SLOTS // 4
            for q in range(4):
                sp.dma_start(xs[q * zslots * P:(q + 1) * zslots * P, :].rearrange("(s p) c -> p s c", p=P),
                             zeros.unsqueeze(1).to_broadcast([P, zslots, C])).then_inc(xs_zero, 16)
            sp.wait_ge(s_ready, 2 * len(STEPS))
            sp.dma_start(wgu_sb, wgu).then_inc(expert_w, 16)
            sp.dma_start(wdn_sb, wdn).then_inc(expert_w, 16)
            sp.wait_ge(scattered, 16 * TOPK * NT)

            def slot_io(t, q, turn, live):
                if live(3):
                    r = (q + 3) % RING
                    if not isinstance(t, int) or t >= 1:
                        sp.wait_ge(xt_ready, t)
                    sp.dma_start(xg[:, r, :], xs[bass.ds((t + 3) * P, P), :]).then_inc(xg_in[r], 16)
                if live(-1):
                    r = (q - 1) % RING
                    sp.wait_ge(y_taken, NT + t)
                    sp.dma_start(ys[bass.ds((t - 1) * P, P), :], yb[:, r, :]).then_inc(y_out[r], 16)

            pipeline(sp.Fori, 0, SLOTS, 3, 1, slot_io)
            for i in range(0, NT, 2):
                sp.wait_ge(mixed, TOPK * (i + 2))
                sp.dma_start(out_v[:, i:i + 2, :], x_sb[:, i:i + 2, :]).then_inc(out_done, 16)
            sp.wait_ge(out_done, 16 * NT // 2)

        @block.gpsimd
        def _(pool):
            pool.memset(identf[:, :], 0.0).then_inc(consts, 1)
            pool.memset(identb[:, :], 0.0).then_inc(consts, 1)
            pool.memset(maskq[:, :], 0.0).then_inc(consts, 1)
            pool.memset(V[:, :, :, D:VC], 0.0).then_inc(consts, 1)
            pool.wait_ge(consts, 4)
            pool.affine_select(out=identf[:, :], in_=identf[:, :], compare_op=ALU.not_equal, fill=1.0, base=0,
                               pattern=[[-1, P]], channel_multiplier=1).then_inc(consts, 1)
            pool.affine_select(out=identb[:, :], in_=identb[:, :], compare_op=ALU.not_equal, fill=1.0, base=0,
                               pattern=[[-1, P]], channel_multiplier=1).then_inc(consts, 1)
            pool.affine_select(out=maskq[:, CW - P:CW], in_=maskq[:, CW - P:CW], compare_op=ALU.is_ge, fill=NEG,
                               base=0, pattern=[[-1, P]], channel_multiplier=1).then_inc(consts, 1)
            pool.memset(V[:, :, :, D:D + 1], 1.0).then_inc(consts, 1)
            pool.iota(iota_e[:, :], pattern=[[1, E]], base=0, channel_multiplier=0,
                      allow_small_or_imprecise_dtypes=True).then_inc(consts, 1)
            pool.iota(iota_s[:, :], pattern=[[1, SLOTS]], base=0, channel_multiplier=0,
                      allow_small_or_imprecise_dtypes=True).then_inc(consts, 1)
            pool.memset(onesb[:, :], 1.0).then_inc(consts, 1)
            pool.wait_ge(consts, 11)
            pool.affine_select(out=before[:, :], in_=onesb[:, :], compare_op=ALU.is_gt, fill=0.0, base=0,
                               pattern=[[1, P]], channel_multiplier=-1).then_inc(consts, 1)
            pool.memset(hots[:, NT, :], 0.0).then_inc(consts, 1)
            pool.memset(csum[:, :, :], 0.0).then_inc(consts, 1)

            ndiag = 0
            for e in ORDER:
                if e[0] == "split":
                    u, b = e[1], e[1] % 2
                    pool.wait_ge(neg_ready, u + 1)
                    if u >= 2:
                        pool.wait_ge(small_ready, 1 + SMALL.index(("shift", u - 2, 1)))
                    pool.tensor_copy(M3[:, b, :, :, 0], neg[:, b]).then_inc(neg_step, 1)
                    pool.wait_ge(neg_step, 4 * u + 1)
                    pool.tensor_tensor(nd1[:, b], neg[:, b], M3[:, b, :, :, 0], ALU.subtract).then_inc(neg_step, 1)
                    pool.wait_ge(neg_step, 4 * u + 2)
                    pool.tensor_copy(M3[:, b, :, :, 1], nd1[:, b]).then_inc(neg_step, 1)
                    pool.wait_ge(neg_step, 4 * u + 3)
                    pool.tensor_tensor(nd2[:, b], nd1[:, b], M3[:, b, :, :, 1], ALU.subtract).then_inc(neg_step, 1)
                    pool.wait_ge(neg_step, 4 * u + 4)
                    pool.tensor_copy(M3[:, b, :, :, 2], nd2[:, b]).then_inc(m3_ready, 1)
                elif e[0] == "values" and e[1] in DIAG:
                    m = e[1]
                    u, j = STEPS[m]
                    lo = P * (j - CT * UNITS[u][0])
                    pool.wait_ge(exp_done, 2 * m + 2)
                    pr = probs[:, m % PSLOT, :, lo:lo + P]
                    pool.affine_select(out=pr, in_=pr, compare_op=ALU.is_ge, fill=0.0, base=0,
                                       pattern=[[0, GH], [1, P]], channel_multiplier=-1).then_inc(masked, 1)
                    ndiag += 1

            pool.wait_ge(xs_zero, 64)
            pool.wait_ge(xn2_ready, NT)
            pool.wait_ge(dest_ready, TOPK)
            for i in range(NT):
                for k in range(TOPK):
                    pool.indirect_dma_start(xs, bass.IndirectOffsetOnAxis(ap=dest_i[:, k, i:i + 1], axis=0),
                                            xn[:, i, :], None).then_inc(scattered, 16)
            for q in range(RING):
                pool.wait_ge(y_out[q], 16 * SLOTS // RING)
            for n in range(TOPK * NT):
                i, k = n // TOPK, n % TOPK
                if n >= RING:
                    pool.wait_ge(mixed, n - RING + 1)
                pool.indirect_dma_start(yg[:, n % RING, :], None, ys,
                                        bass.IndirectOffsetOnAxis(ap=dest_i[:, k, i:i + 1], axis=0)
                                        ).then_inc(yg_in[n % RING], 16)

        @block.scalar
        def _(act):
            def root(c):
                act.wait_ge(ln_step, c + 1)
                act.activation(std[:, CT * c:CT * c + CT], var[:, CT * c:CT * c + CT], ACT.Sqrt).then_inc(std_done, 1)

            def take_xnT(c):
                for h in range(2):
                    act.wait_ge(xnT_ps, 2 * c + h + 1)
                    if c and h == 0:
                        act.wait_ge(qkv_ps, CT * c)
                    act.activation(xnT[:, 2 * h:2 * h + 2, :, :],
                                   ps[:, h, :].rearrange("p (i k t) -> p i k t", i=2, k=KC), ACT.Copy).then_inc(xnT_ready, 1)

            def parts(c):
                act.wait_ge(rope_step, 5 * c + 5)
                if c == 0:
                    act.wait_ge(consts, 8)
                act.activation(V[:, CT * c:CT * c + CT, :, 0:D],
                               ps[:, 2:6, (HQ + HK) * D:QKV].rearrange("p i (g d) -> p i g d", g=HK),
                               ACT.Copy).then_inc(v_ready, 1)
                if c:
                    act.wait_ge(stack_ps, NFILL * c)
                for i in range(CT):
                    act.activation(Qn[:, i, :, 0:3, :], qk[:, i, 0:HQ, :].unsqueeze(2).to_broadcast([P, HQ, 3, D]),
                                   ACT.Copy).then_inc(qpart, 1)
                for s in (0, 3, 5):
                    act.activation(Kn[:, :, :, s, :], qk[:, :, HQ:, :], ACT.Copy).then_inc(kpart, 1)
                act.wait_ge(split_step, 5 * c + 2)
                for i in range(CT):
                    act.activation(Qn[:, i, :, 3:5, :], res[:, i, 0:HQ, :].unsqueeze(2).to_broadcast([P, HQ, 2, D]),
                                   ACT.Copy).then_inc(qpart, 1)
                for s in (1, 4):
                    act.activation(Kn[:, :, :, s, :], res[:, :, HQ:, :], ACT.Copy).then_inc(kpart, 1)

            def take_stack(c):
                for f in range(1, NFILL, 2):
                    act.wait_ge(stack_ps, NFILL * c + f + 1)
                    dst = Qs[0:KROW, 2 * f:2 * f + 2] if f < HQ // 2 else Ks[0:KROW, 2 * f - HQ:2 * f - HQ + 2]
                    act.activation(dst[:, :, CW * c:CW * c + CW],
                                   ps[0:KROW, 7, :].bitcast(BF16).rearrange("p (h t) -> p h t", h=2),
                                   ACT.Copy).then_inc(stack_odd, 1)

            for c in range(NCH):
                root(c)
            for c in range(NCH):
                take_xnT(c)
                parts(c)
                take_stack(c)
            for e in ORDER:
                if e[0] != "score":
                    continue
                _, m, h = e
                u, j = STEPS[m]
                lo = max(0, P * (j - CT * UNITS[u][0]))
                act.wait_ge(s_ready, 2 * m + h + 1)
                if m >= PSLOT and h == 0:
                    act.wait_ge(pv_done, m - PSLOT + 1)
                act.activation(probs[:, m % PSLOT, 2 * h:2 * h + 2, lo:CW],
                               ps[:, SCB + 2 * h:SCB + 2 * h + 2, lo:CW], ACT.Exp, scale=SCALE).then_inc(exp_done, 1)

            act.wait_ge(var2_ready, 1)
            act.activation(std[:, :], var[:, :], ACT.Sqrt).then_inc(std2_done, 1)
            for f in range(1, NT // 2, 2):
                act.wait_ge(turn2_ps, f + 1)
                act.activation(xT_all[:, 2 * f:2 * f + 2, :, :],
                               ps[:, f % 4, :].rearrange("p (i k t) -> p i k t", i=2, k=KC), ACT.Copy).then_inc(turn2_act, 1)
            act.wait_ge(route, 2 * NT + 3)
            act.activation(lexp[:, :, :], lsub[:, :, :], ACT.Exp).then_inc(lexp_done, 1)

            def shared(t, q, turn, live):
                if live(1):
                    n, b = t + 1, (q + 1) % 2
                    act.wait_ge(gu_ready, n + 1)
                    if not isinstance(n, int) or n >= 2:
                        act.wait_ge(h_ready, n - 1)
                    act.activation(gate_act[:, b, :], ps[:, b, 0:SI], ACT.Silu).then_inc(silu_done, 1)
                if live(0):
                    n, b = t, q % 2
                    act.wait_ge(th_ready, n + 1)
                    if not isinstance(n, int) or n >= 2:
                        act.wait_ge(dn_ready, n - 1)
                    act.activation(hT[0:IH, b, :], ps[0:IH, 4 + b, :], ACT.Copy).then_inc(ht_taken, 1)

            pipeline(act.Fori, 0, NT, 1, 1, shared)

            def routed(t, q, turn, live):
                if live(1):
                    n, b = NT + t + 1, (q + 1) % 2
                    act.wait_ge(gu_ready, n + 1)
                    act.wait_ge(h_ready, n - 1)
                    act.activation(gate_act[:, b, 0:I], ps[:, b, 0:I], ACT.Silu).then_inc(silu_done, 1)
                if live(0):
                    n, b = NT + t, q % 2
                    act.wait_ge(th_ready, n + 1)
                    act.wait_ge(dn_ready, n - 1)
                    act.activation(hT[0:IH, b, 0:2 * P], ps[0:IH, 4 + b, 0:2 * P], ACT.Copy).then_inc(ht_taken, 1)

            pipeline(act.Fori, 0, SLOTS, 1, 1, routed)

        @block.vector
        def _(dve):
            def normalise(c, xsrc):
                t0, t1 = CT * c, CT * c + CT
                s = 7 * c
                dve.wait_ge(x_in[c], 16)
                for i in range(t0, t1):
                    dve.bn_stats(stats[:, i, :], xsrc[:, i, :]).then_inc(stats_done, 1)
                for i in range(t0, t1):
                    dve.wait_ge(stats_done, NT * 0 + 2 * t0 + (i - t0) + 1)
                    dve.bn_aggr(mv[:, i, :], stats[:, i, :]).then_inc(stats_done, 1)
                dve.wait_ge(stats_done, 2 * t1)
                dve.tensor_scalar(var[:, t0:t1], mv[:, t0:t1, 1], EPS, None, ALU.add).then_inc(ln_step, 1)

            def finish_normalise(c, xsrc):
                t0, t1 = CT * c, CT * c + CT
                s = 7 * c
                dve.wait_ge(std_done, c + 1)
                dve.reciprocal(rstd0[:, t0:t1], std[:, t0:t1]).then_inc(ln_step2, 1)
                s = 5 * c
                dve.wait_ge(ln_step2, s + 1)
                dve.tensor_tensor(newt[:, t0:t1], rstd0[:, t0:t1], rstd0[:, t0:t1], ALU.mult).then_inc(ln_step2, 1)
                dve.wait_ge(ln_step2, s + 2)
                dve.tensor_tensor(newt2[:, t0:t1], newt[:, t0:t1], var[:, t0:t1], ALU.mult).then_inc(ln_step2, 1)
                dve.wait_ge(ln_step2, s + 3)
                dve.tensor_scalar(newt3[:, t0:t1], newt2[:, t0:t1], -0.5, 1.5, ALU.mult, ALU.add).then_inc(ln_step2, 1)
                dve.wait_ge(ln_step2, s + 4)
                dve.tensor_tensor(rstd[:, t0:t1], newt3[:, t0:t1], rstd0[:, t0:t1], ALU.mult).then_inc(ln_step2, 1)
                dve.wait_ge(ln_step2, s + 5)
                if c == 0:
                    dve.wait_ge(xs_zero, 64)
                for i in range(t0, t1):
                    dve.tensor_scalar(xn[:, i, :], xsrc[:, i, :], mv[:, i, 0:1], rstd[:, i:i + 1],
                                      ALU.subtract, ALU.mult).then_inc(xn_ready, 1)

            def rotate(c):
                s = 5 * c
                dve.wait_ge(qkv_ps, CT * c + CT)
                if c == 0:
                    dve.wait_ge(w_in, 48)
                else:
                    dve.wait_ge(qpart, 8 * c)
                    dve.wait_ge(kpart, 5 * c)
                src = ps[:, 2:6, 0:(HQ + HK) * D].rearrange("p i (h d) -> p i h d", d=D)
                shape = [P, CT, HQ + HK, HALF]
                cos = rope_sb[:, CT * c:CT * c + CT, 0, :].unsqueeze(2).to_broadcast(shape)
                sin = rope_sb[:, CT * c:CT * c + CT, 1, :].unsqueeze(2).to_broadcast(shape)
                nsin = rope_sb[:, CT * c:CT * c + CT, 2, :].unsqueeze(2).to_broadcast(shape)
                a, b = slice(0, HALF), slice(HALF, D)
                dve.tensor_tensor(rc[:, :, :, a], src[:, :, :, a], cos, ALU.mult).then_inc(rope_step, 1)
                dve.tensor_tensor(rc[:, :, :, b], src[:, :, :, b], cos, ALU.mult).then_inc(rope_step, 1)
                dve.tensor_tensor(rs[:, :, :, a], src[:, :, :, b], nsin, ALU.mult).then_inc(rope_step, 1)
                dve.tensor_tensor(rs[:, :, :, b], src[:, :, :, a], sin, ALU.mult).then_inc(rope_step, 1)
                dve.wait_ge(rope_step, s + 4)
                dve.tensor_tensor(qk[:, :, :, :], rc[:, :, :, :], rs[:, :, :, :], ALU.add).then_inc(rope_step, 1)

            def split(c):
                s = 5 * c
                dve.wait_ge(rope_step, 5 * c + 5)
                dve.wait_ge(qpart, 8 * c + 4)
                dve.wait_ge(kpart, 5 * c + 3)
                dve.tensor_tensor(res[:, :, 0:HQ, :], qk[:, :, 0:HQ, :], Qn[:, :, :, 0, :], ALU.subtract).then_inc(split_step, 1)
                dve.tensor_tensor(res[:, :, HQ:, :], qk[:, :, HQ:, :], Kn[:, :, :, 0, :], ALU.subtract).then_inc(split_step, 1)
                dve.wait_ge(split_step, s + 2)
                dve.wait_ge(qpart, 8 * c + 8)
                dve.wait_ge(kpart, 5 * c + 5)
                dve.tensor_tensor(Qn[:, :, :, 5, :], res[:, :, 0:HQ, :], Qn[:, :, :, 3, :], ALU.subtract).then_inc(split_step, 1)
                dve.tensor_tensor(Kn[:, :, :, 2, :], res[:, :, HQ:, :], Kn[:, :, :, 1, :], ALU.subtract).then_inc(split_step, 1)
                dve.nop().then_inc(split_step, 1)

            def take_stack(c):
                for f in range(0, NFILL, 2):
                    dve.wait_ge(stack_ps, NFILL * c + f + 1)
                    dst = Qs[0:KROW, 2 * f:2 * f + 2] if f < HQ // 2 else Ks[0:KROW, 2 * f - HQ:2 * f - HQ + 2]
                    dve.tensor_copy(dst[:, :, CW * c:CW * c + CW],
                                    ps[0:KROW, 6, :].bitcast(BF16).rearrange("p (h t) -> p h t", h=2)).then_inc(stack_even, 1)

            dve.memset(Ks[KROW:P, :, :], 1.0).then_inc(ones_set, 1)
            dve.memset(zeros, 0.0).then_inc(zero_made, 1)
            for c in range(NCH):
                normalise(c, x_sb)
            for c in range(NCH):
                finish_normalise(c, x_sb)
            for c in range(NCH):
                rotate(c)
                split(c)
                take_stack(c)
            small = 0
            for e in ORDER:
                if e[0] == "max":
                    n = e[1]
                    u, hh, r, k = PIECES[n]
                    c = UNITS[u][0]
                    w = CW if k < c else P * (r + 1)
                    dve.wait_ge(a_ready, n + 1)
                    src = ps[:, MAXB + n % 2, 0:w]
                    if k < c:
                        dve.tensor_reduce(part[:, u % 2, hh, r, k:k + 1], src, AX.X, ALU.max).then_inc(a_used, 1)
                    else:
                        if n >= 2 * (NCH + 1):
                            dve.wait_ge(a_used, n - 1)
                        dve.tensor_tensor_reduce(junk[:, n % 2, 0:w], src, maskq[:, CW - w:CW], 1.0, 3 * NEG, ALU.add,
                                                 ALU.max, part[:, u % 2, hh, r, k:k + 1]).then_inc(a_used, 1)
                elif e[0] == "split":
                    u = e[1]
                    c = UNITS[u][0]
                    dve.wait_ge(a_used, PIECES_TO[u])
                    if u >= 2:
                        dve.wait_ge(m3_ready, u - 1)
                    dve.tensor_reduce(neg[:, u % 2], part[:, u % 2, :, :, 0:c + 1], AX.X, ALU.max,
                                      negate=True).then_inc(neg_ready, 1)
                elif e[0] == "shift":
                    _, u, h = e
                    c, g = UNITS[u]
                    small += 1
                    dve.wait_ge(small_ready, small)
                    h0 = GH * g + 2 * h
                    dve.tensor_copy(Qs[KROW:SROW, h0:h0 + 2, CW * c:CW * c + CW],
                                    ps[KROW:SROW, SMB, :].bitcast(BF16).rearrange("p (h t) -> p h t", h=2)
                                    ).then_inc(small_used, 1)
                elif e[0] == "take":
                    u = e[1]
                    dve.wait_ge(pv_done, STEPS_TO[u])
                    if u:
                        dve.wait_ge(small_ready, 1 + SMALL.index(("turn", u - 1)))
                    dve.tensor_copy(OT[:, :], ps[:, OB, :]).then_inc(o_copied, 1)
                elif e[0] == "turn":
                    u = e[1]
                    c, g = UNITS[u]
                    small += 1
                    dve.wait_ge(small_ready, small)
                    o = ps[:, SMB, :].rearrange("p (i h d) -> p i h d", i=CT, h=GH)
                    if u:
                        dve.wait_ge(small_used, SMALL.index(("turn", u - 1)) + 1)
                    dve.reciprocal(rden[:, :, :], o[:, :, :, D]).then_inc(rden_ready, 1)
                    dve.wait_ge(rden_ready, u + 1)
                    if g == 0 and c:
                        dve.wait_ge(small_ready, 1 + SMALL.index(("turn_out", c - 1, 1)))
                    dve.tensor_tensor(
                        attn[:, :, GH * D * g:GH * D * (g + 1)].rearrange("p i (h d) -> p i h d", h=GH), o[:, :, :, 0:D],
                        rden[:, :, :].unsqueeze(3).to_broadcast([P, CT, GH, D]), ALU.mult).then_inc(small_used, 1)
                elif e[0] == "turn_out":
                    small += 1
                    dve.wait_ge(small_ready, small)
                    _, c, h = e
                    dve.tensor_copy(aT[:, :, :, :], ps[:, SMB, :].rearrange("p (i k t) -> p i k t", i=2, k=KC)
                                    ).then_inc(small_used, 1)
                elif e[0] == "project":
                    small += 1
                    dve.wait_ge(small_ready, small)
                    _, c, h = e
                    xt = x_sb[:, CT * c + 2 * h:CT * c + 2 * h + 2, :]
                    dve.wait_ge(xn_ready, NT)
                    dve.tensor_tensor(xt, ps[:, SMB, :].rearrange("p (i n) -> p i n", i=2), xt, ALU.add
                                      ).then_inc(x2_done, 1)
                    dve.wait_ge(x2_done, 2 * c + h + 1)
                    dve.nop().then_inc(small_used, 1)

            for i in range(NT):
                dve.wait_ge(x2_done, i // 2 + 1)
                dve.bn_stats(stats[:, i, :], x_sb[:, i, :]).then_inc(stats2, 1)
            for i in range(NT):
                dve.wait_ge(stats2, i + 1)
                dve.bn_aggr(mv[:, i, :], stats[:, i, :]).then_inc(stats2, 1)
            dve.wait_ge(stats2, 2 * NT)
            dve.tensor_scalar(var[:, :], mv[:, :, 1], EPS, None, ALU.add).then_inc(var2_ready, 1)
            dve.wait_ge(std2_done, 1)
            dve.reciprocal(rstd0[:, :], std[:, :]).then_inc(ln2_step, 1)
            dve.wait_ge(ln2_step, 1)
            dve.tensor_tensor(newt[:, :], rstd0[:, :], rstd0[:, :], ALU.mult).then_inc(ln2_step, 1)
            dve.wait_ge(ln2_step, 2)
            dve.tensor_tensor(newt2[:, :], newt[:, :], var[:, :], ALU.mult).then_inc(ln2_step, 1)
            dve.wait_ge(ln2_step, 3)
            dve.tensor_scalar(newt3[:, :], newt2[:, :], -0.5, 1.5, ALU.mult, ALU.add).then_inc(ln2_step, 1)
            dve.wait_ge(ln2_step, 4)
            dve.tensor_tensor(rstd[:, :], newt3[:, :], rstd0[:, :], ALU.mult).then_inc(ln2_step, 1)
            dve.wait_ge(ln2_step, 5)
            for i in range(NT):
                dve.tensor_scalar(xn[:, i, :], x_sb[:, i, :], mv[:, i, 0:1], rstd[:, i:i + 1],
                                  ALU.subtract, ALU.mult).then_inc(xn2_ready, 1)
            for f in range(0, NT // 2, 2):
                dve.wait_ge(turn2_ps, f + 1)
                dve.tensor_copy(xT_all[:, 2 * f:2 * f + 2, :, :],
                                ps[:, f % 4, :].rearrange("p (i k t) -> p i k t", i=2, k=KC)).then_inc(turn2_dve, 1)

            dve.wait_ge(logits_ps, 1)
            dve.wait_ge(consts, 14)
            dve.tensor_copy(lg[:, :, :], ps[:, 6, 0:NT * E].rearrange("p (i e) -> p i e", i=NT)).then_inc(route, 1)
            dve.wait_ge(route, 1)
            for i in range(NT):
                dve.max(top[:, i, :], lg[:, i, :]).then_inc(route, 1)
            dve.wait_ge(route, 1 + NT)
            dve.tensor_tensor(lsub[:, :, 0:E], lg[:, :, :], top[:, :, 0:1].to_broadcast([P, NT, E]),
                              ALU.subtract).then_inc(route, 1)
            dve.tensor_tensor(lsub[:, :, E:E + 1], top[:, :, 1:2], top[:, :, 0:1], ALU.subtract).then_inc(route, 1)
            for i in range(NT):
                dve.max_index(top_i[:, i, :], top[:, i, :], lg[:, i, :]).then_inc(route, 1)
            R = 2 * NT + 3
            dve.wait_ge(route, R)
            dve.tensor_copy(top_f[:, :, :], top_i[:, :, 0:TOPK]).then_inc(route, 1)
            dve.wait_ge(route, R + 1)
            for k in range(TOPK):
                dve.tensor_tensor(hot[:, k], iota_e[:, :].unsqueeze(1).to_broadcast([P, NT, E]),
                                  top_f[:, :, k:k + 1].to_broadcast([P, NT, E]), ALU.is_equal).then_inc(route, 1)
            dve.wait_ge(route, R + 3)
            dve.tensor_tensor(hots[:, 0:NT, :], hot[:, 0], hot[:, 1], ALU.add).then_inc(hots_ready, 1)
            dve.wait_ge(lexp_done, 1)
            dve.tensor_reduce(lsum[:, :], lexp[:, :, 0:E], AX.X, ALU.add).then_inc(route, 1)
            dve.wait_ge(route, R + 4)
            dve.reciprocal(wtok[:, 0, :], lsum[:, :]).then_inc(route, 1)
            dve.wait_ge(route, R + 5)
            dve.tensor_tensor(wtok[:, 1, :], wtok[:, 0, :], lexp[:, :, E], ALU.mult).then_inc(route, 1)
            dve.wait_ge(pos_ps, 1)
            dve.tensor_scalar(cnt_i[:, :], ps[:, 7, NT * E:(NT + 1) * E], P - 1.0, None, ALU.add).then_inc(route, 1)
            dve.wait_ge(route, R + 7)
            dve.tensor_scalar(cnt_t[:, :], cnt_i[:, :], int(math.log2(P)), None, ALU.logical_shift_right).then_inc(route, 1)
            dve.wait_ge(route, R + 8)
            dve.tensor_copy(tiles[:, :], cnt_t[:, :]).then_inc(route, 1)
            dve.tensor_copy(csum[:, 0, 8:], cnt_t[:, :]).then_inc(route, 1)
            dve.wait_ge(route, R + 10)
            for n, d in enumerate((1, 2, 4, 8)):
                a, b = csum[:, n % 2, :], csum[:, (n + 1) % 2, :]
                dve.tensor_tensor(b[:, 8:], a[:, 8:], a[:, 8 - d:8 - d + E], ALU.add).then_inc(route, 1)
                dve.wait_ge(route, R + 11 + n)
            ends = csum[:, 0, 8:]
            dve.tensor_tensor(s_cmp[:, :, :], iota_s[0:1, :].unsqueeze(2).to_broadcast([1, SLOTS, E]),
                              ends[0:1, :].unsqueeze(1).to_broadcast([1, SLOTS, E]), ALU.is_ge).then_inc(route, 1)
            dve.tensor_tensor(base0[:, :], ends, tiles[:, :], ALU.subtract).then_inc(route, 1)
            dve.wait_ge(route, R + 16)
            dve.tensor_scalar(base[:, :], base0[:, :], float(P), None, ALU.mult).then_inc(route, 1)
            dve.tensor_reduce(s_exp[:, :], s_cmp[:, :, :], AX.X, ALU.add).then_inc(route, 1)
            dve.wait_ge(route, R + 18)
            dve.tensor_scalar(s_exp_i[:, :], s_exp[:, :], float(E - 1), None, ALU.min).then_inc(slots_ready, 1)
            dve.tensor_tensor(where[:, :, :], ps[:, 7, 0:NT * E].rearrange("p (i e) -> p i e", i=NT),
                              base[:, :].unsqueeze(1).to_broadcast([P, NT, E]), ALU.add).then_inc(route, 1)
            dve.wait_ge(route, R + 19)
            for k in range(TOPK):
                dve.tensor_tensor(wsel[:, k], hot[:, k], where[:, :, :], ALU.mult).then_inc(route, 1)
            dve.wait_ge(route, R + 21)
            dve.tensor_reduce(dest[:, :, :], wsel[:, :, :, :], AX.X, ALU.add).then_inc(route, 1)
            dve.wait_ge(route, R + 22)
            for k in range(TOPK):
                dve.tensor_copy(dest_i[:, k, :], dest[:, k, :]).then_inc(dest_ready, 1)

            def shared(t, q, turn, live):
                if live(1):
                    n, b = t + 1, (q + 1) % 2
                    dve.wait_ge(silu_done, n + 1)
                    if not isinstance(n, int) or n >= 2:
                        dve.wait_ge(th_ready, n - 1)
                    dve.tensor_tensor(hidden[:, b, :], gate_act[:, b, :], ps[:, 2 + b, 0:SI], ALU.mult).then_inc(h_ready, 1)
                if live(-1):
                    n, b = t - 1, (q - 1) % 2
                    dve.wait_ge(dn_ready, n + 1)
                    xt = x_sb[:, bass.ds(n, 1), :]
                    dve.tensor_tensor(xt, ps[:, 6 + b, 0:C].unsqueeze(1), xt, ALU.add).then_inc(y_taken, 1)

            pipeline(dve.Fori, 0, NT, 1, 1, shared)

            def routed(t, q, turn, live):
                if live(2):
                    s, b = t + 2, q % 2
                    dve.wait_ge(xt_ready, s + 1)
                    dve.wait_ge(gu_ready, NT + s - 1)
                    dve.tensor_copy(xgT[:, b, :], ps[:, 2 + b, 0:KC * P]).then_inc(xt_taken, 1)
                if live(1):
                    n, b = NT + t + 1, (q + 1) % 2
                    dve.wait_ge(silu_done, n + 1)
                    dve.wait_ge(th_ready, n - 1)
                    dve.tensor_tensor(hidden[:, b, 0:I], gate_act[:, b, 0:I], ps[:, b, I:2 * I], ALU.mult).then_inc(h_ready, 1)
                if live(-1):
                    n, r, b = NT + t - 1, (q - 1) % RING, (q - 1) % 2
                    dve.wait_ge(dn_ready, n + 1)
                    if not isinstance(t, int) or t - 1 >= RING:
                        dve.wait_ge(y_out[r], 16 * (turn + (q - 1) // RING))
                    dve.tensor_copy(yb[:, r, :], ps[:, 6 + b, 0:C]).then_inc(y_taken, 1)

            pipeline(dve.Fori, 0, SLOTS, 2, 1, routed)
            for n in range(TOPK * NT):
                i, k = n // TOPK, n % TOPK
                dve.wait_ge(yg_in[n % RING], 16 * (n // RING + 1))
                if k:
                    dve.wait_ge(mixed, n)
                dve.scalar_tensor_tensor(out=x_sb[:, i, :], in0=yg[:, n % RING, :], scalar=wtok[:, k, i:i + 1],
                                         in1=x_sb[:, i, :], op0=ALU.mult, op1=ALU.add).then_inc(mixed, 1)

        @block.tensor
        def _(pe):
            def turn_x(c):
                for h in range(2):
                    pe.wait_ge(xn_ready, CT * c + 2 * h + 2)
                    if c:
                        pe.wait_ge(xnT_ready, 2 * (c - 1) + h + 1)
                    for i in range(2):
                        for k in range(KC):
                            t = pe.transpose(ps[:, h, (2 * i + k) * P:(2 * i + k + 1) * P],
                                             xn[:, CT * c + 2 * h + i, k * P:(k + 1) * P], identf[:, :])
                    t.then_inc(xnT_ps, 1)

            def project_qkv(c):
                if c == 0:
                    pe.wait_ge(w_in, 48)
                else:
                    pe.wait_ge(v_ready, c)
                    pe.wait_ge(rope_step, 5 * c)
                for i in range(CT):
                    pe.wait_ge(xnT_ready, 2 * c + i // 2 + 1)
                    for k in range(KC):
                        m = pe.matmul(ps[:, 2 + i, 0:QKV], xnT[:, i, k, :], wqkv_sb[:, k, :],
                                      start=(k == 0), stop=(k == KC - 1))
                    m.then_inc(qkv_ps, 1)

            def turn_stack(c):
                pe.wait_ge(split_step, 5 * c + 5)
                pe.wait_ge(qpart, 8 * c + 8)
                pe.wait_ge(kpart, 5 * c + 5)
                for f in range(NFILL):
                    n = NFILL * c + f
                    if n >= 2:
                        pe.wait_ge((stack_even, stack_odd)[f % 2], n // 2)
                    bank = ps[0:KROW, 6 + f % 2, :].bitcast(BF16)
                    for h in range(2):
                        for i in range(CT):
                            hh = 2 * f + h
                            src = Qn[:, i, hh] if hh < HQ else Kn[:, i, hh - HQ]
                            t = pe.transpose(bank[:, (CT * h + i) * P:(CT * h + i + 1) * P],
                                             src.rearrange("p s d -> p (s d)"), identb[:, :])
                    t.then_inc(stack_ps, 1)

            pe.wait_ge(consts, 8)
            pe.wait_ge(ones_set, 1)
            for c in range(NCH):
                turn_x(c)
                project_qkv(c)
                turn_stack(c)
            pe.wait_ge(stack_even, NCH * NFILL // 2)
            pe.wait_ge(stack_odd, NCH * NFILL // 2)
            small = 0
            for e in ORDER:
                if e[0] in ("shift", "turn", "turn_out", "project"):
                    if small:
                        pe.wait_ge(small_used, small)
                    small += 1
                if e[0] == "max":
                    n = e[1]
                    u, hh, r, k = PIECES[n]
                    c, g = UNITS[u]
                    w = CW if k < c else P * (r + 1)
                    if n >= 2:
                        pe.wait_ge(a_used, n - 1)
                    t = (CT * c + r) * P
                    pe.matmul(ps[:, MAXB + n % 2, 0:w], Qs[0:KROW, GH * g + hh, t:t + P],
                              Ks[0:KROW, g, CW * k:CW * k + w], start=True, stop=True).then_inc(a_ready, 1)
                elif e[0] == "shift":
                    _, u, h = e
                    pe.wait_ge(m3_ready, u + 1)
                    bank = ps[KROW:SROW, SMB, :].bitcast(BF16)
                    for q in range(2):
                        for r in range(CT):
                            t = pe.transpose(bank[:, (CT * q + r) * P:(CT * q + r + 1) * P],
                                             M3[:, u % 2, 2 * h + q, r, 0:MROW], identb[:, :])
                    t.then_inc(small_ready, 1)
                elif e[0] == "score":
                    _, m, h = e
                    u, j = STEPS[m]
                    c, g = UNITS[u]
                    lo = max(0, P * (j - CT * c))
                    if j == 0 and h == 0:
                        pe.wait_ge(small_used, SMALL.index(("shift", u, 1)) + 1)
                    if m:
                        pe.wait_ge(exp_done, 2 * (m - 1) + h + 1)
                    for q in range(2):
                        s = pe.matmul(ps[:, SCB + 2 * h + q, lo:CW], Ks[0:SROW, g, P * j:P * j + P],
                                      Qs[0:SROW, GH * g + 2 * h + q, CW * c + lo:CW * (c + 1)], start=True, stop=True)
                    s.then_inc(s_ready, 1)
                elif e[0] == "values":
                    m = e[1]
                    u, j = STEPS[m]
                    c, g = UNITS[u]
                    lo = max(0, P * (j - CT * c))
                    if m in DIAG:
                        pe.wait_ge(masked, DIAG.index(m) + 1)
                    else:
                        pe.wait_ge(exp_done, 2 * m + 2)
                    if j == 0 and u:
                        pe.wait_ge(o_copied, u)
                    for hh in range(GH):
                        o = pe.matmul(ps[VC * hh:VC * hh + VC, OB, lo:CW], V[:, j, g, :], probs[:, m % PSLOT, hh, lo:CW],
                                      start=(j == 0), stop=(j == key_blocks(c) - 1))
                    o.then_inc(pv_done, 1)
                elif e[0] == "turn":
                    u = e[1]
                    pe.wait_ge(o_copied, u + 1)
                    for i in range(CT):
                        t = pe.transpose(ps[:, SMB, i * P:(i + 1) * P], OT[:, i * P:(i + 1) * P], identf[:, :])
                    t.then_inc(small_ready, 1)
                elif e[0] == "turn_out":
                    _, c, h = e
                    pe.wait_ge(small_used, 1 + SMALL.index(("turn", HK * c + HK - 1)))
                    for i in range(2):
                        for k in range(KC):
                            t = pe.transpose(ps[:, SMB, (2 * i + k) * P:(2 * i + k + 1) * P],
                                             attn[:, 2 * h + i, k * P:(k + 1) * P], identf[:, :])
                    t.then_inc(small_ready, 1)
                elif e[0] == "project":
                    for i in range(2):
                        for k in range(KC):
                            t = pe.matmul(ps[:, SMB, i * C:(i + 1) * C], aT[:, i, k, :], wp_sb[:, k, :],
                                          start=(i == 0 and k == 0), stop=(k == KC - 1), skip_group_check=True)
                    t.then_inc(small_ready, 1)

            pe.wait_ge(small_used, len(SMALL))
            pe.wait_ge(o_copied, len(UNITS))
            for f in range(NT // 2):
                pe.wait_ge(xn2_ready, 2 * f + 2)
                if f >= 4:
                    pe.wait_ge((turn2_dve, turn2_act)[f % 2], f // 2 - 1)
                for i in range(2):
                    for k in range(KC):
                        t = pe.transpose(ps[:, f % 4, (2 * i + k) * P:(2 * i + k + 1) * P],
                                         xn[:, 2 * f + i, k * P:(k + 1) * P], identf[:, :])
                t.then_inc(turn2_ps, 1)
            pe.wait_ge(turn2_dve, NT // 4)
            pe.wait_ge(turn2_act, NT // 4)
            pe.wait_ge(ffn_w, 48)
            for i in range(NT):
                for k in range(KC):
                    t = pe.matmul(ps[:, 6, i * E:(i + 1) * E], xT_all[:, i, k, :], wgate_sb[:, k, :],
                                  start=(i == 0 and k == 0), stop=(k == KC - 1), skip_group_check=True)
            t.then_inc(logits_ps, 1)

            def places():
                pe.wait_ge(hots_ready, 1)
                pe.wait_ge(consts, 14)
                pe.matmul(ps[:, 7, 0:(NT + 1) * E], before[:, :], hots[:, :, :].rearrange("p i e -> p (i e)"),
                          start=True, stop=False)
                for i in range(NT):
                    t = pe.matmul(ps[:, 7, (i + 1) * E:(NT + 1) * E].rearrange("p (i e) -> p i e", e=E), onesb[:, :],
                                  hots[:, i:i + 1, :].to_broadcast([P, NT - i, E]), start=False, stop=(i == NT - 1))
                t.then_inc(pos_ps, 1)

            def turn_hidden(n, b, tiles_n):
                pe.wait_ge(h_ready, n + 1)
                if not isinstance(n, int) or n >= 2:
                    pe.wait_ge(ht_taken, n - 1)
                for k in range(tiles_n):
                    t = pe.transpose(ps[0:IH, 4 + b, k * P:(k + 1) * P], hidden[:, b, k * IH:(k + 1) * IH], identf[:, :])
                t.then_inc(th_ready, 1)

            def shared(t, q, turn, live):
                if live(1):
                    n, b = t + 1, (q + 1) % 2
                    if not isinstance(n, int) or n >= 2:
                        pe.wait_ge(h_ready, n - 1)
                    for half in range(2):
                        for k in range(KC):
                            m = pe.matmul(ps[:, 2 * half + b, 0:SI], shared_x(n, k), wsgu_sb[:, k, half * SI:(half + 1) * SI],
                                          start=(k == 0), stop=(k == KC - 1))
                    m.then_inc(gu_ready, 1)
                if live(0):
                    turn_hidden(t, q % 2, SH)
                if live(-1):
                    n, b = t - 1, (q - 1) % 2
                    pe.wait_ge(ht_taken, n + 1)
                    if not isinstance(n, int) or n >= 2:
                        pe.wait_ge(y_taken, n - 1)
                    for k in range(SH):
                        m = pe.matmul(ps[:, 6 + b, 0:C], hT[0:IH, b, k * P:(k + 1) * P], wsdn_sb[0:IH, k, :],
                                      start=(k == 0), stop=(k == SH - 1))
                    m.then_inc(dn_ready, 1)

            def shared_x(n, k):
                return xT_all[:, n, k, :]

            places()
            pe.wait_ge(route, 2 * NT + 3 + 19)
            for t in range(-1, NT + 1):
                shared(t, t % RING, t // RING, lambda d, t=t: 0 <= t + d < NT)

            pe.wait_ge(slots_ready, 1)
            pe.wait_ge(expert_w, 32)

            def routed(t, q, turn, live):
                if live(2):
                    s, b, r = t + 2, q % 2, (q + 2) % RING
                    pe.wait_ge(xg_in[r], 16 * (turn + (q + 2) // RING + 1))
                    if not isinstance(s, int) or s >= 2:
                        pe.wait_ge(xt_taken, s - 1)
                    for k in range(KC):
                        m = pe.transpose(ps[:, 2 + b, k * P:(k + 1) * P], xg[:, r, k * P:(k + 1) * P], identf[:, :])
                    m.then_inc(xt_ready, 1)
                if live(1):
                    s, n, b = t + 1, NT + t + 1, (q + 1) % 2
                    e = pe.value_load(s_exp_i[0:1, bass.ds(s, 1)], min_val=0, max_val=E - 1)
                    pe.wait_ge(xt_taken, s + 1)
                    pe.wait_ge(h_ready, n - 1)
                    for k in range(KC):
                        m = pe.matmul(ps[:, b, 0:2 * I], xgT[:, b, k * P:(k + 1) * P],
                                      wgu_sb[:, bass.ds(e, 1), k, :], start=(k == 0), stop=(k == KC - 1))
                    m.then_inc(gu_ready, 1)
                if live(0):
                    turn_hidden(NT + t, q % 2, 2)
                if live(-1):
                    s, n, b = t - 1, NT + t - 1, (q - 1) % 2
                    e = pe.value_load(s_exp_i[0:1, bass.ds(s, 1)], min_val=0, max_val=E - 1)
                    pe.wait_ge(ht_taken, n + 1)
                    pe.wait_ge(y_taken, n - 1)
                    for k in range(2):
                        m = pe.matmul(ps[:, 6 + b, 0:C], hT[0:IH, b, k * P:(k + 1) * P],
                                      wdn_sb[:, bass.ds(e, 1), k, :], start=(k == 0), stop=(k == 1))
                    m.then_inc(dn_ready, 1)

            pipeline(pe.Fori, 0, SLOTS, 2, 1, routed)


def rope_table():
    import numpy as np
    inv = (1.0 / np.float32(10000.0) ** (np.arange(HALF, dtype=np.float32) / np.float32(HALF))).astype(np.float32)
    ang = (np.arange(T, dtype=np.float32)[:, None] * inv[None, :]).astype(np.float32).astype(np.float64)
    tab = np.stack([np.cos(ang), np.sin(ang), -np.sin(ang)], 1).astype(np.float32)
    return np.ascontiguousarray(tab.reshape(NT, P, 3, HALF).transpose(1, 0, 2, 3))


def layout(inputs):
    import numpy as np
    a = {k: np.asarray(v) for k, v in inputs.items()}
    rows = lambda w: np.ascontiguousarray(w.T.reshape(KC, P, -1).transpose(1, 0, 2))
    wqkv = np.concatenate([a["L0_attn_Wq"], a["L0_attn_Wk"], a["L0_attn_Wv"]], 0)
    return {"x": np.ascontiguousarray(a["L0_attn_x"].reshape(T, C)), "wqkv": rows(wqkv), "wp": rows(a["L0_attn_Wp"]),
            "rope": rope_table(), "wgate": rows(a["L0_ffn_gate_w"]),
            "wgu": np.ascontiguousarray(a["L0_ffn_w_gate_up"].reshape(E, KC, P, 2 * I).transpose(2, 0, 1, 3)),
            "wdn": np.ascontiguousarray(a["L0_ffn_w_down"].reshape(E, 2, IH, C).transpose(2, 0, 1, 3)),
            "wsgu": rows(a["L0_ffn_shared_gate_up"].T),
            "wsdn": np.ascontiguousarray(a["L0_ffn_shared_down"].reshape(SH, IH, C).transpose(1, 0, 2))}


def kernel(**inputs):
    import concourse.bacc as bacc
    from concourse.bass_utils import run_bass_kernel_spmd
    arrays = layout(inputs)
    nc = bacc.Bacc("TRN2", target_bir_lowering=False, num_devices=1)
    args = {k: nc.dram_tensor(k, v.shape, mybir.dt.from_np(v.dtype), kind="ExternalInput").ap() for k, v in arrays.items()}
    out = nc.dram_tensor("out", (T, C), F32, kind="ExternalOutput").ap()
    program(nc, **args, out=out)
    r = run_bass_kernel_spmd(nc, [arrays], core_ids=[0])
    return r.results[0]["out"].reshape(1, T, C)
```

```python
import math
from contextlib import ExitStack

import concourse.bass as bass
from concourse import mybir

F32 = mybir.dt.float32
BF16 = mybir.dt.bfloat16
I32 = mybir.dt.int32
U32 = mybir.dt.uint32
ALU = mybir.AluOpType
ACT = mybir.ActivationFunctionType
AX = mybir.AxisListType

P = 128
T, C = 2048, 256
NT = T // P
HQ, HK, D = 16, 4, 16
GH = HQ // HK
HALF = D // 2
QKV = (HQ + 2 * HK) * D
KC = C // P
NCH, CT, CW = 4, 4, 512
NP_ = 6
KROW = NP_ * D
MROW = 3
SROW = KROW + MROW
VC = 32
NEG = -1.0e30
EPS = 1e-5
SCALE = D ** -0.5
PSLOT = 3
E, I = 16, 176
TOPK = 2
IH = I // 2
SI = 2 * I
SH = SI // IH
SLOTS = (TOPK * T + E * (P - 1)) // P
SLOTS += -SLOTS % 4
RING = 4

CHUNKS = [0, 2, 3, 1]
LAST = NCH - 1
TILES = [CT * c + i for c in CHUNKS for i in range(CT)]
EARLY = 8
LATE0 = EARLY + SLOTS
UNITS = [(c, g) for c in CHUNKS for g in range(HK)]


def key_blocks(c):
    return CT * (c + 1)


STEPS = [(u, j) for u, (c, g) in enumerate(UNITS) for j in range(key_blocks(c))]
PIECES = [(u, hh, r, k) for u, (c, g) in enumerate(UNITS) for r in range(CT) for hh in range(GH)
          for k in range(c + 1)]
STEPS_TO = [sum(1 for s in STEPS if s[0] <= u) for u in range(len(UNITS))]
PIECES_TO = [sum(1 for a in PIECES if a[0] <= u) for u in range(len(UNITS))]
DIAG = [m for m, (u, j) in enumerate(STEPS) if j >= CT * UNITS[u][0]]


def attention_order():
    AHEAD, TO_SHIFT, APART = 3.0, 1.0, 0.7
    order = []
    later = []
    length = [1.0 - max(0, j - CT * UNITS[u][0]) / CT for u, j in STEPS]
    start = [sum(length[:m]) for m in range(len(STEPS))]
    work = [0.15 + (1.0 if k < UNITS[u][0] else (r + 1) / CT) for u, hh, r, k in PIECES]
    done_to = [0.0]
    for w in work:
        done_to.append(done_to[-1] + w)
    first = [start[STEPS_TO[u] - key_blocks(c)] for u, (c, g) in enumerate(UNITS)]
    taken = 0

    def take_maxima(now, ahead, unit):
        nonlocal taken
        left = [(done_to[PIECES_TO[v]] - done_to[taken]) / max(first[v] - AHEAD - now, 1e-3)
                for v in range(unit + 1, len(UNITS)) if PIECES_TO[v] > taken]
        goal = done_to[taken] + max(left, default=0.0) * ahead + carried[0]
        while taken < len(PIECES) and done_to[taken] + work[taken] / 2 < goal and PIECES[taken][0] < unit + DEEP:
            order.append(("max", taken))
            taken += 1
            u = PIECES[taken - 1][0]
            if taken == PIECES_TO[u]:
                order.append(("split", u))
                later.append((now + TO_SHIFT, ("shift", u, 0)))
                later.append((now + TO_SHIFT + APART, ("shift", u, 1)))
        carried[0] = min(goal - done_to[taken], 1.0)

    carried = [0.0]

    def take(u, now):
        order.append(("take", u))
        later.append((now + 1.0, ("turn", u)))
        if u % HK == HK - 1:
            n = u // HK
            for k in range(4):
                later.append((now + 2.0 + k, (("turn_out", "project")[k % 2], n, k // 2)))
            for k, e in enumerate((("stats", n), ("root", n), ("norm", n), ("apply", n), ("turn_x", n, 0),
                                   ("turn_x", n, 1), ("logits", n), ("rank", n))):
                later.append((now + 6.0 + k, e))

    def take_later(upto, must=()):
        for x in sorted(x for x in later if x[0] <= upto or x[1][0:2] == must):
            later.remove(x)
            order.append(x[1])

    for n in range(PIECES_TO[0]):
        order.append(("max", n))
    taken = PIECES_TO[0]
    order.append(("split", 0))
    order.append(("shift", 0, 0))
    order.append(("shift", 0, 1))
    order.append(("score", 0, 0))
    order.append(("score", 0, 1))
    for m, (u, j) in enumerate(STEPS):
        more = m + 1 < len(STEPS)
        q = length[m] / 4
        take_later(start[m], ("shift", STEPS[m + 1][0]) if more and STEPS[m + 1][1] == 0 else ())
        if more:
            order.append(("score", m + 1, 0))
        take_maxima(start[m], q, u)
        if m:
            order.append(("values", m - 1, 0))
        take_maxima(start[m] + q, q, u)
        if more:
            order.append(("score", m + 1, 1))
        take_maxima(start[m] + 2 * q, q, u)
        if m:
            order.append(("values", m - 1, 1))
        take_maxima(start[m] + 3 * q, q, u)
        if m in STEPS_TO:
            take(u - 1, start[m])
    order += [("shared", 0), ("values", m, 0), ("values", m, 1)]
    take(u, 1e6)
    take_later(2e6)
    order += [("shared", 1)]
    take_later(1e9)
    return order


DEEP = 4
ORDER = attention_order()
USES = [e for e in ORDER if e[0] in ("max", "shift", "turn", "turn_out", "project", "turn_x", "logits")]
RBANKS = 3
BANK = {e: n % RBANKS for n, e in enumerate(USES)}
for e in (("turn_x", LAST, 0), ("turn_x", LAST, 1), ("logits", LAST), ("places",), ("tokens",)):
    if e not in BANK:
        USES.append(e)
    BANK[e] = 1 + len(USES) % 2 if e[0] in ("places", "tokens") else BANK[e]
USE = {e: n for n, e in enumerate(USES)}
BEFORE = {e: max([0] + [i + 1 for i in range(n) if BANK[USES[i]] == BANK[e]]) for e, n in USE.items()}


def ring_loop(fori, step):
    def straight(t0, t1):
        for t in range(t0, t1):
            step(t, t % RING, t // RING, lambda d, t=t: t + d < SLOTS)

    loops = (SLOTS - 3) // RING - 1
    straight(0, RING)
    with fori(0, loops) as b:
        for q in range(RING):
            step(RING + q + RING * b, q, 1 + b, lambda d: True)
    straight(RING + RING * loops, SLOTS)


def program(nc, x, wqkv, wp, rope, wgate, wgu, wdn, wsgu, wsdn, out):
    with ExitStack() as ctx:
        def sb(name, shape, dt=F32):
            return ctx.enter_context(nc.sbuf_tensor(name, shape, dt))

        def sem(name):
            return ctx.enter_context(nc.semaphore(name))

        ps = ctx.enter_context(nc.psum_tensor("ps", [P, 8, 512], F32))
        SCB, OB = 3, 7

        x_sb = sb("x_sb", [P, NT, C])
        xn = sb("xn", [P, NT, C])
        wp_sb = sb("wp_sb", [P, KC, C])
        rope_sb = sb("rope_sb", [P, NT, 3, HALF])
        big = sb("big", [P, (HQ + HK) * T], BF16)
        Qs = big[:, 0:HQ * T].rearrange("p (h t) -> p h t", h=HQ)
        Ks = big[:, HQ * T:].rearrange("p (h t) -> p h t", h=HK)
        bigf = big[:, :].bitcast(F32)
        GU0, DN0 = 0, E * KC * 2 * I
        wgu_sb = bigf[:, GU0:DN0].rearrange("p (e k n) -> p e k n", e=E, k=KC)
        wdn_sb = bigf[0:IH, DN0:DN0 + E * 2 * C].rearrange("p (e k n) -> p e k n", e=E, k=2)
        early = sb("early", [P, NT * C + CT * KC * P + 512])
        at = [0]

        def piece(n):
            at[0] += n
            return early[:, at[0] - n:at[0]]

        xnT = piece(CT * KC * P).rearrange("p (i k t) -> p i k t", i=CT, k=KC)
        wqkv_sb = piece(KC * QKV).rearrange("p (k n) -> p k n", k=KC)
        PARTW = CT * NP_ * D
        Qn = [piece(HQ * PARTW // 2).bitcast(BF16).rearrange("p (h n) -> p h n", h=HQ), Qs[:, :, T - CW:T - CW + PARTW]]
        Kn = [piece(HK * PARTW // 2).bitcast(BF16).rearrange("p (h n) -> p h n", h=HK), Ks[:, :, T - CW:T - CW + PARTW]]

        def part_of(parts, c, i, slots):
            v = parts[c % 2].rearrange("p h (i s d) -> p h i s d", i=CT, s=NP_)
            return v[:, :, i, slots, :]

        xT_all = early[:, 0:NT * C].rearrange("p (i k t) -> p i k t", i=NT, k=KC)
        V = sb("V", [P, NT, HK, VC])
        stats = sb("stats", [P, NT, 6])
        mv = sb("mv", [P, NT, 2])
        var = sb("var", [P, NT])
        std = sb("std", [P, NT])
        rstd0 = sb("rstd0", [P, NT])
        newt = sb("newt", [P, NT])
        newt2 = sb("newt2", [P, NT])
        newt3 = sb("newt3", [P, NT])
        rstd = sb("rstd", [P, NT])
        nmr = sb("nmr", [P, NT])
        probs = sb("probs", [P, PSLOT, GH, CW])
        scratch = probs[:, :, :, :].rearrange("p s h t -> p (s h t)")
        RQ = CT * (HQ + HK) * D
        rc, qk0, qk1, res = (scratch[:, i * RQ:(i + 1) * RQ].rearrange("p (i h d) -> p i h d", i=CT, d=D)
                             for i in range(4))
        qk = [qk0, qk1]
        identf = sb("identf", [P, P])
        identb = sb("identb", [P, P], BF16)
        maskq = sb("maskq", [P, 2 * CW - P])
        junk = sb("junk", [P, 2, CW])
        part = sb("part", [P, DEEP, GH, CT, NCH])
        neg = sb("neg", [P, DEEP, GH, CT])
        nd1 = sb("nd1", [P, DEEP, GH, CT])
        nd2 = sb("nd2", [P, DEEP, GH, CT])
        M3 = sb("M3", [P, DEEP, GH, CT, 4], BF16)
        OT = sb("OT", [P, CW])
        rden = sb("rden", [P, CT, GH])
        attn = sb("attn", [P, CT, C])
        aT = sb("aT", [P, 2, KC, P])

        at[0] = 0

        def ffn(n, size):
            at[0] += n * size
            return scratch[:, at[0] - n * size:at[0]].rearrange("p (n m) -> p n m", n=n)

        gate_act = ffn(2, SI)
        hidden = ffn(2, SI)
        hT = ffn(2, SH * P)
        xg = ffn(RING, C)
        xgT = ffn(2, KC * P)
        yb = ffn(RING, C)
        YG = 12
        at[0] -= 2 * RING * C + 2 * KC * P
        yg = ffn(YG, C)
        at[0] -= YG * C
        pos_hot = ffn(TOPK * NT, P // 2).bitcast(BF16)
        slot_val = ffn(TOPK * NT, SLOTS).bitcast(BF16)
        wgate_sb = sb("wgate_sb", [P, KC, E])
        wsgu_sb = sb("wsgu_sb", [P, KC, 2 * SI])
        wsdn_sb = sb("wsdn_sb", [P, SH, C])
        junk_f = junk[:, :, :].rearrange("p a b -> p (a b)")
        slot_hot = attn[:, :, :].rearrange("p a b -> p (a b)").bitcast(BF16)[:, 0:TOPK * NT * SLOTS].rearrange(
            "p (n s) -> p n s", n=TOPK * NT)
        late = early[:, NT * C:]
        hot, wsel = (junk_f[:, i * TOPK * NT * E:(i + 1) * TOPK * NT * E]
                     .rearrange("p (k i e) -> p k i e", k=TOPK, i=NT) for i in range(2))
        where, lg = (late[:, i * NT * E:(i + 1) * NT * E].rearrange("p (i e) -> p i e", i=NT) for i in range(2))
        lsub = late[:, 2 * NT * E:2 * NT * E + NT * (E + 1)].rearrange("p (i e) -> p i e", i=NT)
        lexp = late[:, 2 * NT * E + NT * (E + 1):2 * NT * E + 2 * NT * (E + 1)].rearrange("p (i e) -> p i e", i=NT)
        iota_e = sb("iota_e", [P, E])
        iota_s = sb("iota_s", [P, SLOTS])
        iota_p = sb("iota_p", [P, P])
        own_p = sb("own_p", [P, 1])
        tile_p = sb("tile_p", [P, NT])
        before = sb("before", [P, P], BF16)
        onesb = sb("onesb", [P, P], BF16)
        top = sb("top", [P, NT, 8])
        top_i = sb("top_i", [P, NT, 8], U32)
        top_f = sb("top_f", [P, NT, TOPK])
        lsum = sb("lsum", [P, NT])
        wtok = sb("wtok", [P, TOPK, NT])
        hots = sb("hots", [P, NT + 1, E], BF16)
        cnt_i = sb("cnt_i", [P, E], I32)
        cnt_t = sb("cnt_t", [P, E], I32)
        tiles = sb("tiles", [P, E])
        csum = sb("csum", [P, 2, 8 + E])
        base0 = sb("base0", [P, E])
        base = sb("base", [P, E])
        dest = sb("dest", [P, TOPK, NT])
        dest_i = sb("dest_i", [P, TOPK, NT], U32)
        slot_i = sb("slot_i", [P, TOPK, NT], U32)
        pos_i = sb("pos_i", [P, TOPK, NT], U32)
        slot_f = sb("slot_f", [P, TOPK, NT])
        pos_f = sb("pos_f", [P, TOPK, NT])
        tok_p = sb("tok_p", [P, SLOTS])
        tok_i = sb("tok_i", [P, SLOTS], U32)
        s_cmp = V[:, :, :, :].rearrange("p i g d -> p (i g d)")[0:1, 0:SLOTS * E].rearrange("p (s e) -> p s e", e=E)
        s_exp = sb("s_exp", [1, SLOTS])
        s_exp_i = sb("s_exp_i", [1, SLOTS], I32)

        xd = nc.dram_tensor("xd", (T, C), F32, kind="Internal").ap()
        ys = nc.dram_tensor("ys", (SLOTS * P, C), F32, kind="Internal").ap()

        x_in = [sem(f"x_in{c}") for c in range(NCH)]
        w_in = sem("w_in")
        consts = sem("consts")
        ones_set = sem("ones_set")
        stats_done = sem("stats_done")
        ln_step = sem("ln_step")
        ln_step2 = sem("ln_step2")
        std_done = sem("std_done")
        xn_ready = sem("xn_ready")
        xnT_ps = sem("xnT_ps")
        xnT_ready = sem("xnT_ready")
        qkv_ps = sem("qkv_ps")
        v_ready = sem("v_ready")
        rope_step = sem("rope_step")
        qpart = sem("qpart")
        kpart = sem("kpart")
        split_step = sem("split_step")
        k_step = sem("k_step")
        stack_ready = sem("stack_ready")
        stack_ps = sem("stack_ps")
        stack_even = sem("stack_even")
        stack_odd = sem("stack_odd")
        neg_ready = sem("neg_ready")
        neg_step = sem("neg_step")
        m3_ready = sem("m3_ready")
        s_ready = sem("s_ready")
        exp_done = sem("exp_done")
        masked = sem("masked")
        pv_done = sem("pv_done")
        o_copied = sem("o_copied")
        ring_ready = sem("ring_ready")
        ring_used = sem("ring_used")
        rden_ready = sem("rden_ready")
        x2_done = sem("x2_done")
        ffn_w = sem("ffn_w")
        expert_w = sem("expert_w")
        stats2 = sem("stats2")
        var2_ready = sem("var2_ready")
        std2_done = sem("std2_done")
        ln2_step = sem("ln2_step")
        xn2_ready = sem("xn2_ready")
        route = sem("route")
        lexp_done = sem("lexp_done")
        hots_ready = sem("hots_ready")
        slots_ready = sem("slots_ready")
        dest_ready = sem("dest_ready")
        xg_in = [sem(f"xg_in{q}") for q in range(RING)]
        xt_ready = sem("xt_ready")
        xt_taken = sem("xt_taken")
        gu_ready = sem("gu_ready")
        silu_done = sem("silu_done")
        h_ready = sem("h_ready")
        th_ready = sem("th_ready")
        ht_taken = sem("ht_taken")
        dn_ready = sem("dn_ready")
        y_taken = sem("y_taken")
        tok_ready = sem("tok_ready")
        onehots = sem("onehots")
        xd_out = sem("xd_out")
        places_step = sem("places_step")
        y_out = [sem(f"y_out{q}") for q in range(RING)]
        yg_in = [sem(f"yg_in{q}") for q in range(YG)]
        mixed = sem("mixed")
        out_done = sem("out_done")

        block = ctx.enter_context(nc.Block())
        x_v = x.rearrange("(i p) c -> p i c", p=P)
        out_v = out.rearrange("(i p) c -> p i c", p=P)
        xd_v = xd.rearrange("(i p) c -> p i c", p=P)
        RANKS = 2 * CT + 3
        R = RANKS * NCH
        LOG_P = int(math.log2(P))
        GB, UB, TB, DB, XB = SCB, SCB + 2, 7, 0, 1
        NFILL = (HQ + HK) // 2

        @block.sync
        def _(sp):
            for c in range(NCH):
                sp.dma_start(x_sb[:, CT * c:CT * c + CT, :], x_v[:, CT * c:CT * c + CT, :]).then_inc(x_in[c], 16)
                if c == 0:
                    sp.dma_start(wqkv_sb[:, :, :], wqkv).then_inc(w_in, 16)
                    sp.dma_start(rope_sb[:, :, :, :], rope).then_inc(w_in, 16)
            sp.dma_start(wp_sb[:, :, :], wp).then_inc(w_in, 16)
            sp.dma_start(wgate_sb[:, :, :], wgate).then_inc(ffn_w, 16)
            sp.dma_start(wsgu_sb[:, :, :], wsgu).then_inc(ffn_w, 16)
            sp.dma_start(wsdn_sb[0:IH, :, :], wsdn).then_inc(ffn_w, 16)
            sp.wait_ge(s_ready, 2 * len(STEPS))
            sp.dma_start(wgu_sb, wgu).then_inc(expert_w, 16)
            sp.dma_start(wdn_sb, wdn).then_inc(expert_w, 16)

            def slot_out(t, q, turn, live):
                sp.wait_ge(y_taken, EARLY + t + 1)
                sp.dma_start(ys[bass.ds(t * P, P), :], yb[:, q, :]).then_inc(y_out[q], 16)

            ring_loop(sp.Fori, slot_out)
            for i in range(0, NT, 2):
                sp.wait_ge(mixed, TOPK * (i + 2))
                j = TILES[i]
                sp.dma_start(out_v[:, j:j + 2, :], x_sb[:, j:j + 2, :]).then_inc(out_done, 16)
            sp.wait_ge(out_done, 16 * NT // 2)

        @block.gpsimd
        def _(pool):
            pool.memset(identf[:, :], 0.0).then_inc(consts, 1)
            pool.memset(identb[:, :], 0.0).then_inc(consts, 1)
            pool.memset(maskq[:, :], 0.0).then_inc(consts, 1)
            pool.memset(V[:, :, :, D:VC], 0.0).then_inc(consts, 1)
            pool.wait_ge(consts, 4)
            pool.affine_select(out=identf[:, :], in_=identf[:, :], compare_op=ALU.not_equal, fill=1.0, base=0,
                               pattern=[[-1, P]], channel_multiplier=1).then_inc(consts, 1)
            pool.affine_select(out=identb[:, :], in_=identb[:, :], compare_op=ALU.not_equal, fill=1.0, base=0,
                               pattern=[[-1, P]], channel_multiplier=1).then_inc(consts, 1)
            pool.affine_select(out=maskq[:, CW - P:CW], in_=maskq[:, CW - P:CW], compare_op=ALU.is_ge, fill=NEG,
                               base=0, pattern=[[-1, P]], channel_multiplier=1).then_inc(consts, 1)
            pool.memset(V[:, :, :, D:D + 1], 1.0).then_inc(consts, 1)
            pool.iota(iota_e[:, :], pattern=[[1, E]], base=0, channel_multiplier=0,
                      allow_small_or_imprecise_dtypes=True).then_inc(consts, 1)
            pool.iota(iota_s[:, :], pattern=[[1, SLOTS]], base=0, channel_multiplier=0,
                      allow_small_or_imprecise_dtypes=True).then_inc(consts, 1)
            pool.memset(onesb[:, :], 1.0).then_inc(consts, 1)
            pool.iota(iota_p[:, :], pattern=[[1, P]], base=0, channel_multiplier=0,
                      allow_small_or_imprecise_dtypes=True).then_inc(consts, 1)
            pool.iota(own_p[:, :], pattern=[[0, 1]], base=0, channel_multiplier=1,
                      allow_small_or_imprecise_dtypes=True).then_inc(consts, 1)
            pool.iota(tile_p[:, :], pattern=[[P, NT]], base=0, channel_multiplier=0,
                      allow_small_or_imprecise_dtypes=True).then_inc(consts, 1)
            pool.wait_ge(consts, 14)
            pool.affine_select(out=before[:, :], in_=onesb[:, :], compare_op=ALU.is_gt, fill=0.0, base=0,
                               pattern=[[1, P]], channel_multiplier=-1).then_inc(consts, 1)
            pool.memset(hots[:, NT, :], 0.0).then_inc(consts, 1)
            pool.memset(csum[:, :, :], 0.0).then_inc(consts, 1)

            for e in ORDER:
                if e[0] == "split":
                    u, b = e[1], e[1] % DEEP
                    pool.wait_ge(neg_ready, u + 1)
                    if u >= DEEP:
                        pool.wait_ge(ring_ready, 1 + USE["shift", u - DEEP, 1])
                    pool.tensor_copy(M3[:, b, :, :, 0], neg[:, b]).then_inc(neg_step, 1)
                    pool.wait_ge(neg_step, 4 * u + 1)
                    pool.tensor_tensor(nd1[:, b], neg[:, b], M3[:, b, :, :, 0], ALU.subtract).then_inc(neg_step, 1)
                    pool.wait_ge(neg_step, 4 * u + 2)
                    pool.tensor_copy(M3[:, b, :, :, 1], nd1[:, b]).then_inc(neg_step, 1)
                    pool.wait_ge(neg_step, 4 * u + 3)
                    pool.tensor_tensor(nd2[:, b], nd1[:, b], M3[:, b, :, :, 1], ALU.subtract).then_inc(neg_step, 1)
                    pool.wait_ge(neg_step, 4 * u + 4)
                    pool.tensor_copy(M3[:, b, :, :, 2], nd2[:, b]).then_inc(m3_ready, 1)
                elif e[0] == "values" and e[2] == 0 and e[1] in DIAG:
                    m = e[1]
                    u, j = STEPS[m]
                    lo = P * (j - CT * UNITS[u][0])
                    pool.wait_ge(exp_done, 2 * m + 2)
                    pr = probs[:, m % PSLOT, :, lo:lo + P]
                    pool.affine_select(out=pr, in_=pr, compare_op=ALU.is_ge, fill=0.0, base=0,
                                       pattern=[[0, GH], [1, P]], channel_multiplier=-1).then_inc(masked, 1)

            pool.wait_ge(xd_out, 16 * NCH)
            pool.wait_ge(tok_ready, 1)

            for t in range(SLOTS):
                if t >= RING:
                    pool.wait_ge(xt_ready, t - RING + 1)
                pool.indirect_dma_start(xg[:, t % RING, :], None, xd,
                                        bass.IndirectOffsetOnAxis(ap=tok_i[:, t:t + 1], axis=0)
                                        ).then_inc(xg_in[t % RING], 16)
            for q in range(RING):
                pool.wait_ge(y_out[q], 16 * SLOTS // RING)
            for n in range(TOPK * NT):
                i, k = TILES[n // TOPK], n % TOPK
                if n >= YG:
                    pool.wait_ge(mixed, n - YG + 1)
                pool.indirect_dma_start(yg[:, n % YG, :], None, ys,
                                        bass.IndirectOffsetOnAxis(ap=dest_i[:, k, i:i + 1], axis=0)
                                        ).then_inc(yg_in[n % YG], 16)

        @block.scalar
        def _(act):
            def root(c):
                act.wait_ge(ln_step, c + 1)
                act.activation(std[:, CT * c:CT * c + CT], var[:, CT * c:CT * c + CT], ACT.Sqrt).then_inc(std_done, 1)

            def take_xnT(c):
                for h in range(2):
                    act.wait_ge(xnT_ps, 2 * c + h + 1)
                    if c and h == 0:
                        act.wait_ge(qkv_ps, CT * c)
                    act.activation(xnT[:, 2 * h:2 * h + 2, :, :],
                                   ps[:, h, :].rearrange("p (i k t) -> p i k t", i=2, k=KC), ACT.Copy).then_inc(xnT_ready, 1)

            def values(c):
                act.wait_ge(rope_step, 5 * c + 5)
                if c == 0:
                    act.wait_ge(consts, 8)
                act.activation(V[:, CT * c:CT * c + CT, :, 0:D],
                               ps[:, 2:6, (HQ + HK) * D:QKV].rearrange("p i (g d) -> p i g d", g=HK),
                               ACT.Copy).then_inc(v_ready, 1)

            def first_parts(c):
                act.wait_ge(rope_step, 5 * c + 5)
                if c >= 2:
                    act.wait_ge(stack_ps, NFILL * (c - 1))
                src = qk[c % 2]
                for i in range(CT):
                    act.activation(part_of(Qn, c, i, slice(0, 3)), src[:, i, 0:HQ, :].unsqueeze(2).to_broadcast([P, HQ, 3, D]),
                                   ACT.Copy).then_inc(qpart, 1)
                    act.activation(part_of(Kn, c, i, slice(0, 6, 3)), src[:, i, HQ:, :].unsqueeze(2).to_broadcast([P, HK, 2, D]),
                                   ACT.Copy).then_inc(kpart, 1)
                    act.activation(part_of(Kn, c, i, slice(5, 6)), src[:, i, HQ:, :].unsqueeze(2), ACT.Copy).then_inc(kpart, 1)

            def second_parts(c):
                act.wait_ge(split_step, 2 * CT * c + CT)
                for i in range(CT):
                    act.activation(part_of(Qn, c, i, slice(3, 5)), res[:, i, 0:HQ, :].unsqueeze(2).to_broadcast([P, HQ, 2, D]),
                                   ACT.Copy).then_inc(qpart, 1)
                    act.activation(part_of(Kn, c, i, slice(1, 6, 3))[:, :, 0:2], res[:, i, HQ:, :].unsqueeze(2).to_broadcast([P, HK, 2, D]),
                                   ACT.Copy).then_inc(kpart, 1)

            def take_stack(c):
                for f in range(1, NFILL, 2):
                    act.wait_ge(stack_ps, NFILL * c + f + 1)
                    dst = Qs[0:KROW, 2 * f:2 * f + 2] if f < HQ // 2 else Ks[0:KROW, 2 * f - HQ:2 * f - HQ + 2]
                    act.activation(dst[:, :, CW * c:CW * c + CW],
                                   ps[0:KROW, 7, :].bitcast(BF16).rearrange("p (h t) -> p h t", h=2),
                                   ACT.Copy).then_inc(stack_odd, 1)

            root(0)
            take_xnT(0)
            for c in range(1, NCH):
                root(c)
            values(0)
            first_parts(0)
            for c in range(NCH):
                if c + 1 < NCH:
                    take_xnT(c + 1)
                second_parts(c)
                if c + 1 < NCH:
                    values(c + 1)
                    first_parts(c + 1)
                take_stack(c)
            for e in ORDER:
                if e[0] == "take":
                    u = e[1]
                    act.wait_ge(pv_done, STEPS_TO[u])
                    if u:
                        act.wait_ge(ring_ready, 1 + USE["turn", u - 1])
                    act.activation(OT[:, :], ps[:, OB, :], ACT.Copy).then_inc(o_copied, 1)
                elif e[0] == "root":
                    n, c = e[1], CHUNKS[e[1]]
                    act.wait_ge(var2_ready, n + 1)
                    act.activation(std[:, CT * c:CT * c + CT], var[:, CT * c:CT * c + CT], ACT.Sqrt).then_inc(std2_done, 1)
                elif e[0] == "apply":
                    n, c = e[1], CHUNKS[e[1]]
                    act.wait_ge(ln2_step, 6 * n + 6)
                    for i in range(CT * c, CT * c + CT):
                        act.activation(xn[:, i, :], x_sb[:, i, :], ACT.Identity, bias=nmr[:, i:i + 1],
                                       scale=rstd[:, i:i + 1]).then_inc(xn2_ready, 1)
                elif e[0] == "logits":
                    n, c = e[1], CHUNKS[e[1]]
                    act.wait_ge(xn2_ready, CT * (n + 1))
                    act.dma_start(xd_v[:, CT * c:CT * c + CT, :], xn[:, CT * c:CT * c + CT, :]).then_inc(xd_out, 16)
                if e[0] != "score":
                    continue
                _, m, h = e
                u, j = STEPS[m]
                lo = max(0, P * (j - CT * UNITS[u][0]))
                act.wait_ge(s_ready, 2 * m + h + 1)
                if m >= PSLOT and h == 0:
                    act.wait_ge(pv_done, m - PSLOT + 1)
                act.activation(probs[:, m % PSLOT, 2 * h:2 * h + 2, lo:CW],
                               ps[:, SCB + 2 * h:SCB + 2 * h + 2, lo:CW], ACT.Exp, scale=SCALE).then_inc(exp_done, 1)

            def silu(n, b, w):
                act.wait_ge(gu_ready, n + 1)
                if not isinstance(n, int) or n >= 2:
                    act.wait_ge(h_ready, n - 1)
                act.activation(gate_act[:, b, 0:w], ps[:, GB + b, 0:w], ACT.Silu).then_inc(silu_done, 1)

            def take_hidden(n, b, w):
                act.wait_ge(th_ready, n + 1)
                if not isinstance(n, int) or n >= 2:
                    act.wait_ge(dn_ready, n - 1)
                act.activation(hT[0:IH, b, 0:w], ps[0:IH, TB, 0:w], ACT.Copy).then_inc(ht_taken, 1)

            silu(0, 0, SI)
            silu(1, 1, SI)
            for n in range(EARLY):
                take_hidden(n, n % 2, SH * P)
                silu(n + 2, n % 2, SI if n + 2 < EARLY else I)
                if n == 4:
                    act.wait_ge(route, RANKS * NCH)
                    act.activation(lexp[:, :, :], lsub[:, :, :], ACT.Exp).then_inc(lexp_done, 1)

            def routed(t, q, turn, live):
                take_hidden(EARLY + t, q % 2, 2 * P)
                silu(EARLY + t + 2, q % 2, I if live(2) else SI)

            ring_loop(act.Fori, routed)
            for n in range(LATE0, LATE0 + NT - EARLY):
                take_hidden(n, n % 2, SH * P)
                if n + 2 < LATE0 + NT - EARLY:
                    silu(n + 2, n % 2, SI)

        @block.vector
        def _(dve):
            def normalise(c, xsrc):
                t0, t1 = CT * c, CT * c + CT
                s = 7 * c
                dve.wait_ge(x_in[c], 16)
                for i in range(t0, t1):
                    dve.bn_stats(stats[:, i, :], xsrc[:, i, :]).then_inc(stats_done, 1)
                for i in range(t0, t1):
                    dve.wait_ge(stats_done, NT * 0 + 2 * t0 + (i - t0) + 1)
                    dve.bn_aggr(mv[:, i, :], stats[:, i, :]).then_inc(stats_done, 1)
                dve.wait_ge(stats_done, 2 * t1)
                dve.tensor_scalar(var[:, t0:t1], mv[:, t0:t1, 1], EPS, None, ALU.add).then_inc(ln_step, 1)

            def newton(t, root_done, count, step, s):
                dve.wait_ge(root_done, count)
                dve.reciprocal(rstd0[:, t], std[:, t]).then_inc(step, 1)
                dve.wait_ge(step, s + 1)
                dve.tensor_tensor(newt[:, t], rstd0[:, t], rstd0[:, t], ALU.mult).then_inc(step, 1)
                dve.wait_ge(step, s + 2)
                dve.tensor_tensor(newt2[:, t], newt[:, t], var[:, t], ALU.mult).then_inc(step, 1)
                dve.wait_ge(step, s + 3)
                dve.tensor_scalar(newt3[:, t], newt2[:, t], -0.5, 1.5, ALU.mult, ALU.add).then_inc(step, 1)
                dve.wait_ge(step, s + 4)
                dve.tensor_tensor(rstd[:, t], newt3[:, t], rstd0[:, t], ALU.mult).then_inc(step, 1)

            def finish_normalise(c, xsrc):
                t0, t1 = CT * c, CT * c + CT
                newton(slice(t0, t1), std_done, c + 1, ln_step2, 5 * c)
                dve.wait_ge(ln_step2, 5 * c + 5)
                for i in range(t0, t1):
                    dve.tensor_scalar(xn[:, i, :], xsrc[:, i, :], mv[:, i, 0:1], rstd[:, i:i + 1],
                                      ALU.subtract, ALU.mult).then_inc(xn_ready, 1)

            def rotate(c):
                s = 5 * c
                dst = qk[c % 2]
                dve.wait_ge(qkv_ps, CT * c + CT)
                if c:
                    dve.wait_ge(rope_step, s)
                if c == 0:
                    dve.wait_ge(w_in, 48)
                if c >= 2:
                    dve.wait_ge(qpart, 2 * CT * (c - 2) + CT)
                    dve.wait_ge(kpart, 3 * CT * (c - 2) + 2 * CT)
                src = ps[:, 2:6, 0:(HQ + HK) * D].rearrange("p i (h d) -> p i h d", d=D)
                shape = [P, CT, HQ + HK, HALF]
                cos = rope_sb[:, CT * c:CT * c + CT, 0, :].unsqueeze(2).to_broadcast(shape)
                sin = rope_sb[:, CT * c:CT * c + CT, 1, :].unsqueeze(2).to_broadcast(shape)
                nsin = rope_sb[:, CT * c:CT * c + CT, 2, :].unsqueeze(2).to_broadcast(shape)
                a, b = slice(0, HALF), slice(HALF, D)
                dve.tensor_tensor(rc[:, :, :, a], src[:, :, :, a], cos, ALU.mult).then_inc(rope_step, 1)
                dve.tensor_tensor(rc[:, :, :, b], src[:, :, :, b], cos, ALU.mult).then_inc(rope_step, 1)
                dve.tensor_tensor(dst[:, :, :, a], src[:, :, :, b], nsin, ALU.mult).then_inc(rope_step, 1)
                dve.tensor_tensor(dst[:, :, :, b], src[:, :, :, a], sin, ALU.mult).then_inc(rope_step, 1)
                dve.wait_ge(rope_step, s + 4)
                dve.tensor_tensor(dst, rc, dst, ALU.add).then_inc(rope_step, 1)

            def split_first(c):
                dve.wait_ge(rope_step, 5 * c + 5)
                for i in range(CT):
                    dve.wait_ge(qpart, 2 * CT * c + i + 1)
                    dve.wait_ge(kpart, 3 * CT * c + 2 * i + 2)
                    if c:
                        dve.wait_ge(split_step, 2 * CT * c)
                    dve.tensor_tensor(res[:, i, 0:HQ, :].unsqueeze(2), qk[c % 2][:, i, 0:HQ, :].unsqueeze(2),
                                      part_of(Qn, c, i, slice(0, 1)), ALU.subtract).then_inc(k_step, 1)
                    dve.tensor_tensor(res[:, i, HQ:, :].unsqueeze(2), qk[c % 2][:, i, HQ:, :].unsqueeze(2),
                                      part_of(Kn, c, i, slice(0, 1)), ALU.subtract).then_inc(split_step, 1)

            def split_second(c):
                for i in range(CT):
                    dve.wait_ge(qpart, 2 * CT * c + CT + i + 1)
                    dve.wait_ge(kpart, 3 * CT * c + 2 * CT + i + 1)
                    dve.tensor_tensor(part_of(Qn, c, i, slice(5, 6)), res[:, i, 0:HQ, :].unsqueeze(2),
                                      part_of(Qn, c, i, slice(3, 4)), ALU.subtract).then_inc(k_step, 1)
                    dve.tensor_tensor(part_of(Kn, c, i, slice(2, 3)), res[:, i, HQ:, :].unsqueeze(2),
                                      part_of(Kn, c, i, slice(1, 2)), ALU.subtract).then_inc(split_step, 1)

            def take_stack(c):
                for f in range(0, NFILL, 2):
                    dve.wait_ge(stack_ps, NFILL * c + f + 1)
                    dst = Qs[0:KROW, 2 * f:2 * f + 2] if f < HQ // 2 else Ks[0:KROW, 2 * f - HQ:2 * f - HQ + 2]
                    dve.tensor_copy(dst[:, :, CW * c:CW * c + CW],
                                    ps[0:KROW, 6, :].bitcast(BF16).rearrange("p (h t) -> p h t", h=2)).then_inc(stack_even, 1)

            normalise(0, x_sb)
            finish_normalise(0, x_sb)
            for c in range(1, NCH):
                normalise(c, x_sb)
            dve.memset(Ks[KROW:P, :, 0:T - CW], 1.0).then_inc(ones_set, 1)
            finish_normalise(1, x_sb)
            rotate(0)
            split_first(0)
            for c in range(NCH):
                if c + 1 < NCH:
                    if c + 2 < NCH:
                        finish_normalise(c + 2, x_sb)
                    rotate(c + 1)
                split_second(c)
                if c + 1 < NCH:
                    split_first(c + 1)
                take_stack(c)
            dve.wait_ge(stack_odd, NCH * NFILL // 2)
            dve.memset(Ks[KROW:P, :, T - CW:T], 1.0).then_inc(ones_set, 1)
            for e in ORDER:
                if e in USE:
                    dve.wait_ge(ring_ready, USE[e] + 1)
                    bank = ps[:, BANK[e], :]
                if e[0] == "max":
                    n = e[1]
                    u, hh, r, k = PIECES[n]
                    c = UNITS[u][0]
                    w = CW if k < c else P * (r + 1)
                    src = bank[:, 0:w]
                    if k < c:
                        dve.tensor_reduce(part[:, u % DEEP, hh, r, k:k + 1], src, AX.X, ALU.max).then_inc(ring_used, 1)
                    else:
                        if n >= 2:
                            dve.wait_ge(ring_used, USE["max", n - 2] + 1)
                        dve.tensor_tensor_reduce(junk[:, n % 2, 0:w], src, maskq[:, CW - w:CW], 1.0, 3 * NEG, ALU.add,
                                                 ALU.max, part[:, u % DEEP, hh, r, k:k + 1]).then_inc(ring_used, 1)
                elif e[0] == "split":
                    u = e[1]
                    c = UNITS[u][0]
                    dve.wait_ge(ring_used, USE["max", PIECES_TO[u] - 1] + 1)
                    if u >= DEEP:
                        dve.wait_ge(m3_ready, u - DEEP + 1)
                    dve.tensor_reduce(neg[:, u % DEEP], part[:, u % DEEP, :, :, 0:c + 1], AX.X, ALU.max,
                                      negate=True).then_inc(neg_ready, 1)
                elif e[0] == "shift":
                    _, u, h = e
                    c, g = UNITS[u]
                    h0 = GH * g + 2 * h
                    dve.tensor_copy(Qs[KROW:SROW, h0:h0 + 2, CW * c:CW * c + CW],
                                    bank[KROW:SROW, :].bitcast(BF16).rearrange("p (h t) -> p h t", h=2)
                                    ).then_inc(ring_used, 1)
                elif e[0] == "turn":
                    u = e[1]
                    c, g = UNITS[u]
                    o = bank.rearrange("p (i h d) -> p i h d", i=CT, h=GH)
                    if u:
                        dve.wait_ge(ring_used, USE["turn", u - 1] + 1)
                    dve.reciprocal(rden[:, :, :], o[:, :, :, D]).then_inc(rden_ready, 1)
                    dve.wait_ge(rden_ready, u + 1)
                    if g == 0 and u:
                        dve.wait_ge(ring_ready, 1 + USE["turn_out", u // HK - 1, 1])
                    dve.tensor_tensor(
                        attn[:, :, GH * D * g:GH * D * (g + 1)].rearrange("p i (h d) -> p i h d", h=GH), o[:, :, :, 0:D],
                        rden[:, :, :].unsqueeze(3).to_broadcast([P, CT, GH, D]), ALU.mult).then_inc(ring_used, 1)
                elif e[0] == "turn_out":
                    _, n, h = e
                    if n or h:
                        dve.wait_ge(ring_ready, 1 + USE["project", n - 1 + h, 1 - h])
                    dve.tensor_copy(aT[:, :, :, :], bank.rearrange("p (i k t) -> p i k t", i=2, k=KC)
                                    ).then_inc(ring_used, 1)
                elif e[0] == "project":
                    _, n, h = e
                    c = CHUNKS[n]
                    xt = x_sb[:, CT * c + 2 * h:CT * c + 2 * h + 2, :]
                    dve.wait_ge(xn_ready, NT)
                    dve.tensor_tensor(xt, bank.rearrange("p (i n) -> p i n", i=2), xt, ALU.add
                                      ).then_inc(x2_done, 1)
                    dve.wait_ge(x2_done, 2 * n + h + 1)
                    dve.nop().then_inc(ring_used, 1)
                elif e[0] == "stats":
                    n, c = e[1], CHUNKS[e[1]]
                    dve.wait_ge(x2_done, 2 * n + 2)
                    for i in range(CT * c, CT * c + CT):
                        dve.bn_stats(stats[:, i, :], x_sb[:, i, :]).then_inc(stats2, 1)
                    for i in range(CT):
                        dve.wait_ge(stats2, 2 * CT * n + i + 1)
                        dve.bn_aggr(mv[:, CT * c + i, :], stats[:, CT * c + i, :]).then_inc(stats2, 1)
                    dve.wait_ge(stats2, 2 * CT * (n + 1))
                    dve.tensor_scalar(var[:, CT * c:CT * c + CT], mv[:, CT * c:CT * c + CT, 1], EPS, None,
                                      ALU.add).then_inc(var2_ready, 1)
                elif e[0] == "norm":
                    n, c = e[1], CHUNKS[e[1]]
                    newton(slice(CT * c, CT * c + CT), std2_done, n + 1, ln2_step, 6 * n)
                    dve.wait_ge(ln2_step, 6 * n + 5)
                    dve.scalar_tensor_tensor(out=nmr[:, CT * c:CT * c + CT], in0=mv[:, CT * c:CT * c + CT, 0], scalar=-1.0,
                                             in1=rstd[:, CT * c:CT * c + CT], op0=ALU.mult, op1=ALU.mult
                                             ).then_inc(ln2_step, 1)
                elif e[0] == "turn_x":
                    _, n, h = e
                    i = CT * CHUNKS[n] + 2 * h
                    dve.tensor_copy(xT_all[:, i:i + 2, :, :], bank.rearrange("p (i k t) -> p i k t", i=2, k=KC)
                                    ).then_inc(ring_used, 1)
                elif e[0] == "logits":
                    c = CHUNKS[e[1]]
                    dve.wait_ge(consts, 17)
                    dve.tensor_copy(lg[:, CT * c:CT * c + CT, :], bank[:, 0:CT * E].rearrange("p (i e) -> p i e", i=CT)
                                    ).then_inc(ring_used, 1)
                elif e[0] == "rank":
                    n, c = e[1], CHUNKS[e[1]]
                    t = slice(CT * c, CT * c + CT)
                    dve.wait_ge(ring_used, USE["logits", n] + 1)
                    for i in range(CT * c, CT * c + CT):
                        dve.max(top[:, i, :], lg[:, i, :]).then_inc(route, 1)
                    dve.wait_ge(route, RANKS * n + CT)
                    dve.tensor_tensor(lsub[:, t, 0:E], lg[:, t, :], top[:, t, 0:1].to_broadcast([P, CT, E]),
                                      ALU.subtract).then_inc(route, 1)
                    dve.tensor_tensor(lsub[:, t, E:E + 1], top[:, t, 1:2], top[:, t, 0:1], ALU.subtract).then_inc(route, 1)
                    for i in range(CT * c, CT * c + CT):
                        dve.max_index(top_i[:, i, :], top[:, i, :], lg[:, i, :]).then_inc(route, 1)
                    dve.wait_ge(route, RANKS * n + 2 * CT + 2)
                    dve.tensor_copy(top_f[:, t, :], top_i[:, t, 0:TOPK]).then_inc(route, 1)

            def routes():
                dve.wait_ge(route, RANKS * NCH)
                for k in range(TOPK):
                    dve.tensor_tensor(hot[:, k], iota_e[:, :].unsqueeze(1).to_broadcast([P, NT, E]),
                                      top_f[:, :, k:k + 1].to_broadcast([P, NT, E]), ALU.is_equal).then_inc(route, 1)
                dve.wait_ge(route, R + 2)
                dve.tensor_tensor(hots[:, 0:NT, :], hot[:, 0], hot[:, 1], ALU.add).then_inc(hots_ready, 1)

            def places():
                bank = ps[:, BANK["places",], :]
                dve.wait_ge(ring_ready, USE["places",] + 1)
                dve.tensor_scalar(cnt_i[:, :], bank[:, NT * E:(NT + 1) * E], P - 1.0, None, ALU.add).then_inc(places_step, 1)
                dve.wait_ge(places_step, 1)
                dve.tensor_scalar(cnt_t[:, :], cnt_i[:, :], LOG_P, None, ALU.logical_shift_right).then_inc(places_step, 1)
                dve.wait_ge(places_step, 2)
                dve.tensor_copy(tiles[:, :], cnt_t[:, :]).then_inc(places_step, 1)
                dve.tensor_copy(csum[:, 0, 8:], cnt_t[:, :]).then_inc(places_step, 1)
                dve.wait_ge(places_step, 4)
                for n, d in enumerate((1, 2, 4, 8)):
                    a, b = csum[:, n % 2, :], csum[:, (n + 1) % 2, :]
                    dve.tensor_tensor(b[:, 8:], a[:, 8:], a[:, 8 - d:8 - d + E], ALU.add).then_inc(places_step, 1)
                    dve.wait_ge(places_step, 5 + n)
                ends = csum[:, 0, 8:]
                dve.tensor_tensor(base0[:, :], ends, tiles[:, :], ALU.subtract).then_inc(places_step, 1)
                dve.wait_ge(places_step, 9)
                dve.tensor_scalar(base[:, :], base0[:, :], float(P), None, ALU.mult).then_inc(places_step, 1)
                dve.wait_ge(places_step, 10)
                dve.tensor_tensor(where[:, :, :], bank[:, 0:NT * E].rearrange("p (i e) -> p i e", i=NT),
                                  base[:, :].unsqueeze(1).to_broadcast([P, NT, E]), ALU.add).then_inc(places_step, 1)
                dve.wait_ge(places_step, 11)
                for k in range(TOPK):
                    dve.tensor_tensor(wsel[:, k], hot[:, k], where[:, :, :], ALU.mult).then_inc(places_step, 1)
                dve.wait_ge(places_step, 13)
                dve.nop().then_inc(ring_used, 1)
                dve.tensor_reduce(dest[:, :, :], wsel[:, :, :, :], AX.X, ALU.add).then_inc(places_step, 1)
                dve.wait_ge(places_step, 14)
                dve.tensor_copy(dest_i[:, :, :], dest[:, :, :]).then_inc(dest_ready, 1)
                dve.wait_ge(dest_ready, 1)
                dve.tensor_scalar(slot_i[:, :, :], dest_i[:, :, :], LOG_P, None, ALU.logical_shift_right).then_inc(places_step, 1)
                dve.tensor_scalar(pos_i[:, :, :], dest_i[:, :, :], P - 1, None, ALU.bitwise_and).then_inc(places_step, 1)
                dve.wait_ge(places_step, 16)
                dve.tensor_copy(slot_f[:, :, :], slot_i[:, :, :]).then_inc(places_step, 1)
                dve.tensor_copy(pos_f[:, :, :], pos_i[:, :, :]).then_inc(places_step, 1)
                dve.wait_ge(places_step, 18)

            def slot_experts():
                dve.tensor_tensor(s_cmp[:, :, :], iota_s[0:1, :].unsqueeze(2).to_broadcast([1, SLOTS, E]),
                                  csum[0:1, 0, 8:].unsqueeze(1).to_broadcast([1, SLOTS, E]), ALU.is_ge).then_inc(places_step, 1)
                dve.wait_ge(places_step, 19)
                dve.tensor_reduce(s_exp[:, :], s_cmp[:, :, :], AX.X, ALU.add).then_inc(places_step, 1)
                dve.wait_ge(places_step, 20)
                dve.tensor_scalar(s_exp_i[:, :], s_exp[:, :], float(E - 1), None, ALU.min).then_inc(slots_ready, 1)

            def slot_onehots():
                dve.tensor_tensor(slot_hot[:, :, :], iota_s[:, :].unsqueeze(1).to_broadcast([P, TOPK * NT, SLOTS]),
                                  slot_f[:, :, :].rearrange("p k i -> p (k i)").unsqueeze(2).to_broadcast([P, TOPK * NT, SLOTS]),
                                  ALU.is_equal).then_inc(onehots, 1)
                dve.wait_ge(onehots, 1)
                dve.tensor_scalar(slot_val[:, :, 0:SLOTS], slot_hot[:, :, :], own_p[:, 0:1], None, ALU.mult).then_inc(onehots, 1)
                for k in range(TOPK):
                    dve.tensor_tensor(slot_val[:, k * NT:(k + 1) * NT, SLOTS:], slot_hot[:, k * NT:(k + 1) * NT, :],
                                      tile_p[:, :].unsqueeze(2).to_broadcast([P, NT, SLOTS]), ALU.mult).then_inc(onehots, 1)

            def pos_onehots():
                for n in range(TOPK * NT):
                    k, i = n // NT, n % NT
                    dve.tensor_scalar(pos_hot[:, n, :], iota_p[:, :], pos_f[:, k, i:i + 1], None,
                                      ALU.is_equal).then_inc(onehots, 1)

            def tokens():
                bank = ps[:, BANK["tokens",], :]
                dve.wait_ge(ring_ready, USE["tokens",] + 1)
                dve.tensor_copy(tok_p[:, :], bank[:, 0:SLOTS]).then_inc(places_step, 1)
                dve.wait_ge(places_step, 21)
                dve.tensor_tensor(tok_i[:, :], tok_p[:, :], bank[:, SLOTS:2 * SLOTS], ALU.add).then_inc(tok_ready, 1)
                dve.wait_ge(tok_ready, 1)
                dve.nop().then_inc(ring_used, 1)

            def weights():
                dve.wait_ge(lexp_done, 1)
                dve.tensor_reduce(lsum[:, :], lexp[:, :, 0:E], AX.X, ALU.add).then_inc(places_step, 1)
                dve.wait_ge(places_step, 22)
                dve.reciprocal(wtok[:, 0, :], lsum[:, :]).then_inc(places_step, 1)
                dve.wait_ge(places_step, 23)
                dve.tensor_tensor(wtok[:, 1, :], wtok[:, 0, :], lexp[:, :, E], ALU.mult).then_inc(places_step, 1)

            def gate(n, b, up):
                w = up.shape[1]
                dve.wait_ge(silu_done, n + 1)
                if not isinstance(n, int) or n >= 2:
                    dve.wait_ge(th_ready, n - 1)
                dve.tensor_tensor(hidden[:, b, 0:w], gate_act[:, b, 0:w], up, ALU.mult).then_inc(h_ready, 1)

            def shared_gate(n):
                gate(n, n % 2, ps[:, UB + n % 2, 0:SI])

            def routed_gate(n, b):
                gate(n, b, ps[:, GB + b, I:2 * I])

            def take_slot(s, b):
                dve.wait_ge(xt_ready, s + 1)
                if not isinstance(s, int) or s >= 2:
                    dve.wait_ge(gu_ready, EARLY + s - 1)
                dve.tensor_copy(xgT[:, b, :], ps[:, XB + b, 0:KC * P]).then_inc(xt_taken, 1)

            def add_shared(n):
                i = TILES[n] if n < EARLY else TILES[n - SLOTS]
                dve.wait_ge(dn_ready, n + 1)
                dve.tensor_tensor(x_sb[:, i, :], ps[:, DB, 0:C], x_sb[:, i, :], ALU.add).then_inc(y_taken, 1)

            shared_gate(0)
            routes()
            for n in range(EARLY):
                if n + 1 < EARLY:
                    shared_gate(n + 1)
                else:
                    routed_gate(n + 1, 0)
                if n == 1:
                    places()
                if n == 2:
                    slot_experts()
                    slot_onehots()
                if n == 3:
                    pos_onehots()
                if n == 4:
                    tokens()
                if n >= EARLY - 3:
                    take_slot(n - EARLY + 3, (n - EARLY + 3) % 2)
                add_shared(n)
                if n == EARLY - 3:
                    weights()

            def routed(t, q, turn, live):
                n = EARLY + t
                if live(1):
                    routed_gate(n + 1, (q + 1) % 2)
                else:
                    shared_gate(n + 1)
                if live(3):
                    take_slot(t + 3, (q + 3) % 2)
                dve.wait_ge(dn_ready, n + 1)
                if not isinstance(t, int) or t >= RING:
                    dve.wait_ge(y_out[q], 16 * turn)
                dve.tensor_copy(yb[:, q, :], ps[:, DB, 0:C]).then_inc(y_taken, 1)

            ring_loop(dve.Fori, routed)

            def mix(n):
                i, k = TILES[n // TOPK], n % TOPK
                dve.wait_ge(yg_in[n % YG], 16 * (n // YG + 1))
                if k:
                    dve.wait_ge(mixed, n)
                dve.scalar_tensor_tensor(out=x_sb[:, i, :], in0=yg[:, n % YG, :], scalar=wtok[:, k, i:i + 1],
                                         in1=x_sb[:, i, :], op0=ALU.mult, op1=ALU.add).then_inc(mixed, 1)

            for n in range(LATE0, LATE0 + NT - EARLY):
                if n + 1 < LATE0 + NT - EARLY:
                    shared_gate(n + 1)
                add_shared(n)
                dve.wait_ge(y_taken, n + 1)
                for k in range(2 * TOPK * (n - LATE0), 2 * TOPK * (n - LATE0 + 1)):
                    mix(k)

        @block.tensor
        def _(pe):
            def turn_x(c):
                for h in range(2):
                    pe.wait_ge(xn_ready, CT * c + 2 * h + 2)
                    if c:
                        pe.wait_ge(xnT_ready, 2 * (c - 1) + h + 1)
                    for i in range(2):
                        for k in range(KC):
                            t = pe.transpose(ps[:, h, (2 * i + k) * P:(2 * i + k + 1) * P],
                                             xn[:, CT * c + 2 * h + i, k * P:(k + 1) * P], identf[:, :])
                    t.then_inc(xnT_ps, 1)

            def project_qkv(c):
                if c == 0:
                    pe.wait_ge(w_in, 48)
                else:
                    pe.wait_ge(v_ready, c)
                    pe.wait_ge(rope_step, 5 * c)
                for i in range(CT):
                    pe.wait_ge(xnT_ready, 2 * c + i // 2 + 1)
                    for k in range(KC):
                        m = pe.matmul(ps[:, 2 + i, 0:QKV], xnT[:, i, k, :], wqkv_sb[:, k, :],
                                      start=(k == 0), stop=(k == KC - 1))
                    m.then_inc(qkv_ps, 1)

            def turn_stack(c):
                pe.wait_ge(split_step, 2 * CT * (c + 1))
                pe.wait_ge(k_step, 2 * CT * (c + 1))
                pe.wait_ge(qpart, 2 * CT * (c + 1))
                pe.wait_ge(kpart, 3 * CT * (c + 1))
                for f in range(NFILL):
                    n = NFILL * c + f
                    if n >= 2:
                        pe.wait_ge((stack_even, stack_odd)[f % 2], n // 2)
                    bank = ps[0:KROW, 6 + f % 2, :].bitcast(BF16)
                    for h in range(2):
                        for i in range(CT):
                            hh = 2 * f + h
                            src = Qn[c % 2][:, hh, :] if hh < HQ else Kn[c % 2][:, hh - HQ, :]
                            t = pe.transpose(bank[:, (CT * h + i) * P:(CT * h + i + 1) * P],
                                             src[:, i * KROW:(i + 1) * KROW], identb[:, :])
                    t.then_inc(stack_ps, 1)

            pe.wait_ge(consts, 8)
            turn_x(0)
            project_qkv(0)
            for c in range(NCH):
                if c + 1 < NCH:
                    turn_x(c + 1)
                    project_qkv(c + 1)
                turn_stack(c)
            pe.wait_ge(ones_set, 2)
            pe.wait_ge(stack_even, NCH * NFILL // 2)
            pe.wait_ge(stack_odd, NCH * NFILL // 2)
            def shared_up(n):
                i = TILES[n] if n < EARLY else TILES[n - SLOTS]
                if n >= 2:
                    pe.wait_ge(h_ready, n - 1)
                else:
                    pe.wait_ge(exp_done, 2 * len(STEPS))
                for half in range(2):
                    for k in range(KC):
                        m = pe.matmul(ps[:, (GB, UB)[half] + n % 2, 0:SI], xT_all[:, i, k, :],
                                      wsgu_sb[:, k, half * SI:(half + 1) * SI], start=(k == 0), stop=(k == KC - 1))
                m.then_inc(gu_ready, 1)

            def free_bank(e):
                if BEFORE[e]:
                    pe.wait_ge(ring_used, BEFORE[e])
                return ps[:, BANK[e], :]

            for e in ORDER:
                if e in USE:
                    bank = free_bank(e)
                if e[0] == "max":
                    n = e[1]
                    u, hh, r, k = PIECES[n]
                    c, g = UNITS[u]
                    w = CW if k < c else P * (r + 1)
                    t = (CT * c + r) * P
                    pe.matmul(bank[:, 0:w], Qs[0:KROW, GH * g + hh, t:t + P],
                              Ks[0:KROW, g, CW * k:CW * k + w], start=True, stop=True).then_inc(ring_ready, 1)
                elif e[0] == "shift":
                    _, u, h = e
                    pe.wait_ge(m3_ready, u + 1)
                    rows = bank[KROW:SROW, :].bitcast(BF16)
                    for q in range(2):
                        for r in range(CT):
                            t = pe.transpose(rows[:, (CT * q + r) * P:(CT * q + r + 1) * P],
                                             M3[:, u % DEEP, 2 * h + q, r, 0:MROW], identb[:, :])
                    t.then_inc(ring_ready, 1)
                elif e[0] == "score":
                    _, m, h = e
                    u, j = STEPS[m]
                    c, g = UNITS[u]
                    lo = max(0, P * (j - CT * c))
                    if j == 0 and h == 0:
                        pe.wait_ge(ring_used, USE["shift", u, 1] + 1)
                    if m:
                        pe.wait_ge(exp_done, 2 * (m - 1) + h + 1)
                    for q in range(2):
                        s = pe.matmul(ps[:, SCB + 2 * h + q, lo:CW], Ks[0:SROW, g, P * j:P * j + P],
                                      Qs[0:SROW, GH * g + 2 * h + q, CW * c + lo:CW * (c + 1)], start=True, stop=True)
                    s.then_inc(s_ready, 1)
                elif e[0] == "values":
                    _, m, h = e
                    u, j = STEPS[m]
                    c, g = UNITS[u]
                    lo, hi = max(h * CW // 2, P * (j - CT * c)), (h + 1) * CW // 2
                    if m in DIAG:
                        pe.wait_ge(masked, DIAG.index(m) + 1)
                    else:
                        pe.wait_ge(exp_done, 2 * m + 2)
                    if j == 0 and u:
                        pe.wait_ge(o_copied, u)
                    for hh in range(GH):
                        if lo < hi:
                            o = pe.matmul(ps[VC * hh:VC * hh + VC, OB, lo:hi], V[:, j, g, :], probs[:, m % PSLOT, hh, lo:hi],
                                          start=(j == 0 and h == 0), stop=(j == key_blocks(c) - 1),
                                          skip_group_check=True)
                    if h == 1:
                        o.then_inc(pv_done, 1)
                elif e[0] == "turn":
                    u = e[1]
                    pe.wait_ge(o_copied, u + 1)
                    for i in range(CT):
                        t = pe.transpose(bank[:, i * P:(i + 1) * P], OT[:, i * P:(i + 1) * P], identf[:, :])
                    t.then_inc(ring_ready, 1)
                elif e[0] == "turn_out":
                    _, n, h = e
                    pe.wait_ge(ring_used, 1 + USE["turn", HK * n + HK - 1])
                    for i in range(2):
                        for k in range(KC):
                            t = pe.transpose(bank[:, (2 * i + k) * P:(2 * i + k + 1) * P],
                                             attn[:, 2 * h + i, k * P:(k + 1) * P], identf[:, :])
                    t.then_inc(ring_ready, 1)
                elif e[0] == "project":
                    pe.wait_ge(ring_used, 1 + USE["turn_out", e[1], e[2]])
                    for i in range(2):
                        for k in range(KC):
                            t = pe.matmul(bank[:, i * C:(i + 1) * C], aT[:, i, k, :], wp_sb[:, k, :],
                                          start=(i == 0 and k == 0), stop=(k == KC - 1), skip_group_check=True)
                    t.then_inc(ring_ready, 1)
                elif e[0] == "turn_x":
                    _, n, h = e
                    pe.wait_ge(xn2_ready, CT * n + 2 * h + 2)
                    for i in range(2):
                        for k in range(KC):
                            t = pe.transpose(bank[:, (2 * i + k) * P:(2 * i + k + 1) * P],
                                             xn[:, CT * CHUNKS[n] + 2 * h + i, k * P:(k + 1) * P], identf[:, :])
                    t.then_inc(ring_ready, 1)
                elif e[0] == "logits":
                    pe.wait_ge(ring_used, 1 + USE["turn_x", e[1], 1])
                    pe.wait_ge(ffn_w, 48)
                    for i in range(CT):
                        for k in range(KC):
                            t = pe.matmul(bank[:, i * E:(i + 1) * E], xT_all[:, CT * CHUNKS[e[1]] + i, k, :], wgate_sb[:, k, :],
                                          start=(i == 0 and k == 0), stop=(k == KC - 1), skip_group_check=True)
                    t.then_inc(ring_ready, 1)
                elif e[0] == "shared":
                    shared_up(e[1])

            def places():
                bank = free_bank(("places",))
                pe.wait_ge(hots_ready, 1)
                pe.wait_ge(consts, 17)
                pe.matmul(bank[:, 0:(NT + 1) * E], before[:, :], hots[:, :, :].rearrange("p i e -> p (i e)"),
                          start=True, stop=False)
                for i in range(NT):
                    t = pe.matmul(bank[:, (i + 1) * E:(NT + 1) * E].rearrange("p (i e) -> p i e", e=E), onesb[:, :],
                                  hots[:, i:i + 1, :].to_broadcast([P, NT - i, E]), start=False, stop=(i == NT - 1))
                t.then_inc(ring_ready, 1)

            def tokens():
                bank = free_bank(("tokens",))
                pe.wait_ge(onehots, 2 + TOPK + TOPK * NT)
                for n in range(TOPK * NT):
                    t = pe.matmul(bank[:, 0:2 * SLOTS], pos_hot[:, n, :], slot_val[:, n, :],
                                  start=(n == 0), stop=(n == TOPK * NT - 1))
                t.then_inc(ring_ready, 1)

            def turn_hidden(n, b, parts):
                pe.wait_ge(h_ready, n + 1)
                if not isinstance(n, int) or n >= 1:
                    pe.wait_ge(ht_taken, n)
                for k in range(parts):
                    t = pe.transpose(ps[0:IH, TB, k * P:(k + 1) * P], hidden[:, b, k * IH:(k + 1) * IH], identf[:, :])
                t.then_inc(th_ready, 1)

            def shared_down(n):
                pe.wait_ge(ht_taken, n + 1)
                if n:
                    pe.wait_ge(y_taken, n)
                for k in range(SH):
                    m = pe.matmul(ps[:, DB, 0:C], hT[0:IH, n % 2, k * P:(k + 1) * P], wsdn_sb[0:IH, k, :],
                                  start=(k == 0), stop=(k == SH - 1))
                m.then_inc(dn_ready, 1)

            def turn_slot(s, q, turn):
                pe.wait_ge(xg_in[q], 16 * (turn + 1))
                if not isinstance(s, int) or s >= 2:
                    pe.wait_ge(xt_taken, s - 1)
                for k in range(KC):
                    m = pe.transpose(ps[:, XB + q % 2, k * P:(k + 1) * P], xg[:, q, k * P:(k + 1) * P], identf[:, :])
                m.then_inc(xt_ready, 1)

            expert_reg = [pe.alloc_register(f"expert{q}") for q in range(RING)]

            def load_expert(s, q):
                pe.reg_load(expert_reg[q], s_exp_i[0:1, bass.ds(s, 1)])

            def routed_up(s, q, b):
                e = pe.snap(expert_reg[q], min_val=0, max_val=E - 1)
                pe.wait_ge(xt_taken, s + 1)
                pe.wait_ge(h_ready, EARLY + s - 1)
                for k in range(KC):
                    m = pe.matmul(ps[:, GB + b, 0:2 * I], xgT[:, b, k * P:(k + 1) * P],
                                  wgu_sb[:, bass.ds(e, 1), k, :], start=(k == 0), stop=(k == KC - 1))
                m.then_inc(gu_ready, 1)

            for n in range(EARLY):
                if n == 1:
                    places()
                if n == 4:
                    tokens()
                turn_hidden(n, n % 2, SH)
                if n + 2 < EARLY:
                    shared_up(n + 2)
                else:
                    if n + 2 == EARLY:
                        pe.wait_ge(expert_w, 32)
                        pe.wait_ge(slots_ready, 1)
                        load_expert(0, 0)
                    routed_up(n + 2 - EARLY, n + 2 - EARLY, n % 2)
                    load_expert(n + 3 - EARLY, n + 3 - EARLY)
                if n == EARLY - 3:
                    pe.wait_ge(ring_used, len(USES))
                if n >= EARLY - 3:
                    turn_slot(n + 3 - EARLY, n + 3 - EARLY, 0)
                shared_down(n)

            def routed(t, q, turn, live):
                n = EARLY + t
                turn_hidden(n, q % 2, 2)
                if live(2):
                    routed_up(t + 2, (q + 2) % RING, q % 2)
                    if live(3):
                        load_expert(t + 3, (q + 3) % RING)
                else:
                    shared_up(n + 2)
                if live(3):
                    turn_slot(t + 3, (q + 3) % RING, turn + (q + 3) // RING)
                e = pe.snap(expert_reg[q], min_val=0, max_val=E - 1)
                pe.wait_ge(ht_taken, n + 1)
                pe.wait_ge(y_taken, n)
                for k in range(2):
                    m = pe.matmul(ps[:, DB, 0:C], hT[0:IH, q % 2, k * P:(k + 1) * P],
                                  wdn_sb[:, bass.ds(e, 1), k, :], start=(k == 0), stop=(k == 1))
                m.then_inc(dn_ready, 1)

            ring_loop(pe.Fori, routed)
            for n in range(LATE0, LATE0 + NT - EARLY):
                turn_hidden(n, n % 2, SH)
                if n + 2 < LATE0 + NT - EARLY:
                    shared_up(n + 2)
                shared_down(n)


def rope_table():
    import numpy as np
    inv = (1.0 / np.float32(10000.0) ** (np.arange(HALF, dtype=np.float32) / np.float32(HALF))).astype(np.float32)
    ang = (np.arange(T, dtype=np.float32)[:, None] * inv[None, :]).astype(np.float32).astype(np.float64)
    tab = np.stack([np.cos(ang), np.sin(ang), -np.sin(ang)], 1).astype(np.float32)
    return np.ascontiguousarray(tab.reshape(NT, P, 3, HALF).transpose(1, 0, 2, 3))


def layout(inputs):
    import numpy as np
    a = {k: np.asarray(v) for k, v in inputs.items()}
    rows = lambda w: np.ascontiguousarray(w.T.reshape(KC, P, -1).transpose(1, 0, 2))
    wqkv = np.concatenate([a["L0_attn_Wq"], a["L0_attn_Wk"], a["L0_attn_Wv"]], 0)
    return {"x": np.ascontiguousarray(a["L0_attn_x"].reshape(T, C)), "wqkv": rows(wqkv), "wp": rows(a["L0_attn_Wp"]),
            "rope": rope_table(), "wgate": rows(a["L0_ffn_gate_w"]),
            "wgu": np.ascontiguousarray(a["L0_ffn_w_gate_up"].reshape(E, KC, P, 2 * I).transpose(2, 0, 1, 3)),
            "wdn": np.ascontiguousarray(a["L0_ffn_w_down"].reshape(E, 2, IH, C).transpose(2, 0, 1, 3)),
            "wsgu": rows(a["L0_ffn_shared_gate_up"].T),
            "wsdn": np.ascontiguousarray(a["L0_ffn_shared_down"].reshape(SH, IH, C).transpose(1, 0, 2))}


def kernel(**inputs):
    import concourse.bacc as bacc
    from concourse.bass_utils import run_bass_kernel_spmd
    arrays = layout(inputs)
    nc = bacc.Bacc("TRN2", target_bir_lowering=False, num_devices=1)
    args = {k: nc.dram_tensor(k, v.shape, mybir.dt.from_np(v.dtype), kind="ExternalInput").ap() for k, v in arrays.items()}
    out = nc.dram_tensor("out", (T, C), F32, kind="ExternalOutput").ap()
    program(nc, **args, out=out)
    r = run_bass_kernel_spmd(nc, [arrays], core_ids=[0])
    return r.results[0]["out"].reshape(1, T, C)
```

```python
import math
from contextlib import ExitStack

import concourse.bass as bass
from concourse import mybir

F32 = mybir.dt.float32
BF16 = mybir.dt.bfloat16
I32 = mybir.dt.int32
U32 = mybir.dt.uint32
ALU = mybir.AluOpType
ACT = mybir.ActivationFunctionType
AX = mybir.AxisListType

P = 128
T, C = 2048, 256
NT = T // P
HQ, HK, D = 16, 4, 16
GH = HQ // HK
HALF = D // 2
QKV = (HQ + 2 * HK) * D
KC = C // P
NCH, CT, CW = 4, 4, 512
NP_ = 6
KROW = NP_ * D
MROW = 3
SROW = KROW + MROW
VC = 32
NEG = -1.0e30
EPS = 1e-5
SCALE = D ** -0.5
PSLOT = 3
DEEP = 5
RBANKS = 3
NFILL = (HQ + HK) // 2
PREP = 2
E, I = 16, 176
TOPK = 2
IH = I // 2
SI = 2 * I
SH = (SI + P - 1) // P
SREST = SI - (SH - 1) * P
SLOTS = (TOPK * T + E * (P - 1)) // P
RING = 4

CHUNKS = [0, 2, 3, 1]
LAST = NCH - 1
TILES = [CT * c + i for c in CHUNKS for i in range(CT)]
EARLY = 12
LATE0 = EARLY + SLOTS
UNITS = [(c, g) for c in CHUNKS for g in range(HK)]


def key_blocks(c):
    return CT * (c + 1)


STEPS = [(u, j) for u, (c, g) in enumerate(UNITS) for j in range(key_blocks(c))]
PIECES = [(u, hh, r, k) for u, (c, g) in enumerate(UNITS) for r in range(CT) for hh in range(GH)
          for k in range(c + 1)]
STEPS_TO = [sum(1 for s in STEPS if s[0] <= u) for u in range(len(UNITS))]
PIECES_TO = [sum(1 for a in PIECES if a[0] <= u) for u in range(len(UNITS))]
DIAG = [m for m, (u, j) in enumerate(STEPS) if j >= CT * UNITS[u][0]]


def engine_order():
    AHEAD = 3.0
    TO_SHIFT, APART = 1.0, 0.7
    TO_TURN, TO_PROJECT, TO_NORM, BETWEEN = 2.0, 3.5, 7.5, 1.5
    FILL = 0.4
    EACH_FILL = 2.0
    OVERHEAD = 0.15
    order = []
    later = []
    length = [1.0 - max(0, j - CT * UNITS[u][0]) / CT for u, j in STEPS]
    start = [sum(length[:m]) for m in range(len(STEPS))]
    work = [OVERHEAD + (1.0 if k < UNITS[u][0] else (r + 1) / CT) for u, hh, r, k in PIECES]
    done_to = [0.0]
    for w in work:
        done_to.append(done_to[-1] + w)
    first = [start[STEPS_TO[u] - key_blocks(c)] for u, (c, g) in enumerate(UNITS)]
    taken = 0
    carried = 0.0

    def take_piece(now):
        nonlocal taken
        order.append(("max", taken))
        taken += 1
        u = PIECES[taken - 1][0]
        if taken == PIECES_TO[u]:
            order.append(("split", u))
            later.append((now + TO_SHIFT, ("shift", u, 0)))
            later.append((now + TO_SHIFT + APART, ("shift", u, 1)))

    def take_maxima(now, ahead, unit):
        nonlocal carried
        left = [(done_to[PIECES_TO[v]] - done_to[taken]) / max(first[v] - AHEAD - now, 1e-3)
                for v in range(unit + 1, len(UNITS)) if PIECES_TO[v] > taken]
        goal = done_to[taken] + max(left, default=0.0) * ahead + carried
        while taken < len(PIECES) and done_to[taken] + work[taken] / 2 < goal and PIECES[taken][0] < unit + DEEP:
            take_piece(now)
        carried = min(goal - done_to[taken], 1.0)

    def take(u, now):
        order.append(("take", u))
        later.append((now + TO_TURN, ("turn", u)))
        if u % HK == HK - 1:
            n = u // HK
            for k in range(4):
                later.append((now + TO_PROJECT + k, (("turn_out", "project")[k // 2], n, k % 2)))
            for k, e in enumerate((("stats", n), ("root", n), ("norm", n), ("apply", n, 0), ("apply", n, 1),
                                   ("apply", n, 2), ("apply", n, 3), ("turn_x", n, 0), ("turn_x", n, 1),
                                   ("logits", n), ("rank", n))):
                later.append((now + TO_NORM + BETWEEN * k, e))

    def take_later(upto, must=()):
        for x in sorted(x for x in later if x[0] <= upto or x[1][0:2] == must):
            later.remove(x)
            order.append(x[1])

    now = -100.0
    quota = 0.0
    for c in range(PREP, NCH):
        for f in range(NFILL):
            order.append(("stack", c, f))
            take_later(now)
            if c > PREP or f:
                quota += EACH_FILL
            while quota > 0 and taken < PIECES_TO[DEEP - 1]:
                quota -= work[taken]
                take_piece(now)
            now += FILL
    order.append(("ones",))
    while taken < PIECES_TO[0]:
        take_piece(now)
    take_later(now, ("shift", 0))
    order.append(("score", 0, 0))
    order.append(("score", 0, 1))
    for m, (u, j) in enumerate(STEPS):
        more = m + 1 < len(STEPS)
        q = length[m] / 4
        take_later(start[m], ("shift", STEPS[m + 1][0]) if more and STEPS[m + 1][1] == 0 else ())
        if more:
            order.append(("score", m + 1, 0))
        take_maxima(start[m], q, u)
        if m:
            order.append(("values", m - 1, 0))
        take_maxima(start[m] + q, q, u)
        if more:
            order.append(("score", m + 1, 1))
        take_maxima(start[m] + 2 * q, q, u)
        if m:
            order.append(("values", m - 1, 1))
        take_maxima(start[m] + 3 * q, q, u)
        if m in STEPS_TO:
            take(u - 1, start[m])
    n = LAST
    order += [("up", 0), ("values", m, 0), ("values", m, 1), ("take", u), ("up", 1), ("turn", u), ("gate", 0),
              ("hide", 0), ("turn_out", n, 0), ("turn_out", n, 1), ("up", 2), ("gate", 1), ("project", n, 0),
              ("project", n, 1), ("stats", n), ("root", n), ("down", 0), ("hide", 1), ("norm", n),
              ("apply", n, 0), ("apply", n, 1), ("apply", n, 2), ("apply", n, 3),
              ("up", 3), ("gate", 2), ("down", 1), ("turn_x", n, 0), ("turn_x", n, 1), ("hide", 2), ("up", 4),
              ("logits", n), ("gate", 3), ("down", 2), ("hide", 3), ("rank", n), ("up", 5), ("routes",), ("gate", 4),
              ("down", 3), ("hide", 4), ("up", 6), ("gate", 5), ("places",), ("gate", 6), ("down", 4), ("hide", 5),
              ("up", 7), ("gate", 7), ("slot_onehots",), ("hide", 6), ("up", 8), ("down", 5),
              ("gate", 8), ("pos_onehots", 0), ("hide", 7), ("up", 9), ("down", 6),
              ("gate", 9), ("pos_onehots", 1), ("hide", 8), ("up", 10), ("down", 7),
              ("tokens",), ("gate", 10), ("hide", 9), ("up", 11), ("down", 8), ("gate", 11), ("experts",),
              ("hide", 10), ("down", 9), ("down", 10)]
    return order


ORDER = engine_order()
USES = [e for e in ORDER if e[0] in ("max", "shift", "turn", "turn_out", "project", "turn_x", "logits", "places",
                                     "tokens")]
RING_END = USES.index(("turn", len(UNITS) - 1))
BANK = {e: n % RBANKS if n < RING_END else 1 + n % 2 for n, e in enumerate(USES)}
USE = {e: n for n, e in enumerate(USES)}
BEFORE = {e: max([0] + [i + 1 for i in range(n) if BANK[USES[i]] == BANK[e]]) for e, n in USE.items()}


def ring_loop(fori, step):
    def straight(t0, t1):
        for t in range(t0, t1):
            step(t, t % RING, t // RING, lambda d, t=t: t + d < SLOTS)

    loops = (SLOTS - 3) // RING - 1
    straight(0, RING)
    with fori(0, loops) as b:
        for q in range(RING):
            step(RING + q + RING * b, q, 1 + b, lambda d: True)
    straight(RING + RING * loops, SLOTS)


def program(nc, x, wqkv, wp, rope, wgate, wgu, wdn, wsgu, wsdn, out):
    with ExitStack() as ctx:
        def sb(name, shape, dt=F32):
            return ctx.enter_context(nc.sbuf_tensor(name, shape, dt))

        def sem(name):
            return ctx.enter_context(nc.semaphore(name))

        ps = ctx.enter_context(nc.psum_tensor("ps", [P, 8, 512], F32))
        SCB, OB = 3, 7

        x_sb = sb("x_sb", [P, NT, C])
        xn = sb("xn", [P, NT, C])
        wp_sb = sb("wp_sb", [P, KC, C])
        rope_sb = sb("rope_sb", [P, NT, 3, HALF])
        big = sb("big", [P, (HQ + HK) * T], BF16)
        Qs = big[:, 0:HQ * T].rearrange("p (h t) -> p h t", h=HQ)
        Ks = big[:, HQ * T:].rearrange("p (h t) -> p h t", h=HK)
        bigf = big[:, :].bitcast(F32)
        GU0, DN0 = 0, E * KC * 2 * I
        wgu_sb = bigf[:, GU0:DN0].rearrange("p (e k n) -> p e k n", e=E, k=KC)
        wdn_sb = bigf[0:IH, DN0:DN0 + E * 2 * C].rearrange("p (e k n) -> p e k n", e=E, k=2)
        early = sb("early", [P, NT * C + CT * KC * P + 512])
        at = [0]

        def piece(n):
            at[0] += n
            return early[:, at[0] - n:at[0]]

        xnT = piece(CT * KC * P).rearrange("p (i k t) -> p i k t", i=CT, k=KC)
        wqkv_sb = piece(KC * QKV).rearrange("p (k n) -> p k n", k=KC)
        PARTW = CT * NP_ * D
        Qn = [piece(HQ * PARTW // 2).bitcast(BF16).rearrange("p (h n) -> p h n", h=HQ), Qs[:, :, T - CW:T - CW + PARTW]]
        Kn = [piece(HK * PARTW // 2).bitcast(BF16).rearrange("p (h n) -> p h n", h=HK), Ks[:, :, T - CW:T - CW + PARTW]]

        def part_of(parts, c, i, slots):
            v = parts[c % 2].rearrange("p h (i s d) -> p h i s d", i=CT, s=NP_)
            return v[:, :, i, slots, :]

        xT_all = early[:, 0:NT * C].rearrange("p (i k t) -> p i k t", i=NT, k=KC)
        V = sb("V", [P, NT, HK, VC])
        stats = sb("stats", [P, NT, 6])
        mv = sb("mv", [P, NT, 2])
        var = sb("var", [P, NT])
        std = sb("std", [P, NT])
        rstd0 = sb("rstd0", [P, NT])
        newt = sb("newt", [P, NT])
        newt2 = sb("newt2", [P, NT])
        newt3 = sb("newt3", [P, NT])
        rstd = sb("rstd", [P, NT])
        nmr = sb("nmr", [P, NT])
        probs = sb("probs", [P, PSLOT, GH, CW])
        scratch = probs[:, :, :, :].rearrange("p s h t -> p (s h t)")
        RQ = CT * (HQ + HK) * D
        rc, qk0, qk1, res = (scratch[:, i * RQ:(i + 1) * RQ].rearrange("p (i h d) -> p i h d", i=CT, d=D)
                             for i in range(4))
        qk = [qk0, qk1]
        identf = sb("identf", [P, P])
        identb = sb("identb", [P, P], BF16)
        maskq = sb("maskq", [P, 2 * CW - P])
        unread = sb("unread", [P, 2, CW])
        part = sb("part", [P, DEEP, GH, CT, NCH])
        neg = sb("neg", [P, DEEP, GH, CT])
        nd1 = sb("nd1", [P, DEEP, GH, CT])
        nd2 = sb("nd2", [P, DEEP, GH, CT])
        M3 = sb("M3", [P, DEEP, GH, CT, 4], BF16)
        OT = sb("OT", [P, CW])
        rden = sb("rden", [P, CT, GH])
        attn = sb("attn", [P, CT, C])
        aT = sb("aT", [P, CT, KC, P])

        at[0] = 0

        def ffn(n, size):
            at[0] += n * size
            return scratch[:, at[0] - n * size:at[0]].rearrange("p (n m) -> p n m", n=n)

        gate_act = ffn(2, SI)
        hidden = ffn(2, SI)
        hT = ffn(2, SH * P)
        xg = ffn(RING, C)
        xgT = ffn(2, KC * P)
        yb = ffn(RING, C)
        YG = NT // 2
        yg = xn[:, :, :].rearrange("p (n k) c -> p n (k c)", k=TOPK)
        at[0] -= 2 * RING * C + 2 * KC * P
        pos_hot = ffn(TOPK * NT, P // 2).bitcast(BF16)
        slot_val = ffn(TOPK * NT, SLOTS).bitcast(BF16)
        wgate_sb = sb("wgate_sb", [P, KC, E])
        wsgu_sb = sb("wsgu_sb", [P, KC, 2 * SI])
        wsdn_sb = sb("wsdn_sb", [P, SH, C])
        unread_f = unread[:, :, :].rearrange("p a b -> p (a b)")
        slot_hot = attn[:, :, :].rearrange("p a b -> p (a b)").bitcast(BF16)[:, 0:TOPK * NT * SLOTS].rearrange(
            "p (n s) -> p n s", n=TOPK * NT)
        late = early[:, NT * C:]
        hot, wsel = (unread_f[:, i * TOPK * NT * E:(i + 1) * TOPK * NT * E]
                     .rearrange("p (k i e) -> p k i e", k=TOPK, i=NT) for i in range(2))
        where, lg = (late[:, i * NT * E:(i + 1) * NT * E].rearrange("p (i e) -> p i e", i=NT) for i in range(2))
        lsub = late[:, 2 * NT * E:2 * NT * E + NT * (E + 1)].rearrange("p (i e) -> p i e", i=NT)
        lexp = late[:, 2 * NT * E + NT * (E + 1):2 * NT * E + 2 * NT * (E + 1)].rearrange("p (i e) -> p i e", i=NT)
        iota_e = sb("iota_e", [P, E])
        iota_s = sb("iota_s", [P, SLOTS])
        iota_p = sb("iota_p", [P, P], BF16)
        own_n = sb("own_n", [P, TOPK])
        tile_n = sb("tile_n", [P, NT])
        spare = sb("spare", [P, SLOTS])
        before = sb("before", [P, P], BF16)
        onesb = sb("onesb", [P, P], BF16)
        top = sb("top", [P, NT, 8])
        top_i = sb("top_i", [P, NT, 8], U32)
        top_f = sb("top_f", [P, NT, TOPK])
        lsum = sb("lsum", [P, NT])
        wtok = sb("wtok", [P, TOPK, NT])
        hots = sb("hots", [P, NT + 1, E], BF16)
        cnt_i = sb("cnt_i", [P, E], I32)
        cnt_t = sb("cnt_t", [P, E], I32)
        tiles = sb("tiles", [P, E])
        csum = sb("csum", [P, 2, 8 + E])
        base0 = sb("base0", [P, E])
        base = sb("base", [P, E])
        dest = sb("dest", [P, TOPK, NT])
        dest_i = sb("dest_i", [P, TOPK, NT], U32)
        slot_i = sb("slot_i", [P, TOPK, NT], U32)
        pos_i = sb("pos_i", [P, TOPK, NT], U32)
        slot_f = sb("slot_f", [P, TOPK, NT])
        pos_f = sb("pos_f", [P, TOPK, NT])
        num_p = sb("num_p", [P, SLOTS])
        num = sb("num", [P, SLOTS])
        num_i = sb("num_i", [P, SLOTS], U32)
        to_spare = sb("to_spare", [P, SLOTS])
        row_i = sb("row_i", [P, SLOTS], U32)
        tok_i = sb("tok_i", [P, SLOTS], U32)
        s_cmp = V[:, :, :, :].rearrange("p i g d -> p (i g d)")[0:1, 0:SLOTS * E].rearrange("p (s e) -> p s e", e=E)
        s_exp = sb("s_exp", [1, SLOTS])
        s_exp_i = sb("s_exp_i", [1, SLOTS], I32)

        xd = nc.dram_tensor("xd", (T, C), F32, kind="Internal").ap()
        ys = nc.dram_tensor("ys", (TOPK * T + SLOTS * P, C), F32, kind="Internal").ap()

        x_in = [sem(f"x_in{c}") for c in range(NCH)]
        w_in = sem("w_in")
        wp_in = sem("wp_in")
        consts = sem("consts")
        ones_set = sem("ones_set")
        stats_done = sem("stats_done")
        ln_step = sem("ln_step")
        ln_step2 = sem("ln_step2")
        std_done = sem("std_done")
        xn_ready = sem("xn_ready")
        xnT_ps = sem("xnT_ps")
        xnT_ready = sem("xnT_ready")
        qkv_ps = sem("qkv_ps")
        v_ready = sem("v_ready")
        rope_step = sem("rope_step")
        qpart = sem("qpart")
        kpart = sem("kpart")
        split_step = sem("split_step")
        k_step = sem("k_step")
        stack_ps = sem("stack_ps")
        stack_even = sem("stack_even")
        stack_odd = sem("stack_odd")
        neg_ready = sem("neg_ready")
        neg_step = sem("neg_step")
        m3_ready = sem("m3_ready")
        s_ready = sem("s_ready")
        exp_done = sem("exp_done")
        masked = sem("masked")
        pv_done = sem("pv_done")
        o_copied = sem("o_copied")
        ring_ready = sem("ring_ready")
        ring_used = sem("ring_used")
        rden_ready = sem("rden_ready")
        x2_done = sem("x2_done")
        ffn_w = sem("ffn_w")
        expert_w = sem("expert_w")
        stats2 = sem("stats2")
        var2_ready = sem("var2_ready")
        std2_done = sem("std2_done")
        ln2_step = sem("ln2_step")
        xn2_ready = sem("xn2_ready")
        route = sem("route")
        lexp_done = sem("lexp_done")
        hots_ready = sem("hots_ready")
        slots_ready = sem("slots_ready")
        dest_ready = sem("dest_ready")
        xg_in = [sem(f"xg_in{q}") for q in range(RING)]
        xt_ready = sem("xt_ready")
        xt_taken = sem("xt_taken")
        gu_ready = sem("gu_ready")
        silu_done = sem("silu_done")
        h_ready = sem("h_ready")
        th_ready = sem("th_ready")
        ht_taken = sem("ht_taken")
        ht_full = sem("ht_full")
        dn_ready = sem("dn_ready")
        y_taken = sem("y_taken")
        tok_ready = sem("tok_ready")
        rows_ready = sem("rows_ready")
        onehots = sem("onehots")
        xd_out = sem("xd_out")
        places_step = sem("places_step")
        num_step = sem("num_step")
        y_out = [sem(f"y_out{q}") for q in range(RING)]
        yg_in = [sem(f"yg_in{q}") for q in range(YG)]
        mixed = sem("mixed")
        out_done = sem("out_done")

        block = ctx.enter_context(nc.Block())
        x_v = x.rearrange("(i p) c -> p i c", p=P)
        out_v = out.rearrange("(i p) c -> p i c", p=P)
        xd_v = xd.rearrange("(i p) c -> p i c", p=P)
        RANKS = 2 * CT + 3
        R = RANKS * NCH
        LOG_P, LOG_K = int(math.log2(P)), int(math.log2(TOPK))
        GB, UB, TB, DB, XB = SCB, SCB + 2, 7, 0, 1

        @block.sync
        def _(sp):
            for c in range(NCH):
                sp.dma_start(x_sb[:, CT * c:CT * c + CT, :], x_v[:, CT * c:CT * c + CT, :]).then_inc(x_in[c], 16)
                if c == 0:
                    sp.dma_start(wqkv_sb[:, :, :], wqkv).then_inc(w_in, 16)
                    sp.dma_start(rope_sb[:, :, :, :], rope).then_inc(w_in, 16)
            sp.dma_start(wp_sb[:, :, :], wp).then_inc(wp_in, 16)
            sp.dma_start(wgate_sb[:, :, :], wgate).then_inc(ffn_w, 16)
            sp.dma_start(wsgu_sb[:, :, :], wsgu).then_inc(ffn_w, 16)
            sp.dma_start(wsdn_sb[:, 0:SH - 1, :], wsdn[0:(SH - 1) * P, :].rearrange("(k p) n -> p k n", p=P)).then_inc(ffn_w, 16)
            sp.dma_start(wsdn_sb[0:SREST, SH - 1, :], wsdn[(SH - 1) * P:, :]).then_inc(ffn_w, 16)
            sp.wait_ge(s_ready, 2 * len(STEPS))
            sp.dma_start(wgu_sb, wgu).then_inc(expert_w, 16)
            sp.dma_start(wdn_sb, wdn).then_inc(expert_w, 16)
            for q in range(RING):
                sp.wait_ge(y_out[q], 16 * len(range(q, SLOTS, RING)))
            sp.wait_ge(xd_out, 16 * NCH)

            def load_outputs(j):
                i = TILES[j]
                sp.dma_start(yg[:, j % YG, :], ys[TOPK * P * i:TOPK * P * (i + 1), :].rearrange("(p k) c -> p (k c)", k=TOPK)
                             ).then_inc(yg_in[j % YG], 16)

            for j in range(YG):
                load_outputs(j)
            for j in range(NT):
                sp.wait_ge(mixed, TOPK * (j + 1))
                if j + YG < NT:
                    load_outputs(j + YG)
                if j % 2:
                    i = TILES[j - 1]
                    sp.dma_start(out_v[:, i:i + 2, :], x_sb[:, i:i + 2, :]).then_inc(out_done, 16)
            sp.wait_ge(out_done, 16 * NT // 2)

        @block.gpsimd
        def _(pool):
            pool.memset(identf[:, :], 0.0).then_inc(consts, 1)
            pool.memset(identb[:, :], 0.0).then_inc(consts, 1)
            pool.memset(maskq[:, :], 0.0).then_inc(consts, 1)
            pool.memset(V[:, :, :, D:VC], 0.0).then_inc(consts, 1)
            pool.wait_ge(consts, 4)
            pool.affine_select(out=identf[:, :], in_=identf[:, :], compare_op=ALU.not_equal, fill=1.0, base=0,
                               pattern=[[-1, P]], channel_multiplier=1).then_inc(consts, 1)
            pool.affine_select(out=identb[:, :], in_=identb[:, :], compare_op=ALU.not_equal, fill=1.0, base=0,
                               pattern=[[-1, P]], channel_multiplier=1).then_inc(consts, 1)
            pool.affine_select(out=maskq[:, CW - P:CW], in_=maskq[:, CW - P:CW], compare_op=ALU.is_ge, fill=NEG,
                               base=0, pattern=[[-1, P]], channel_multiplier=1).then_inc(consts, 1)
            pool.memset(V[:, :, :, D:D + 1], 1.0).then_inc(consts, 1)
            pool.iota(iota_e[:, :], pattern=[[1, E]], base=0, channel_multiplier=0,
                      allow_small_or_imprecise_dtypes=True).then_inc(consts, 1)
            pool.iota(iota_s[:, :], pattern=[[1, SLOTS]], base=0, channel_multiplier=0,
                      allow_small_or_imprecise_dtypes=True).then_inc(consts, 1)
            pool.memset(onesb[:, :], 1.0).then_inc(consts, 1)
            pool.iota(iota_p[:, :], pattern=[[1, P]], base=0, channel_multiplier=0,
                      allow_small_or_imprecise_dtypes=True).then_inc(consts, 1)
            pool.iota(own_n[:, :], pattern=[[1, TOPK]], base=1, channel_multiplier=TOPK,
                      allow_small_or_imprecise_dtypes=True).then_inc(consts, 1)
            pool.iota(tile_n[:, :], pattern=[[TOPK * P, NT]], base=0, channel_multiplier=0,
                      allow_small_or_imprecise_dtypes=True).then_inc(consts, 1)
            pool.iota(spare[:, :], pattern=[[P, SLOTS]], base=TOPK * T + 1, channel_multiplier=1,
                      allow_small_or_imprecise_dtypes=True).then_inc(consts, 1)
            pool.wait_ge(consts, 15)
            pool.affine_select(out=before[:, :], in_=onesb[:, :], compare_op=ALU.is_gt, fill=0.0, base=0,
                               pattern=[[1, P]], channel_multiplier=-1).then_inc(consts, 1)
            pool.memset(hots[:, NT, :], 0.0).then_inc(consts, 1)
            pool.memset(csum[:, :, :], 0.0).then_inc(consts, 1)

            pool.wait_ge(consts, 18)
            pool.memset(Ks[KROW:P, :, 0:T - CW], 1.0).then_inc(ones_set, 1)
            pool.wait_ge(ones_set, 1)
            splits = 0
            for e in ORDER:
                if e[0] == "ones":
                    pool.wait_ge(stack_odd, NCH * NFILL // 2)
                    pool.wait_ge(stack_even, NCH * NFILL // 2)
                    if splits:
                        pool.wait_ge(m3_ready, splits)
                    pool.memset(Ks[KROW:P, :, T - CW:T], 1.0).then_inc(ones_set, 1)
                    pool.wait_ge(ones_set, 2)
                elif e[0] == "split":
                    u, b = e[1], e[1] % DEEP
                    pool.wait_ge(neg_ready, u + 1)
                    if u >= DEEP:
                        pool.wait_ge(ring_ready, 1 + USE["shift", u - DEEP, 1])
                    pool.tensor_copy(M3[:, b, :, :, 0], neg[:, b]).then_inc(neg_step, 1)
                    pool.wait_ge(neg_step, 4 * u + 1)
                    pool.tensor_tensor(nd1[:, b], neg[:, b], M3[:, b, :, :, 0], ALU.subtract).then_inc(neg_step, 1)
                    pool.wait_ge(neg_step, 4 * u + 2)
                    pool.tensor_copy(M3[:, b, :, :, 1], nd1[:, b]).then_inc(neg_step, 1)
                    pool.wait_ge(neg_step, 4 * u + 3)
                    pool.tensor_tensor(nd2[:, b], nd1[:, b], M3[:, b, :, :, 1], ALU.subtract).then_inc(neg_step, 1)
                    pool.wait_ge(neg_step, 4 * u + 4)
                    pool.tensor_copy(M3[:, b, :, :, 2], nd2[:, b]).then_inc(m3_ready, 1)
                    splits += 1
                elif e[0] == "values" and e[2] == 0 and e[1] in DIAG:
                    m = e[1]
                    u, j = STEPS[m]
                    lo = P * (j - CT * UNITS[u][0])
                    pool.wait_ge(exp_done, 2 * m + 2)
                    pr = probs[:, m % PSLOT, :, lo:lo + P]
                    pool.affine_select(out=pr, in_=pr, compare_op=ALU.is_ge, fill=0.0, base=0,
                                       pattern=[[0, GH], [1, P]], channel_multiplier=-1).then_inc(masked, 1)

            pool.wait_ge(xd_out, 16 * NCH)
            pool.wait_ge(tok_ready, 1)

            BEHIND = RING + 3
            for t in range(SLOTS + BEHIND):
                if t < SLOTS:
                    if t >= RING:
                        pool.wait_ge(xt_ready, t - RING + 1)
                    pool.indirect_dma_start(xg[:, t % RING, :], None, xd,
                                            bass.IndirectOffsetOnAxis(ap=tok_i[:, t:t + 1], axis=0)
                                            ).then_inc(xg_in[t % RING], 16)
                if t >= BEHIND:
                    s = t - BEHIND
                    if s == 0:
                        pool.wait_ge(rows_ready, 1)
                    pool.wait_ge(y_taken, EARLY + s + 1)
                    pool.indirect_dma_start(ys, bass.IndirectOffsetOnAxis(ap=row_i[:, s:s + 1], axis=0),
                                            yb[:, s % RING, :], None).then_inc(y_out[s % RING], 16)

        @block.scalar
        def _(act):
            def root(c):
                act.wait_ge(ln_step, c + 1)
                act.activation(std[:, CT * c:CT * c + CT], var[:, CT * c:CT * c + CT], ACT.Sqrt).then_inc(std_done, 1)

            def take_xnT(c):
                for h in range(2):
                    act.wait_ge(xnT_ps, 2 * c + h + 1)
                    if c and h == 0:
                        act.wait_ge(qkv_ps, CT * c)
                    act.activation(xnT[:, 2 * h:2 * h + 2, :, :],
                                   ps[:, h, :].rearrange("p (i k t) -> p i k t", i=2, k=KC), ACT.Copy).then_inc(xnT_ready, 1)

            def values(c):
                act.wait_ge(rope_step, 5 * c + 4)
                if c == 0:
                    act.wait_ge(consts, 8)
                act.activation(V[:, CT * c:CT * c + CT, :, 0:D],
                               ps[:, 2:6, (HQ + HK) * D:QKV].rearrange("p i (g d) -> p i g d", g=HK),
                               ACT.Copy).then_inc(v_ready, 1)

            def first_part(c, i):
                act.wait_ge(rope_step, 5 * c + 5)
                if c >= 2:
                    act.wait_ge(stack_ps, NFILL * (c - 1))
                src = qk[c % 2]
                act.activation(part_of(Qn, c, i, slice(0, 3)), src[:, i, 0:HQ, :].unsqueeze(2).to_broadcast([P, HQ, 3, D]),
                               ACT.Copy).then_inc(qpart, 1)
                act.activation(part_of(Kn, c, i, slice(0, 6, 3)), src[:, i, HQ:, :].unsqueeze(2).to_broadcast([P, HK, 2, D]),
                               ACT.Copy).then_inc(kpart, 1)
                act.activation(part_of(Kn, c, i, slice(5, 6)), src[:, i, HQ:, :].unsqueeze(2), ACT.Copy).then_inc(kpart, 1)

            def second_parts(c):
                act.wait_ge(split_step, 2 * CT * c + CT)
                for i in range(CT):
                    act.activation(part_of(Qn, c, i, slice(3, 5)), res[:, i, 0:HQ, :].unsqueeze(2).to_broadcast([P, HQ, 2, D]),
                                   ACT.Copy).then_inc(qpart, 1)
                    act.activation(part_of(Kn, c, i, slice(1, 6, 3))[:, :, 0:2], res[:, i, HQ:, :].unsqueeze(2).to_broadcast([P, HK, 2, D]),
                                   ACT.Copy).then_inc(kpart, 1)

            def take_stack(c, f):
                act.wait_ge(stack_ps, NFILL * c + f + 1)
                dst = Qs[0:KROW, 2 * f:2 * f + 2] if f < HQ // 2 else Ks[0:KROW, 2 * f - HQ:2 * f - HQ + 2]
                act.activation(dst[:, :, CW * c:CW * c + CW],
                               ps[0:KROW, 6 + f % 2, :].bitcast(BF16).rearrange("p (h t) -> p h t", h=2),
                               ACT.Copy).then_inc((stack_even, stack_odd)[f % 2], 1)

            root(0)
            take_xnT(0)
            for c in range(1, NCH):
                root(c)
            take_xnT(1)
            values(0)
            for i in range(CT):
                first_part(0, i)
            second_parts(0)

            def stack_step(c, f):
                if f == 0:
                    if c + 2 < NCH:
                        take_xnT(c + 2)
                    if c + 1 < NCH:
                        values(c + 1)
                        first_part(c + 1, 0)
                if f % 2 == 0 and c < PREP:
                    return
                if c + 1 < NCH and f == NFILL - 3:
                    second_parts(c + 1)
                take_stack(c, f)
                if c + 1 < NCH and f in (1, 3):
                    first_part(c + 1, 1 + f // 2)
                if c + 1 < NCH and f == 3:
                    first_part(c + 1, 3)

            for c in range(PREP):
                for f in range(NFILL):
                    stack_step(c, f)

            def silu(n, b, w):
                act.wait_ge(gu_ready, n + 1)
                if not isinstance(n, int) or n >= 2:
                    act.wait_ge(h_ready, n - 1)
                act.activation(gate_act[:, b, 0:w], ps[:, GB + b, 0:w], ACT.Silu).then_inc(silu_done, 1)

            def take_hidden(n, b, shared=False):
                act.wait_ge(th_ready, n + 1)
                if not isinstance(n, int) or n >= 2:
                    act.wait_ge(dn_ready, n - 1)
                if shared:
                    full = (SH - 1) * P
                    act.activation(hT[:, b, 0:full], ps[:, TB, 0:full], ACT.Copy).then_inc(ht_full, 1)
                    act.activation(hT[0:SREST, b, full:full + P], ps[0:SREST, TB, full:full + P], ACT.Copy).then_inc(ht_taken, 1)
                else:
                    act.activation(hT[0:IH, b, 0:2 * P], ps[0:IH, TB, 0:2 * P], ACT.Copy).then_inc(ht_taken, 1)

            for e in ORDER:
                if e[0] == "stack":
                    stack_step(e[1], e[2])
                elif e[0] == "up":
                    silu(e[1], e[1] % 2, SI)
                elif e[0] == "hide":
                    take_hidden(e[1], e[1] % 2, True)
                elif e == ("pos_onehots", 0):
                    act.wait_ge(route, RANKS * NCH)
                    act.activation(lexp[:, :, :], lsub[:, :, :], ACT.Exp).then_inc(lexp_done, 1)
                elif e[0] == "take":
                    u = e[1]
                    act.wait_ge(pv_done, STEPS_TO[u])
                    if u:
                        act.wait_ge(ring_ready, 1 + USE["turn", u - 1])
                    act.activation(OT[:, :], ps[:, OB, :], ACT.Copy).then_inc(o_copied, 1)
                elif e[0] == "root":
                    n, c = e[1], CHUNKS[e[1]]
                    act.wait_ge(var2_ready, n + 1)
                    act.activation(std[:, CT * c:CT * c + CT], var[:, CT * c:CT * c + CT], ACT.Sqrt).then_inc(std2_done, 1)
                elif e[0] == "apply":
                    _, n, i = e
                    act.wait_ge(ln2_step, 6 * n + 6)
                    i += CT * CHUNKS[n]
                    act.activation(xn[:, i, :], x_sb[:, i, :], ACT.Identity, bias=nmr[:, i:i + 1],
                                   scale=rstd[:, i:i + 1]).then_inc(xn2_ready, 1)
                elif e[0] == "logits":
                    n, c = e[1], CHUNKS[e[1]]
                    act.wait_ge(xn2_ready, CT * (n + 1))
                    act.dma_start(xd_v[:, CT * c:CT * c + CT, :], xn[:, CT * c:CT * c + CT, :]).then_inc(xd_out, 16)
                if e[0] != "score":
                    continue
                _, m, h = e
                u, j = STEPS[m]
                lo = max(0, P * (j - CT * UNITS[u][0]))
                act.wait_ge(s_ready, 2 * m + h + 1)
                if m >= PSLOT and h == 0:
                    act.wait_ge(pv_done, m - PSLOT + 1)
                act.activation(probs[:, m % PSLOT, 2 * h:2 * h + 2, lo:CW],
                               ps[:, SCB + 2 * h:SCB + 2 * h + 2, lo:CW], ACT.Exp, scale=SCALE).then_inc(exp_done, 1)

            take_hidden(EARLY - 1, (EARLY - 1) % 2, True)
            for n in range(EARLY, EARLY + 2):
                silu(n, n % 2, I)

            def routed(t, q, turn, live):
                take_hidden(EARLY + t, q % 2)
                silu(EARLY + t + 2, q % 2, I if live(2) else SI)

            ring_loop(act.Fori, routed)
            for n in range(LATE0, LATE0 + NT - EARLY):
                take_hidden(n, n % 2, True)
                if n + 2 < LATE0 + NT - EARLY:
                    silu(n + 2, n % 2, SI)

        @block.vector
        def _(dve):
            def normalise(c):
                t0, t1 = CT * c, CT * c + CT
                dve.wait_ge(x_in[c], 16)
                for i in range(t0, t1):
                    dve.bn_stats(stats[:, i, :], x_sb[:, i, :]).then_inc(stats_done, 1)
                for i in range(t0, t1):
                    dve.wait_ge(stats_done, t0 + i + 1)
                    dve.bn_aggr(mv[:, i, :], stats[:, i, :]).then_inc(stats_done, 1)
                dve.wait_ge(stats_done, 2 * t1)
                dve.tensor_scalar(var[:, t0:t1], mv[:, t0:t1, 1], EPS, None, ALU.add).then_inc(ln_step, 1)

            def newton(t, root_done, count, step, s):
                dve.wait_ge(root_done, count)
                dve.reciprocal(rstd0[:, t], std[:, t]).then_inc(step, 1)
                dve.wait_ge(step, s + 1)
                dve.tensor_tensor(newt[:, t], rstd0[:, t], rstd0[:, t], ALU.mult).then_inc(step, 1)
                dve.wait_ge(step, s + 2)
                dve.tensor_tensor(newt2[:, t], newt[:, t], var[:, t], ALU.mult).then_inc(step, 1)
                dve.wait_ge(step, s + 3)
                dve.tensor_scalar(newt3[:, t], newt2[:, t], -0.5, 1.5, ALU.mult, ALU.add).then_inc(step, 1)
                dve.wait_ge(step, s + 4)
                dve.tensor_tensor(rstd[:, t], newt3[:, t], rstd0[:, t], ALU.mult).then_inc(step, 1)

            def finish_normalise(c):
                t0, t1 = CT * c, CT * c + CT
                newton(slice(t0, t1), std_done, c + 1, ln_step2, 5 * c)
                dve.wait_ge(ln_step2, 5 * c + 5)
                for i in range(t0, t1):
                    dve.tensor_scalar(xn[:, i, :], x_sb[:, i, :], mv[:, i, 0:1], rstd[:, i:i + 1],
                                      ALU.subtract, ALU.mult).then_inc(xn_ready, 1)

            def rotate(c, steps=range(5)):
                s = 5 * c
                dst = qk[c % 2]
                src = ps[:, 2:6, 0:(HQ + HK) * D].rearrange("p i (h d) -> p i h d", d=D)
                shape = [P, CT, HQ + HK, HALF]
                a, b = slice(0, HALF), slice(HALF, D)
                products = ((rc, a, a, 0), (rc, b, b, 0), (dst, a, b, 2), (dst, b, a, 1))
                for n in steps:
                    if n == 0:
                        dve.wait_ge(qkv_ps, CT * c + CT)
                        if c:
                            dve.wait_ge(rope_step, s)
                        if c == 0:
                            dve.wait_ge(w_in, 32)
                        if c >= 2:
                            dve.wait_ge(qpart, 2 * CT * (c - 2) + CT)
                            dve.wait_ge(kpart, 3 * CT * (c - 2) + 2 * CT)
                    if n < 4:
                        to, half, of, row = products[n]
                        dve.tensor_tensor(to[:, :, :, half], src[:, :, :, of], rope_sb[:, CT * c:CT * c + CT, row, :]
                                          .unsqueeze(2).to_broadcast(shape), ALU.mult).then_inc(rope_step, 1)
                    else:
                        dve.wait_ge(rope_step, s + 4)
                        dve.tensor_tensor(dst, rc, dst, ALU.add).then_inc(rope_step, 1)

            def split_first(c, i):
                dve.wait_ge(qpart, 2 * CT * c + i + 1)
                dve.wait_ge(kpart, 3 * CT * c + 2 * i + 2)
                if c:
                    dve.wait_ge(split_step, 2 * CT * c)
                dve.tensor_tensor(res[:, i, 0:HQ, :].unsqueeze(2), qk[c % 2][:, i, 0:HQ, :].unsqueeze(2),
                                  part_of(Qn, c, i, slice(0, 1)), ALU.subtract).then_inc(k_step, 1)
                dve.tensor_tensor(res[:, i, HQ:, :].unsqueeze(2), qk[c % 2][:, i, HQ:, :].unsqueeze(2),
                                  part_of(Kn, c, i, slice(0, 1)), ALU.subtract).then_inc(split_step, 1)

            def split_second(c):
                for i in range(CT):
                    dve.wait_ge(qpart, 2 * CT * c + CT + i + 1)
                    dve.wait_ge(kpart, 3 * CT * c + 2 * CT + i + 1)
                    dve.tensor_tensor(part_of(Qn, c, i, slice(5, 6)), res[:, i, 0:HQ, :].unsqueeze(2),
                                      part_of(Qn, c, i, slice(3, 4)), ALU.subtract).then_inc(k_step, 1)
                    dve.tensor_tensor(part_of(Kn, c, i, slice(2, 3)), res[:, i, HQ:, :].unsqueeze(2),
                                      part_of(Kn, c, i, slice(1, 2)), ALU.subtract).then_inc(split_step, 1)

            def take_stack(c, f):
                dve.wait_ge(stack_ps, NFILL * c + f + 1)
                dst = Qs[0:KROW, 2 * f:2 * f + 2] if f < HQ // 2 else Ks[0:KROW, 2 * f - HQ:2 * f - HQ + 2]
                dve.tensor_copy(dst[:, :, CW * c:CW * c + CW],
                                ps[0:KROW, 6, :].bitcast(BF16).rearrange("p (h t) -> p h t", h=2)).then_inc(stack_even, 1)

            normalise(0)
            finish_normalise(0)
            for c in range(1, NCH):
                normalise(c)
            finish_normalise(1)
            rotate(0)
            finish_normalise(2)
            dve.wait_ge(rope_step, 5)
            for i in range(CT):
                split_first(0, i)
            rotate(1)
            split_second(0)

            def stack_step(c, f):
                if f % 2:
                    return
                if c + 1 < NCH and f == 0:
                    dve.wait_ge(rope_step, 5 * (c + 2))
                if c < PREP:
                    take_stack(c, f)
                if c + 1 < NCH and f < 6:
                    for i in ((0,), (1,), (2, 3))[f // 2]:
                        split_first(c + 1, i)
                if c + 3 < NCH and f == 2:
                    finish_normalise(c + 3)
                if c + 2 < NCH and f in (6, 8):
                    rotate(c + 2, ((0, 1), (2, 3))[f // 2 - 3])
                if c + 1 < NCH and f == 8:
                    split_second(c + 1)
                if c + 2 < NCH and f == 8:
                    rotate(c + 2, (4,))

            for c in range(PREP):
                for f in range(NFILL):
                    stack_step(c, f)

            def routes():
                dve.wait_ge(route, RANKS * NCH)
                for k in range(TOPK):
                    dve.tensor_tensor(hot[:, k], iota_e[:, :].unsqueeze(1).to_broadcast([P, NT, E]),
                                      top_f[:, :, k:k + 1].to_broadcast([P, NT, E]), ALU.is_equal).then_inc(route, 1)
                dve.wait_ge(route, R + 2)
                dve.tensor_tensor(hots[:, 0:NT, :], hot[:, 0], hot[:, 1], ALU.add).then_inc(hots_ready, 1)

            def places():
                bank = ps[:, BANK["places",], :]
                dve.wait_ge(ring_ready, USE["places",] + 1)
                dve.tensor_scalar(cnt_i[:, :], bank[:, NT * E:(NT + 1) * E], P - 1.0, None, ALU.add).then_inc(places_step, 1)
                dve.wait_ge(places_step, 1)
                dve.tensor_scalar(cnt_t[:, :], cnt_i[:, :], LOG_P, None, ALU.logical_shift_right).then_inc(places_step, 1)
                dve.wait_ge(places_step, 2)
                dve.tensor_copy(tiles[:, :], cnt_t[:, :]).then_inc(places_step, 1)
                dve.tensor_copy(csum[:, 0, 8:], cnt_t[:, :]).then_inc(places_step, 1)
                dve.wait_ge(places_step, 4)
                for n, d in enumerate((1, 2, 4, 8)):
                    a, b = csum[:, n % 2, :], csum[:, (n + 1) % 2, :]
                    dve.tensor_tensor(b[:, 8:], a[:, 8:], a[:, 8 - d:8 - d + E], ALU.add).then_inc(places_step, 1)
                    dve.wait_ge(places_step, 5 + n)
                ends = csum[:, 0, 8:]
                dve.tensor_tensor(base0[:, :], ends, tiles[:, :], ALU.subtract).then_inc(places_step, 1)
                dve.wait_ge(places_step, 9)
                dve.tensor_scalar(base[:, :], base0[:, :], float(P), None, ALU.mult).then_inc(places_step, 1)
                dve.wait_ge(places_step, 10)
                dve.tensor_tensor(where[:, :, :], bank[:, 0:NT * E].rearrange("p (i e) -> p i e", i=NT),
                                  base[:, :].unsqueeze(1).to_broadcast([P, NT, E]), ALU.add).then_inc(places_step, 1)
                dve.wait_ge(places_step, 11)
                for k in range(TOPK):
                    dve.tensor_tensor(wsel[:, k], hot[:, k], where[:, :, :], ALU.mult).then_inc(places_step, 1)
                dve.wait_ge(places_step, 13)
                dve.nop().then_inc(ring_used, 1)
                dve.tensor_reduce(dest[:, :, :], wsel[:, :, :, :], AX.X, ALU.add).then_inc(places_step, 1)
                dve.wait_ge(places_step, 14)
                dve.tensor_copy(dest_i[:, :, :], dest[:, :, :]).then_inc(dest_ready, 1)
                dve.wait_ge(dest_ready, 1)
                dve.tensor_scalar(slot_i[:, :, :], dest_i[:, :, :], LOG_P, None, ALU.logical_shift_right).then_inc(places_step, 1)
                dve.tensor_scalar(pos_i[:, :, :], dest_i[:, :, :], P - 1, None, ALU.bitwise_and).then_inc(places_step, 1)
                dve.wait_ge(places_step, 16)
                dve.tensor_copy(slot_f[:, :, :], slot_i[:, :, :]).then_inc(places_step, 1)
                dve.tensor_copy(pos_f[:, :, :], pos_i[:, :, :]).then_inc(places_step, 1)
                dve.wait_ge(places_step, 18)

            def slot_onehots():
                dve.tensor_tensor(slot_hot[:, :, :], iota_s[:, :].unsqueeze(1).to_broadcast([P, TOPK * NT, SLOTS]),
                                  slot_f[:, :, :].rearrange("p k i -> p (k i)").unsqueeze(2).to_broadcast([P, TOPK * NT, SLOTS]),
                                  ALU.is_equal).then_inc(onehots, 1)
                dve.wait_ge(onehots, 1)
                for k in range(TOPK):
                    dve.tensor_scalar(slot_val[:, k * NT:(k + 1) * NT, 0:SLOTS], slot_hot[:, k * NT:(k + 1) * NT, :],
                                      own_n[:, k:k + 1], None, ALU.mult).then_inc(onehots, 1)
                for k in range(TOPK):
                    dve.tensor_tensor(slot_val[:, k * NT:(k + 1) * NT, SLOTS:], slot_hot[:, k * NT:(k + 1) * NT, :],
                                      tile_n[:, :].unsqueeze(2).to_broadcast([P, NT, SLOTS]), ALU.mult).then_inc(onehots, 1)

            def pos_onehots(k):
                for i in range(NT):
                    dve.tensor_scalar(pos_hot[:, k * NT + i, :], iota_p[:, :], pos_f[:, k, i:i + 1], None,
                                      ALU.is_equal).then_inc(onehots, 1)

            def tokens():
                bank = ps[:, BANK["tokens",], :]
                dve.wait_ge(ring_ready, USE["tokens",] + 1)
                dve.tensor_copy(num_p[:, :], bank[:, 0:SLOTS]).then_inc(num_step, 1)
                dve.wait_ge(num_step, 1)
                dve.tensor_tensor(num[:, :], num_p[:, :], bank[:, SLOTS:2 * SLOTS], ALU.add).then_inc(num_step, 1)
                dve.wait_ge(num_step, 2)
                dve.nop().then_inc(ring_used, 1)
                dve.tensor_scalar(num_i[:, :], num[:, :], -1.0, 0.0, ALU.add, ALU.max).then_inc(num_step, 1)
                dve.wait_ge(num_step, 3)
                dve.tensor_scalar(tok_i[:, :], num_i[:, :], LOG_K, None, ALU.logical_shift_right).then_inc(tok_ready, 1)
                dve.scalar_tensor_tensor(out=to_spare[:, :], in0=num[:, :], scalar=0.0, in1=spare[:, :],
                                         op0=ALU.is_equal, op1=ALU.mult).then_inc(num_step, 1)
                dve.wait_ge(num_step, 4)
                dve.scalar_tensor_tensor(out=row_i[:, :], in0=num[:, :], scalar=-1.0, in1=to_spare[:, :],
                                         op0=ALU.add, op1=ALU.add).then_inc(rows_ready, 1)

            def slot_experts():
                dve.tensor_tensor(s_cmp[:, :, :], iota_s[0:1, :].unsqueeze(2).to_broadcast([1, SLOTS, E]),
                                  csum[0:1, 0, 8:].unsqueeze(1).to_broadcast([1, SLOTS, E]), ALU.is_ge).then_inc(places_step, 1)
                dve.wait_ge(places_step, 19)
                dve.tensor_reduce(s_exp[:, :], s_cmp[:, :, :], AX.X, ALU.add).then_inc(places_step, 1)
                dve.wait_ge(places_step, 20)
                dve.tensor_scalar(s_exp_i[:, :], s_exp[:, :], float(E - 1), None, ALU.min).then_inc(slots_ready, 1)

            def weights():
                dve.wait_ge(lexp_done, 1)
                dve.tensor_reduce(lsum[:, :], lexp[:, :, 0:E], AX.X, ALU.add).then_inc(places_step, 1)
                dve.wait_ge(places_step, 21)
                dve.reciprocal(wtok[:, 0, :], lsum[:, :]).then_inc(places_step, 1)
                dve.wait_ge(places_step, 22)
                dve.tensor_tensor(wtok[:, 1, :], wtok[:, 0, :], lexp[:, :, E], ALU.mult).then_inc(places_step, 1)

            def gate(n, b, up):
                w = up.shape[1]
                dve.wait_ge(silu_done, n + 1)
                if not isinstance(n, int) or n >= 2:
                    dve.wait_ge(th_ready, n - 1)
                dve.tensor_tensor(hidden[:, b, 0:w], gate_act[:, b, 0:w], up, ALU.mult).then_inc(h_ready, 1)

            def shared_gate(n):
                gate(n, n % 2, ps[:, UB + n % 2, 0:SI])

            def routed_gate(n, b):
                gate(n, b, ps[:, GB + b, I:2 * I])

            def take_slot(s, b):
                dve.wait_ge(xt_ready, s + 1)
                if not isinstance(s, int) or s >= 2:
                    dve.wait_ge(gu_ready, EARLY + s - 1)
                dve.tensor_copy(xgT[:, b, :], ps[:, XB + b, 0:KC * P]).then_inc(xt_taken, 1)

            def add_shared(n):
                i = TILES[n] if n < EARLY else TILES[n - SLOTS]
                dve.wait_ge(dn_ready, n + 1)
                dve.tensor_tensor(x_sb[:, i, :], ps[:, DB, 0:C], x_sb[:, i, :], ALU.add).then_inc(y_taken, 1)

            for e in ORDER:
                if e in USE:
                    dve.wait_ge(ring_ready, USE[e] + 1)
                    bank = ps[:, BANK[e], :]
                if e[0] == "stack":
                    stack_step(e[1], e[2])
                elif e[0] == "gate":
                    shared_gate(e[1])
                elif e[0] == "down":
                    add_shared(e[1])
                elif e[0] == "routes":
                    routes()
                elif e[0] == "places":
                    places()
                elif e[0] == "slot_onehots":
                    slot_onehots()
                elif e[0] == "pos_onehots":
                    pos_onehots(e[1])
                elif e[0] == "tokens":
                    tokens()
                elif e[0] == "experts":
                    slot_experts()
                elif e[0] == "max":
                    n = e[1]
                    u, hh, r, k = PIECES[n]
                    c = UNITS[u][0]
                    w = CW if k < c else P * (r + 1)
                    src = bank[:, 0:w]
                    if k < c:
                        dve.tensor_reduce(part[:, u % DEEP, hh, r, k:k + 1], src, AX.X, ALU.max).then_inc(ring_used, 1)
                    else:
                        if n >= 2:
                            dve.wait_ge(ring_used, USE["max", n - 2] + 1)
                        dve.tensor_tensor_reduce(unread[:, n % 2, 0:w], src, maskq[:, CW - w:CW], 1.0, 3 * NEG, ALU.add,
                                                 ALU.max, part[:, u % DEEP, hh, r, k:k + 1]).then_inc(ring_used, 1)
                elif e[0] == "split":
                    u = e[1]
                    c = UNITS[u][0]
                    dve.wait_ge(ring_used, USE["max", PIECES_TO[u] - 1] + 1)
                    if u >= DEEP:
                        dve.wait_ge(m3_ready, u - DEEP + 1)
                    dve.tensor_reduce(neg[:, u % DEEP], part[:, u % DEEP, :, :, 0:c + 1], AX.X, ALU.max,
                                      negate=True).then_inc(neg_ready, 1)
                elif e[0] == "shift":
                    _, u, h = e
                    c, g = UNITS[u]
                    h0 = GH * g + 2 * h
                    dve.tensor_copy(Qs[KROW:SROW, h0:h0 + 2, CW * c:CW * c + CW],
                                    bank[KROW:SROW, :].bitcast(BF16).rearrange("p (h t) -> p h t", h=2)
                                    ).then_inc(ring_used, 1)
                elif e[0] == "turn":
                    u = e[1]
                    c, g = UNITS[u]
                    o = bank.rearrange("p (i h d) -> p i h d", i=CT, h=GH)
                    if u:
                        dve.wait_ge(ring_used, USE["turn", u - 1] + 1)
                    dve.reciprocal(rden[:, :, :], o[:, :, :, D]).then_inc(rden_ready, 1)
                    dve.wait_ge(rden_ready, u + 1)
                    if g == 0 and u:
                        dve.wait_ge(ring_ready, 1 + USE["turn_out", u // HK - 1, 1])
                    dve.tensor_tensor(
                        attn[:, :, GH * D * g:GH * D * (g + 1)].rearrange("p i (h d) -> p i h d", h=GH), o[:, :, :, 0:D],
                        rden[:, :, :].unsqueeze(3).to_broadcast([P, CT, GH, D]), ALU.mult).then_inc(ring_used, 1)
                elif e[0] == "turn_out":
                    _, n, h = e
                    if n:
                        dve.wait_ge(ring_ready, 1 + USE["project", n - 1, h])
                    dve.tensor_copy(aT[:, 2 * h:2 * h + 2, :, :], bank.rearrange("p (i k t) -> p i k t", i=2, k=KC)
                                    ).then_inc(ring_used, 1)
                elif e[0] == "project":
                    _, n, h = e
                    c = CHUNKS[n]
                    xt = x_sb[:, CT * c + 2 * h:CT * c + 2 * h + 2, :]
                    dve.wait_ge(xn_ready, NT)
                    dve.tensor_tensor(xt, bank.rearrange("p (i n) -> p i n", i=2), xt, ALU.add
                                      ).then_inc(x2_done, 1)
                    dve.wait_ge(x2_done, 2 * n + h + 1)
                    dve.nop().then_inc(ring_used, 1)
                elif e[0] == "stats":
                    n, c = e[1], CHUNKS[e[1]]
                    dve.wait_ge(x2_done, 2 * n + 2)
                    for i in range(CT * c, CT * c + CT):
                        dve.bn_stats(stats[:, i, :], x_sb[:, i, :]).then_inc(stats2, 1)
                    for i in range(CT):
                        dve.wait_ge(stats2, 2 * CT * n + i + 1)
                        dve.bn_aggr(mv[:, CT * c + i, :], stats[:, CT * c + i, :]).then_inc(stats2, 1)
                    dve.wait_ge(stats2, 2 * CT * (n + 1))
                    dve.tensor_scalar(var[:, CT * c:CT * c + CT], mv[:, CT * c:CT * c + CT, 1], EPS, None,
                                      ALU.add).then_inc(var2_ready, 1)
                elif e[0] == "norm":
                    n, c = e[1], CHUNKS[e[1]]
                    newton(slice(CT * c, CT * c + CT), std2_done, n + 1, ln2_step, 6 * n)
                    dve.wait_ge(ln2_step, 6 * n + 5)
                    dve.scalar_tensor_tensor(out=nmr[:, CT * c:CT * c + CT], in0=mv[:, CT * c:CT * c + CT, 0], scalar=-1.0,
                                             in1=rstd[:, CT * c:CT * c + CT], op0=ALU.mult, op1=ALU.mult
                                             ).then_inc(ln2_step, 1)
                elif e[0] == "turn_x":
                    _, n, h = e
                    i = CT * CHUNKS[n] + 2 * h
                    dve.tensor_copy(xT_all[:, i:i + 2, :, :], bank.rearrange("p (i k t) -> p i k t", i=2, k=KC)
                                    ).then_inc(ring_used, 1)
                elif e[0] == "logits":
                    c = CHUNKS[e[1]]
                    dve.wait_ge(consts, 18)
                    dve.tensor_copy(lg[:, CT * c:CT * c + CT, :], bank[:, 0:CT * E].rearrange("p (i e) -> p i e", i=CT)
                                    ).then_inc(ring_used, 1)
                elif e[0] == "rank":
                    n, c = e[1], CHUNKS[e[1]]
                    t = slice(CT * c, CT * c + CT)
                    dve.wait_ge(ring_used, USE["logits", n] + 1)
                    for i in range(CT * c, CT * c + CT):
                        dve.max(top[:, i, :], lg[:, i, :]).then_inc(route, 1)
                    dve.wait_ge(route, RANKS * n + CT)
                    dve.tensor_tensor(lsub[:, t, 0:E], lg[:, t, :], top[:, t, 0:1].to_broadcast([P, CT, E]),
                                      ALU.subtract).then_inc(route, 1)
                    dve.tensor_tensor(lsub[:, t, E:E + 1], top[:, t, 1:2], top[:, t, 0:1], ALU.subtract).then_inc(route, 1)
                    for i in range(CT * c, CT * c + CT):
                        dve.max_index(top_i[:, i, :], top[:, i, :], lg[:, i, :]).then_inc(route, 1)
                    dve.wait_ge(route, RANKS * n + 2 * CT + 2)
                    dve.tensor_copy(top_f[:, t, :], top_i[:, t, 0:TOPK]).then_inc(route, 1)

            weights()
            take_slot(0, 0)
            add_shared(EARLY - 1)
            take_slot(1, 1)
            routed_gate(EARLY, 0)
            take_slot(2, 0)

            def routed(t, q, turn, live):
                n = EARLY + t
                if live(1):
                    routed_gate(n + 1, (q + 1) % 2)
                else:
                    shared_gate(n + 1)
                if live(3):
                    take_slot(t + 3, (q + 3) % 2)
                dve.wait_ge(dn_ready, n + 1)
                if not isinstance(t, int) or t >= RING:
                    dve.wait_ge(y_out[q], 16 * turn)
                dve.tensor_copy(yb[:, q, :], ps[:, DB, 0:C]).then_inc(y_taken, 1)

            ring_loop(dve.Fori, routed)

            def mix(j):
                i = TILES[j]
                dve.wait_ge(yg_in[j % YG], 16 * (j // YG + 1))
                for k in range(TOPK):
                    if k:
                        dve.wait_ge(mixed, TOPK * j + k)
                    dve.scalar_tensor_tensor(out=x_sb[:, i, :], in0=yg[:, j % YG, k * C:(k + 1) * C],
                                             scalar=wtok[:, k, i:i + 1], in1=x_sb[:, i, :], op0=ALU.mult,
                                             op1=ALU.add).then_inc(mixed, 1)

            late = NT - EARLY
            FIRST_MIX = (0, 3, 7, 11, NT)
            for n in range(LATE0, LATE0 + late):
                if n + 1 < LATE0 + late:
                    shared_gate(n + 1)
                add_shared(n)
                dve.wait_ge(y_taken, n + 1)
                d = n - LATE0
                for j in range(FIRST_MIX[d], FIRST_MIX[d + 1]):
                    mix(j)

        @block.tensor
        def _(pe):
            def turn_x(c):
                for h in range(2):
                    pe.wait_ge(xn_ready, CT * c + 2 * h + 2)
                    if c:
                        pe.wait_ge(xnT_ready, 2 * (c - 1) + h + 1)
                    for i in range(2):
                        for k in range(KC):
                            t = pe.transpose(ps[:, h, (2 * i + k) * P:(2 * i + k + 1) * P],
                                             xn[:, CT * c + 2 * h + i, k * P:(k + 1) * P], identf[:, :])
                    t.then_inc(xnT_ps, 1)

            def project_qkv(c, i):
                if i == 0 and c == 0:
                    pe.wait_ge(w_in, 32)
                elif i == 0:
                    pe.wait_ge(v_ready, c)
                    pe.wait_ge(rope_step, 5 * c - 1)
                pe.wait_ge(xnT_ready, 2 * c + i // 2 + 1)
                for k in range(KC):
                    m = pe.matmul(ps[:, 2 + i, 0:QKV], xnT[:, i, k, :], wqkv_sb[:, k, :],
                                  start=(k == 0), stop=(k == KC - 1))
                m.then_inc(qkv_ps, 1)

            def turn_stack(c, f):
                if f == 0:
                    pe.wait_ge(split_step, 2 * CT * (c + 1))
                    pe.wait_ge(k_step, 2 * CT * (c + 1))
                    pe.wait_ge(qpart, 2 * CT * (c + 1))
                    pe.wait_ge(kpart, 3 * CT * (c + 1))
                n = NFILL * c + f
                if n >= 2:
                    pe.wait_ge((stack_even, stack_odd)[f % 2], n // 2)
                bank = ps[0:KROW, 6 + f % 2, :].bitcast(BF16)
                for h in range(2):
                    for i in range(CT):
                        hh = 2 * f + h
                        src = Qn[c % 2][:, hh, :] if hh < HQ else Kn[c % 2][:, hh - HQ, :]
                        t = pe.transpose(bank[:, (CT * h + i) * P:(CT * h + i + 1) * P],
                                         src[:, i * KROW:(i + 1) * KROW], identb[:, :])
                t.then_inc(stack_ps, 1)

            def keep_warm(n):
                for _ in range(n):
                    pe.matmul(ps[:, 7, 0:P], identb[:, :], identb[:, :], start=True, stop=True)

            pe.wait_ge(consts, 8)
            keep_warm(40)
            for c in range(2):
                turn_x(c)
                for i in range(CT):
                    project_qkv(c, i)

            def stack_step(c, f):
                if c + 2 < NCH and f == 0:
                    turn_x(c + 2)
                turn_stack(c, f)
                if c + 2 < NCH and 0 < f <= CT:
                    project_qkv(c + 2, f - 1)

            for c in range(PREP):
                for f in range(NFILL):
                    stack_step(c, f)

            def shared_up(n):
                i = TILES[n] if n < EARLY else TILES[n - SLOTS]
                if n >= 2:
                    pe.wait_ge(h_ready, n - 1)
                else:
                    pe.wait_ge(exp_done, 2 * len(STEPS))
                for half in range(2):
                    for k in range(KC):
                        m = pe.matmul(ps[:, (GB, UB)[half] + n % 2, 0:SI], xT_all[:, i, k, :],
                                      wsgu_sb[:, k, half * SI:(half + 1) * SI], start=(k == 0), stop=(k == KC - 1))
                m.then_inc(gu_ready, 1)

            whole = UNITS.index((NCH - 1, 0))

            def free_bank(e):
                if BEFORE[e]:
                    pe.wait_ge(ring_used, BEFORE[e])
                return ps[:, BANK[e], :]

            def places():
                bank = free_bank(("places",))
                pe.wait_ge(hots_ready, 1)
                pe.wait_ge(consts, 18)
                pe.matmul(bank[:, 0:(NT + 1) * E], before[:, :], hots[:, :, :].rearrange("p i e -> p (i e)"),
                          start=True, stop=False)
                for i in range(NT):
                    t = pe.matmul(bank[:, (i + 1) * E:(NT + 1) * E].rearrange("p (i e) -> p i e", e=E), onesb[:, :],
                                  hots[:, i:i + 1, :].to_broadcast([P, NT - i, E]), start=False, stop=(i == NT - 1))
                t.then_inc(ring_ready, 1)

            def tokens():
                bank = free_bank(("tokens",))
                pe.wait_ge(onehots, 1 + 2 * TOPK + TOPK * NT)
                for n in range(TOPK * NT):
                    t = pe.matmul(bank[:, 0:2 * SLOTS], pos_hot[:, n, :], slot_val[:, n, :],
                                  start=(n == 0), stop=(n == TOPK * NT - 1))
                t.then_inc(ring_ready, 1)

            def turn_hidden(n, b, shared=False):
                pe.wait_ge(h_ready, n + 1)
                if not isinstance(n, int) or n >= 1:
                    pe.wait_ge(ht_taken, n)
                for k in range(SH if shared else 2):
                    lo, hi = (k * P, min((k + 1) * P, SI)) if shared else (k * IH, (k + 1) * IH)
                    t = pe.transpose(ps[0:hi - lo, TB, k * P:(k + 1) * P], hidden[:, b, lo:hi], identf[:, :])
                t.then_inc(th_ready, 1)

            def shared_down(n):
                pe.wait_ge(ht_taken, n + 1)
                if n:
                    pe.wait_ge(y_taken, n)
                pe.wait_ge(ht_full, (n if n < EARLY else n - SLOTS) + 1)
                for k in range(SH):
                    rows = P if k < SH - 1 else SREST
                    m = pe.matmul(ps[:, DB, 0:C], hT[0:rows, n % 2, k * P:(k + 1) * P], wsdn_sb[0:rows, k, :],
                                  start=(k == 0), stop=(k == SH - 1))
                m.then_inc(dn_ready, 1)

            for e in ORDER:
                if e in USE:
                    bank = free_bank(e)
                if e[0] == "stack":
                    stack_step(e[1], e[2])
                elif e[0] == "max":
                    n = e[1]
                    if n == PIECES_TO[whole - 1]:
                        pe.wait_ge(stack_even, NCH * NFILL // 2)
                        pe.wait_ge(stack_odd, NCH * NFILL // 2)
                    if n == 0:
                        pe.wait_ge(xnT_ready, 2 * NCH)
                        pe.wait_ge(v_ready, NCH)
                        pe.wait_ge(rope_step, 5 * NCH)
                    u, hh, r, k = PIECES[n]
                    c, g = UNITS[u]
                    w = CW if k < c else P * (r + 1)
                    t = (CT * c + r) * P
                    pe.matmul(bank[:, 0:w], Qs[0:KROW, GH * g + hh, t:t + P],
                              Ks[0:KROW, g, CW * k:CW * k + w], start=True, stop=True).then_inc(ring_ready, 1)
                elif e[0] == "shift":
                    _, u, h = e
                    pe.wait_ge(m3_ready, u + 1)
                    rows = bank[KROW:SROW, :].bitcast(BF16)
                    for q in range(2):
                        for r in range(CT):
                            t = pe.transpose(rows[:, (CT * q + r) * P:(CT * q + r + 1) * P],
                                             M3[:, u % DEEP, 2 * h + q, r, 0:MROW], identb[:, :])
                    t.then_inc(ring_ready, 1)
                elif e[0] == "score":
                    _, m, h = e
                    u, j = STEPS[m]
                    c, g = UNITS[u]
                    lo = max(0, P * (j - CT * c))
                    if m == 0 and h == 0:
                        pe.wait_ge(ones_set, 1)
                        pe.wait_ge(stack_even, NCH * NFILL // 2)
                        pe.wait_ge(stack_odd, NCH * NFILL // 2)
                    if u == whole and j == 0 and h == 0:
                        pe.wait_ge(ones_set, 2)
                    if j == 0 and h == 0:
                        pe.wait_ge(ring_used, USE["shift", u, 1] + 1)
                    if m:
                        pe.wait_ge(exp_done, 2 * (m - 1) + h + 1)
                    for q in range(2):
                        s = pe.matmul(ps[:, SCB + 2 * h + q, lo:CW], Ks[0:SROW, g, P * j:P * j + P],
                                      Qs[0:SROW, GH * g + 2 * h + q, CW * c + lo:CW * (c + 1)], start=True, stop=True)
                    s.then_inc(s_ready, 1)
                elif e[0] == "values":
                    _, m, h = e
                    u, j = STEPS[m]
                    c, g = UNITS[u]
                    lo, hi = max(h * CW // 2, P * (j - CT * c)), (h + 1) * CW // 2
                    if m in DIAG:
                        pe.wait_ge(masked, DIAG.index(m) + 1)
                    else:
                        pe.wait_ge(exp_done, 2 * m + 2)
                    if j == 0 and u:
                        pe.wait_ge(o_copied, u)
                    for hh in range(GH):
                        if lo < hi:
                            o = pe.matmul(ps[VC * hh:VC * hh + VC, OB, lo:hi], V[:, j, g, :], probs[:, m % PSLOT, hh, lo:hi],
                                          start=(j == 0 and h == 0), stop=(j == key_blocks(c) - 1),
                                          skip_group_check=True)
                    if h == 1:
                        o.then_inc(pv_done, 1)
                elif e[0] == "turn":
                    u = e[1]
                    pe.wait_ge(o_copied, u + 1)
                    for i in range(CT):
                        t = pe.transpose(bank[:, i * P:(i + 1) * P], OT[:, i * P:(i + 1) * P], identf[:, :])
                    t.then_inc(ring_ready, 1)
                elif e[0] == "turn_out":
                    _, n, h = e
                    pe.wait_ge(ring_used, 1 + USE["turn", HK * n + HK - 1])
                    for i in range(2):
                        for k in range(KC):
                            t = pe.transpose(bank[:, (2 * i + k) * P:(2 * i + k + 1) * P],
                                             attn[:, 2 * h + i, k * P:(k + 1) * P], identf[:, :])
                    t.then_inc(ring_ready, 1)
                elif e[0] == "project":
                    _, n, h = e
                    pe.wait_ge(wp_in, 16)
                    pe.wait_ge(ring_used, 1 + USE["turn_out", n, h])
                    for i in range(2):
                        for k in range(KC):
                            t = pe.matmul(bank[:, i * C:(i + 1) * C], aT[:, 2 * h + i, k, :], wp_sb[:, k, :],
                                          start=(i == 0 and k == 0), stop=(k == KC - 1), skip_group_check=True)
                    t.then_inc(ring_ready, 1)
                elif e[0] == "turn_x":
                    _, n, h = e
                    pe.wait_ge(xn2_ready, CT * n + 2 * h + 2)
                    for i in range(2):
                        for k in range(KC):
                            t = pe.transpose(bank[:, (2 * i + k) * P:(2 * i + k + 1) * P],
                                             xn[:, CT * CHUNKS[n] + 2 * h + i, k * P:(k + 1) * P], identf[:, :])
                    t.then_inc(ring_ready, 1)
                elif e[0] == "logits":
                    pe.wait_ge(ring_used, 1 + USE["turn_x", e[1], 1])
                    pe.wait_ge(ffn_w, 64)
                    for i in range(CT):
                        for k in range(KC):
                            t = pe.matmul(bank[:, i * E:(i + 1) * E], xT_all[:, CT * CHUNKS[e[1]] + i, k, :], wgate_sb[:, k, :],
                                          start=(i == 0 and k == 0), stop=(k == KC - 1), skip_group_check=True)
                    t.then_inc(ring_ready, 1)
                elif e[0] == "up":
                    shared_up(e[1])
                elif e[0] == "hide":
                    turn_hidden(e[1], e[1] % 2, True)
                elif e[0] == "down":
                    if e[1] == 0:
                        pe.wait_ge(ring_used, RING_END)
                    shared_down(e[1])
                elif e[0] == "places":
                    places()
                elif e[0] == "tokens":
                    tokens()

            def turn_slot(s, q, turn):
                pe.wait_ge(xg_in[q], 16 * (turn + 1))
                if not isinstance(s, int) or s >= 2:
                    pe.wait_ge(xt_taken, s - 1)
                for k in range(KC):
                    m = pe.transpose(ps[:, XB + q % 2, k * P:(k + 1) * P], xg[:, q, k * P:(k + 1) * P], identf[:, :])
                m.then_inc(xt_ready, 1)

            expert_reg = [pe.alloc_register(f"expert{q}") for q in range(RING)]

            def load_expert(s, q):
                pe.reg_load(expert_reg[q], s_exp_i[0:1, bass.ds(s, 1)])

            def routed_up(s, q, b):
                e = pe.snap(expert_reg[q], min_val=0, max_val=E - 1)
                pe.wait_ge(xt_taken, s + 1)
                pe.wait_ge(h_ready, EARLY + s - 1)
                for k in range(KC):
                    m = pe.matmul(ps[:, GB + b, 0:2 * I], xgT[:, b, k * P:(k + 1) * P],
                                  wgu_sb[:, bass.ds(e, 1), k, :], start=(k == 0), stop=(k == KC - 1))
                m.then_inc(gu_ready, 1)

            turn_hidden(EARLY - 1, (EARLY - 1) % 2, True)
            pe.wait_ge(ring_used, len(USES))
            turn_slot(0, 0, 0)
            shared_down(EARLY - 1)
            pe.wait_ge(expert_w, 32)
            pe.wait_ge(slots_ready, 1)
            load_expert(0, 0)
            turn_slot(1, 1, 0)
            routed_up(0, 0, 0)
            load_expert(1, 1)
            turn_slot(2, 2, 0)
            routed_up(1, 1, 1)
            load_expert(2, 2)

            def routed(t, q, turn, live):
                n = EARLY + t
                turn_hidden(n, q % 2)
                if live(2):
                    routed_up(t + 2, (q + 2) % RING, q % 2)
                    if live(3):
                        load_expert(t + 3, (q + 3) % RING)
                else:
                    shared_up(n + 2)
                if live(3):
                    turn_slot(t + 3, (q + 3) % RING, turn + (q + 3) // RING)
                e = pe.snap(expert_reg[q], min_val=0, max_val=E - 1)
                pe.wait_ge(ht_taken, n + 1)
                pe.wait_ge(y_taken, n)
                for k in range(2):
                    m = pe.matmul(ps[:, DB, 0:C], hT[0:IH, q % 2, k * P:(k + 1) * P],
                                  wdn_sb[:, bass.ds(e, 1), k, :], start=(k == 0), stop=(k == 1))
                m.then_inc(dn_ready, 1)

            ring_loop(pe.Fori, routed)
            for n in range(LATE0, LATE0 + NT - EARLY):
                turn_hidden(n, n % 2, True)
                if n + 2 < LATE0 + NT - EARLY:
                    shared_up(n + 2)
                shared_down(n)


def rope_table():
    import numpy as np
    inv = (1.0 / np.float32(10000.0) ** (np.arange(HALF, dtype=np.float32) / np.float32(HALF))).astype(np.float32)
    ang = (np.arange(T, dtype=np.float32)[:, None] * inv[None, :]).astype(np.float32).astype(np.float64)
    tab = np.stack([np.cos(ang), np.sin(ang), -np.sin(ang)], 1).astype(np.float32)
    return np.ascontiguousarray(tab.reshape(NT, P, 3, HALF).transpose(1, 0, 2, 3))


def layout(inputs):
    import numpy as np
    a = {k: np.asarray(v) for k, v in inputs.items()}
    rows = lambda w: np.ascontiguousarray(w.T.reshape(KC, P, -1).transpose(1, 0, 2))
    wqkv = np.concatenate([a["L0_attn_Wq"], a["L0_attn_Wk"], a["L0_attn_Wv"]], 0)
    return {"x": np.ascontiguousarray(a["L0_attn_x"].reshape(T, C)), "wqkv": rows(wqkv), "wp": rows(a["L0_attn_Wp"]),
            "rope": rope_table(), "wgate": rows(a["L0_ffn_gate_w"]),
            "wgu": np.ascontiguousarray(a["L0_ffn_w_gate_up"].reshape(E, KC, P, 2 * I).transpose(2, 0, 1, 3)),
            "wdn": np.ascontiguousarray(a["L0_ffn_w_down"].reshape(E, 2, IH, C).transpose(2, 0, 1, 3)),
            "wsgu": rows(a["L0_ffn_shared_gate_up"].T),
            "wsdn": np.ascontiguousarray(a["L0_ffn_shared_down"])}


def kernel(**inputs):
    import concourse.bacc as bacc
    from concourse.bass_utils import run_bass_kernel_spmd
    arrays = layout(inputs)
    nc = bacc.Bacc("TRN2", target_bir_lowering=False, num_devices=1)
    args = {k: nc.dram_tensor(k, v.shape, mybir.dt.from_np(v.dtype), kind="ExternalInput").ap() for k, v in arrays.items()}
    out = nc.dram_tensor("out", (T, C), F32, kind="ExternalOutput").ap()
    program(nc, **args, out=out)
    r = run_bass_kernel_spmd(nc, [arrays], core_ids=[0])
    return r.results[0]["out"].reshape(1, T, C)
```
